# Optimizing a Trainium2 kernel written in Bass

```python
import numpy as np
import jax
import jax.numpy as jnp

def _softmax(x, axis=-1):
    return jax.nn.softmax(x, axis=axis)

def _gelu(x):
    return jax.nn.gelu(x, approximate=True)

def _silu(x):
    return jax.nn.silu(x)

def _sigmoid(x):
    return jax.nn.sigmoid(x)

def _layernorm(x, axis=-1, eps=1e-05):
    m = jnp.mean(x, axis=axis, keepdims=True)
    v = jnp.var(x, axis=axis, keepdims=True)
    return (x - m) / jnp.sqrt(v + eps)

def _scatter_add(tgt, idx, src, axis=0):
    return tgt.at[idx].add(src)

def _segment_sum(src, seg, n):
    return jax.ops.segment_sum(src, seg, n)
kernel_name = 'mk_xattn_ffn_d4_seqx_r8_967a18'

def setup_inputs(seed: int=0):
    np.random.seed(seed)
    _w = jnp.asarray

    def _rec_inputs():
        import jax
        import jax.numpy as jnp
        _rk = jax.random.key(seed)
        x = 7.22e-05 + 1 * jax.random.normal(jax.random.fold_in(_rk, 1), (32, 128, 128), jnp.float32)
        _lenS = 128 - jax.random.randint(jax.random.fold_in(_rk, 7), (32,), 0, max(1, 128 // 4) + 1, jnp.int32)
        _lenS2 = 128 - jax.random.randint(jax.random.fold_in(_rk, 8), (32,), 0, max(1, 128 // 4) + 1, jnp.int32)
        _ctx_1024P = jax.random.normal(jax.random.fold_in(_rk, 11), (32, 16, 128), jnp.float32)
        _ctx_1024c = jax.random.dirichlet(jax.random.fold_in(_rk, 511), 0.3 * jnp.ones((16,), jnp.float32), (32, 128))
        _ctx_1024t = jnp.einsum('bsk,bkd->bsd', _ctx_1024c, _ctx_1024P)
        _ctx_1024t = _ctx_1024t * jax.lax.rsqrt(jnp.mean(jnp.square(_ctx_1024t)) + 1e-12) * 0.953939
        ctx_1024 = 4.13588e-05 + 0.999923 * (_ctx_1024t + 0.3 * jax.random.normal(jax.random.fold_in(_rk, 611), (32, 128, 128), jnp.float32))
        _validS = jnp.arange(128)[None, :] < _lenS[:, None]
        _validS2 = jnp.arange(128)[None, :] < _lenS2[:, None]
        _causal = jnp.tril(jnp.ones((128, 128), dtype=bool))
        mask_SxS2_bk1 = jnp.broadcast_to(_validS2[0:1, :], (128, 128))
        return (x, ctx_1024, mask_SxS2_bk1)
    x, ctx_1024, mask_SxS2_bk1 = _rec_inputs()

    def _L0_xattn_setup():
        import jax, jax.numpy as jnp
        import numpy as np
        HID = 128
        HEADS = 16
        HEAD_DIM = HID // HEADS
        NEG = -10000000000.0
        key = jax.random.key(seed)
        ks = jax.random.split(key, 12)
        B, S = (4, 256)
        scale = 1.0 / np.sqrt(HID)
        inp = {'query': jax.random.normal(ks[0], (B, S, HID), dtype=jnp.float32), 'key': jax.random.normal(ks[1], (B, S, HID), dtype=jnp.float32), 'value': jax.random.normal(ks[2], (B, S, HID), dtype=jnp.float32), 'Wq': jax.random.normal(ks[3], (HID, HID), dtype=jnp.float32) * scale, 'bq': jnp.zeros((HID,), dtype=jnp.float32), 'Wk': jax.random.normal(ks[4], (HID, HID), dtype=jnp.float32) * scale, 'bk': jnp.zeros((HID,), dtype=jnp.float32), 'Wv': jax.random.normal(ks[5], (HID, HID), dtype=jnp.float32) * scale, 'bv': jnp.zeros((HID,), dtype=jnp.float32), 'Wo': jax.random.normal(ks[6], (HID, HID), dtype=jnp.float32) * scale, 'bo': jnp.zeros((HID,), dtype=jnp.float32)}
        return inp
    _L0_xattn_all = _L0_xattn_setup()
    _L0_xattn_in = {k: v for k, v in _L0_xattn_all.items() if k in ('Wq', 'bq', 'Wk', 'bk', 'Wv', 'bv', 'Wo', 'bo')}
    del _L0_xattn_all

    def _L0_ffn_setup():
        import jax, jax.numpy as jnp
        import numpy as np
        DIM = 128
        INTER = 64
        E = 8
        TOP_K = 2
        ROUTE_SCALE = 1.0
        key = jax.random.key(seed)
        ks = jax.random.split(key, 8)
        s_d = 1.0 / np.sqrt(DIM)
        s_f = 1.0 / np.sqrt(INTER)
        x = jax.random.normal(ks[0], (2, 256, DIM), dtype=jnp.float32)
        gate_w = jax.random.uniform(ks[1], (E, DIM), jnp.float32, -s_d, s_d)
        wg = jax.random.uniform(ks[2], (E, INTER, DIM), jnp.float32, -s_d, s_d)
        wu = jax.random.uniform(ks[3], (E, INTER, DIM), jnp.float32, -s_d, s_d)
        wd = jax.random.uniform(ks[4], (E, DIM, INTER), jnp.float32, -s_f, s_f)
        sg = jax.random.uniform(ks[5], (INTER, DIM), jnp.float32, -s_d, s_d)
        su = jax.random.uniform(ks[6], (INTER, DIM), jnp.float32, -s_d, s_d)
        sd = jax.random.uniform(ks[7], (DIM, INTER), jnp.float32, -s_f, s_f)
        return {'x': x, 'gate_w': gate_w, 'wg': wg, 'wu': wu, 'wd': wd, 'sg': sg, 'su': su, 'sd': sd}
    _L0_ffn_all = _L0_ffn_setup()
    _L0_ffn_in = {k: v for k, v in _L0_ffn_all.items() if k in ('gate_w', 'wg', 'wu', 'wd', 'sg', 'su', 'sd')}
    del _L0_ffn_all

    def _L1_xattn_setup():
        import jax, jax.numpy as jnp
        import numpy as np
        EMBED_DIM = 128
        NUM_HEADS = 16
        HEAD_DIM = EMBED_DIM // NUM_HEADS
        key = jax.random.key(seed)
        ks = jax.random.split(key, 10)
        B, T, E = (2, 256, EMBED_DIM)

        def xavier(k, shape):
            fan_in, fan_out = (shape[1], shape[0])
            limit = (6.0 / (fan_in + fan_out)) ** 0.5
            return jax.random.uniform(k, shape, jnp.float32, -limit, limit)
        return {'query': jax.random.normal(ks[0], (B, T, E), jnp.float32), 'key': jax.random.normal(ks[1], (B, T, E), jnp.float32), 'value': jax.random.normal(ks[2], (B, T, E), jnp.float32), 'Wq': xavier(ks[3], (E, E)), 'Wk': xavier(ks[4], (E, E)), 'Wv': xavier(ks[5], (E, E)), 'bq': jnp.zeros((E,), jnp.float32), 'bk': jnp.zeros((E,), jnp.float32), 'bv': jnp.zeros((E,), jnp.float32), 'Wo': xavier(ks[6], (E, E)), 'bo': jnp.zeros((E,), jnp.float32)}
    _L1_xattn_all = _L1_xattn_setup()
    _L1_xattn_in = {k: v for k, v in _L1_xattn_all.items() if k in ('Wq', 'Wk', 'Wv', 'bq', 'bk', 'bv', 'Wo', 'bo')}
    del _L1_xattn_all

    def _L1_ffn_setup():
        import jax, jax.numpy as jnp
        import numpy as np
        NUM_EXPERTS = 8
        N_EMBD = 128
        D_FF = 4 * N_EMBD
        B, S = (4, 256)
        key = jax.random.key(seed)
        ks = jax.random.split(key, 6)
        x = jax.random.normal(ks[0], (B, S, N_EMBD), dtype=jnp.float32)
        gate_w = jax.random.normal(ks[1], (N_EMBD, NUM_EXPERTS), dtype=jnp.float32) * 0.02
        w1 = jax.random.normal(ks[2], (NUM_EXPERTS, N_EMBD, D_FF), dtype=jnp.float32) * 0.02
        b1 = jnp.zeros((NUM_EXPERTS, D_FF), dtype=jnp.float32)
        w2 = jax.random.normal(ks[3], (NUM_EXPERTS, D_FF, N_EMBD), dtype=jnp.float32) * 0.02
        b2 = jnp.zeros((NUM_EXPERTS, N_EMBD), dtype=jnp.float32)
        return {'x': x, 'gate_w': gate_w, 'w1': w1, 'b1': b1, 'w2': w2, 'b2': b2}
    _L1_ffn_all = _L1_ffn_setup()
    _L1_ffn_in = {k: v for k, v in _L1_ffn_all.items() if k in ('gate_w', 'w1', 'b1', 'w2', 'b2')}
    del _L1_ffn_all

    def _L2_xattn_setup():
        import jax, jax.numpy as jnp
        import numpy as np
        import math
        D_MODEL = 128
        NUM_HEADS = 16
        D_K = D_MODEL // NUM_HEADS
        B, S = (4, 256)
        key = jax.random.key(seed)
        ks = jax.random.split(key, 12)
        q = jax.random.normal(ks[0], (B, S, D_MODEL), dtype=jnp.float32)
        k = jax.random.normal(ks[1], (B, S, D_MODEL), dtype=jnp.float32)
        v = jax.random.normal(ks[2], (B, S, D_MODEL), dtype=jnp.float32)
        mask = jnp.triu(jnp.ones((S, S), dtype=bool), k=1)
        limit = math.sqrt(6.0 / (D_MODEL + D_MODEL))

        def xavier(kk):
            return jax.random.uniform(kk, (D_MODEL, D_MODEL), jnp.float32, -limit, limit)
        blim = 1.0 / math.sqrt(D_MODEL)

        def bias(kk):
            return jax.random.uniform(kk, (D_MODEL,), jnp.float32, -blim, blim)
        return {'q': q, 'k': k, 'v': v, 'mask': mask, 'wq': xavier(ks[3]), 'bq': bias(ks[4]), 'wk': xavier(ks[5]), 'bk': bias(ks[6]), 'wv': xavier(ks[7]), 'bv': bias(ks[8]), 'wo': xavier(ks[9]), 'bo': bias(ks[10])}
    _L2_xattn_all = _L2_xattn_setup()
    _L2_xattn_in = {k: v for k, v in _L2_xattn_all.items() if k in ('wq', 'bq', 'wk', 'bk', 'wv', 'bv', 'wo', 'bo')}
    del _L2_xattn_all

    def _L2_ffn_setup():
        import jax, jax.numpy as jnp
        import numpy as np
        NUM_EXPERTS = 8
        HIDDEN = 128
        INTER = 128
        BATCH = 2
        SEQ = 128
        TOP_K = 2
        SWIGLU_ALPHA = 1.702
        LIMIT = 7.0

        def _grouped_mm(x, w, expert_ids):
            onehot = jax.nn.one_hot(expert_ids, w.shape[0], dtype=x.dtype)
            y_all = jnp.einsum('tk,ekn->etn', x, w)
            return jnp.einsum('te,etn->tn', onehot, y_all)

        def _gpt_oss_swiglu(x):
            gate = jnp.minimum(x[..., ::2], LIMIT)
            up = jnp.clip(x[..., 1::2], -LIMIT, LIMIT)
            glu = gate * jax.nn.sigmoid(gate * SWIGLU_ALPHA)
            return (up + 1.0) * glu
        key = jax.random.key(seed)
        ks = jax.random.split(key, 7)
        hidden_states = jax.random.normal(ks[0], (BATCH, SEQ, HIDDEN), jnp.float32)
        router_indices = jax.random.randint(ks[1], (BATCH * SEQ, TOP_K), 0, NUM_EXPERTS)
        routing_weights = jax.nn.softmax(jax.random.normal(ks[2], (BATCH * SEQ, NUM_EXPERTS), jnp.float32), axis=-1)
        scale = 0.02
        gate_up_proj = jax.random.normal(ks[3], (NUM_EXPERTS, HIDDEN, 2 * INTER), jnp.float32) * scale
        gate_up_proj_bias = jax.random.normal(ks[4], (NUM_EXPERTS, 2 * INTER), jnp.float32) * scale
        down_proj = jax.random.normal(ks[5], (NUM_EXPERTS, INTER, HIDDEN), jnp.float32) * scale
        down_proj_bias = jax.random.normal(ks[6], (NUM_EXPERTS, HIDDEN), jnp.float32) * scale
        return {'hidden_states': hidden_states, 'router_indices': router_indices, 'routing_weights': routing_weights, 'gate_up_proj': gate_up_proj, 'gate_up_proj_bias': gate_up_proj_bias, 'down_proj': down_proj, 'down_proj_bias': down_proj_bias}
    _L2_ffn_all = _L2_ffn_setup()
    _L2_ffn_in = {k: v for k, v in _L2_ffn_all.items() if k in ('router_indices', 'routing_weights', 'gate_up_proj', 'gate_up_proj_bias', 'down_proj', 'down_proj_bias')}
    del _L2_ffn_all

    def _L3_xattn_setup():
        import jax, jax.numpy as jnp
        import numpy as np
        D_MODEL = 128
        NUM_HEADS = 16
        HEAD_DIM = D_MODEL // NUM_HEADS
        MAX_SEQ = 64

        def rope_tables(seq_len, dim):
            inv_freq = 1.0 / 10000.0 ** (jnp.arange(0, dim, 2, dtype=jnp.float32) / dim)
            t = jnp.arange(seq_len, dtype=jnp.float32)
            freqs = jnp.einsum('i,j->ij', t, inv_freq)
            emb = jnp.concatenate([freqs, freqs], axis=-1)
            return (jnp.cos(emb), jnp.sin(emb))

        def rotate_half(x):
            x1, x2 = jnp.split(x, 2, axis=-1)
            return jnp.concatenate([-x2, x1], axis=-1)
        key = jax.random.key(seed)
        ks = jax.random.split(key, 12)
        B, S, D = (16, 64, D_MODEL)
        s = 1.0 / np.sqrt(D)
        inp = {'query': jax.random.normal(ks[0], (B, S, D), jnp.float32), 'key': jax.random.normal(ks[1], (B, S, D), jnp.float32), 'value': jax.random.normal(ks[2], (B, S, D), jnp.float32), 'Wq': jax.random.normal(ks[3], (D, D), jnp.float32) * s, 'bq': jnp.zeros((D,), jnp.float32), 'Wk': jax.random.normal(ks[4], (D, D), jnp.float32) * s, 'bk': jnp.zeros((D,), jnp.float32), 'Wv': jax.random.normal(ks[5], (D, D), jnp.float32) * s, 'bv': jnp.zeros((D,), jnp.float32), 'Wo': jax.random.normal(ks[6], (D, D), jnp.float32) * s, 'bo': jnp.zeros((D,), jnp.float32)}
        return inp
    _L3_xattn_all = _L3_xattn_setup()
    _L3_xattn_in = {k: v for k, v in _L3_xattn_all.items() if k in ('Wq', 'bq', 'Wk', 'bk', 'Wv', 'bv', 'Wo', 'bo')}
    del _L3_xattn_all

    def _L3_ffn_setup():
        import jax, jax.numpy as jnp
        import numpy as np
        TOP_K = 8
        CAPACITY = 64

        def _silu(x):
            return x * jax.nn.sigmoid(x)
        key = jax.random.key(seed)
        ks = jax.random.split(key, 7)
        B, S, H, E, I, Is = (2, 128, 128, 64, 64, 256)
        s = 0.05
        return {'hidden_states': jax.random.normal(ks[0], (B, S, H), jnp.float32), 'gate_w': jax.random.normal(ks[1], (H, E), jnp.float32) * s, 'shared_gate_w': jax.random.normal(ks[2], (H, 1), jnp.float32) * s, 'shared_gate_up_w': jax.random.normal(ks[3], (H, 2 * Is), jnp.float32) * s, 'shared_down_w': jax.random.normal(ks[4], (Is, H), jnp.float32) * s, 'expert_gate_up_w': jax.random.normal(ks[5], (E, H, 2 * I), jnp.float32) * s, 'expert_down_w': jax.random.normal(ks[6], (E, I, H), jnp.float32) * s}
    _L3_ffn_all = _L3_ffn_setup()
    _L3_ffn_in = {k: v for k, v in _L3_ffn_all.items() if k in ('gate_w', 'shared_gate_w', 'shared_gate_up_w', 'shared_down_w', 'expert_gate_up_w', 'expert_down_w')}
    del _L3_ffn_all
    return {'x': x, 'ctx_1024': ctx_1024, 'mask_SxS2_bk1': mask_SxS2_bk1, 'L0_xattn_Wq': _L0_xattn_in['Wq'], 'L0_xattn_bq': _L0_xattn_in['bq'], 'L0_xattn_Wk': _L0_xattn_in['Wk'], 'L0_xattn_bk': _L0_xattn_in['bk'], 'L0_xattn_Wv': _L0_xattn_in['Wv'], 'L0_xattn_bv': _L0_xattn_in['bv'], 'L0_xattn_Wo': _L0_xattn_in['Wo'], 'L0_xattn_bo': _L0_xattn_in['bo'], 'L0_ffn_gate_w': _L0_ffn_in['gate_w'], 'L0_ffn_wg': _L0_ffn_in['wg'], 'L0_ffn_wu': _L0_ffn_in['wu'], 'L0_ffn_wd': _L0_ffn_in['wd'], 'L0_ffn_sg': _L0_ffn_in['sg'], 'L0_ffn_su': _L0_ffn_in['su'], 'L0_ffn_sd': _L0_ffn_in['sd'], 'L1_xattn_Wq': _L1_xattn_in['Wq'], 'L1_xattn_Wk': _L1_xattn_in['Wk'], 'L1_xattn_Wv': _L1_xattn_in['Wv'], 'L1_xattn_bq': _L1_xattn_in['bq'], 'L1_xattn_bk': _L1_xattn_in['bk'], 'L1_xattn_bv': _L1_xattn_in['bv'], 'L1_xattn_Wo': _L1_xattn_in['Wo'], 'L1_xattn_bo': _L1_xattn_in['bo'], 'L1_ffn_gate_w': _L1_ffn_in['gate_w'], 'L1_ffn_w1': _L1_ffn_in['w1'], 'L1_ffn_b1': _L1_ffn_in['b1'], 'L1_ffn_w2': _L1_ffn_in['w2'], 'L1_ffn_b2': _L1_ffn_in['b2'], 'L2_xattn_wq': _L2_xattn_in['wq'], 'L2_xattn_bq': _L2_xattn_in['bq'], 'L2_xattn_wk': _L2_xattn_in['wk'], 'L2_xattn_bk': _L2_xattn_in['bk'], 'L2_xattn_wv': _L2_xattn_in['wv'], 'L2_xattn_bv': _L2_xattn_in['bv'], 'L2_xattn_wo': _L2_xattn_in['wo'], 'L2_xattn_bo': _L2_xattn_in['bo'], 'L2_ffn_router_indices': _L2_ffn_in['router_indices'], 'L2_ffn_routing_weights': _L2_ffn_in['routing_weights'], 'L2_ffn_gate_up_proj': _L2_ffn_in['gate_up_proj'], 'L2_ffn_gate_up_proj_bias': _L2_ffn_in['gate_up_proj_bias'], 'L2_ffn_down_proj': _L2_ffn_in['down_proj'], 'L2_ffn_down_proj_bias': _L2_ffn_in['down_proj_bias'], 'L3_xattn_Wq': _L3_xattn_in['Wq'], 'L3_xattn_bq': _L3_xattn_in['bq'], 'L3_xattn_Wk': _L3_xattn_in['Wk'], 'L3_xattn_bk': _L3_xattn_in['bk'], 'L3_xattn_Wv': _L3_xattn_in['Wv'], 'L3_xattn_bv': _L3_xattn_in['bv'], 'L3_xattn_Wo': _L3_xattn_in['Wo'], 'L3_xattn_bo': _L3_xattn_in['bo'], 'L3_ffn_gate_w': _L3_ffn_in['gate_w'], 'L3_ffn_shared_gate_w': _L3_ffn_in['shared_gate_w'], 'L3_ffn_shared_gate_up_w': _L3_ffn_in['shared_gate_up_w'], 'L3_ffn_shared_down_w': _L3_ffn_in['shared_down_w'], 'L3_ffn_expert_gate_up_w': _L3_ffn_in['expert_gate_up_w'], 'L3_ffn_expert_down_w': _L3_ffn_in['expert_down_w']}

def reference(x, ctx_1024, mask_SxS2_bk1, L0_xattn_Wq, L0_xattn_bq, L0_xattn_Wk, L0_xattn_bk, L0_xattn_Wv, L0_xattn_bv, L0_xattn_Wo, L0_xattn_bo, L0_ffn_gate_w, L0_ffn_wg, L0_ffn_wu, L0_ffn_wd, L0_ffn_sg, L0_ffn_su, L0_ffn_sd, L1_xattn_Wq, L1_xattn_Wk, L1_xattn_Wv, L1_xattn_bq, L1_xattn_bk, L1_xattn_bv, L1_xattn_Wo, L1_xattn_bo, L1_ffn_gate_w, L1_ffn_w1, L1_ffn_b1, L1_ffn_w2, L1_ffn_b2, L2_xattn_wq, L2_xattn_bq, L2_xattn_wk, L2_xattn_bk, L2_xattn_wv, L2_xattn_bv, L2_xattn_wo, L2_xattn_bo, L2_ffn_router_indices, L2_ffn_routing_weights, L2_ffn_gate_up_proj, L2_ffn_gate_up_proj_bias, L2_ffn_down_proj, L2_ffn_down_proj_bias, L3_xattn_Wq, L3_xattn_bq, L3_xattn_Wk, L3_xattn_bk, L3_xattn_Wv, L3_xattn_bv, L3_xattn_Wo, L3_xattn_bo, L3_ffn_gate_w, L3_ffn_shared_gate_w, L3_ffn_shared_gate_up_w, L3_ffn_shared_down_w, L3_ffn_expert_gate_up_w, L3_ffn_expert_down_w):
    import jax
    import jax.numpy as jnp

    def _L0_xattn_ref(query, key, value, Wq, bq, Wk, bk, Wv, bv, Wo, bo):
        import jax, jax.numpy as jnp
        import numpy as np
        HID = 128
        HEADS = 16
        HEAD_DIM = HID // HEADS
        NEG = -10000000000.0
        B, S, _ = query.shape
        q = query @ Wq.T + bq
        k = key @ Wk.T + bk
        v = value @ Wv.T + bv
        q = q.reshape(B, S, HEADS, HEAD_DIM).transpose(0, 2, 1, 3)
        k = k.reshape(B, S, HEADS, HEAD_DIM).transpose(0, 2, 1, 3)
        v = v.reshape(B, S, HEADS, HEAD_DIM).transpose(0, 2, 1, 3)
        attn = jnp.einsum('bhqd,bhkd->bhqk', q, k)
        causal = jnp.tril(jnp.ones((S, S), dtype=bool))
        attn = jnp.where(causal, attn, NEG)
        attn = jax.nn.softmax(attn, axis=-1)
        x = jnp.einsum('bhqk,bhkd->bhqd', attn, v)
        x = x.transpose(0, 2, 1, 3).reshape(B, S, HID)
        return x @ Wo.T + bo

    def _L0_ffn_ref(x, gate_w, wg, wu, wd, sg, su, sd):
        import jax, jax.numpy as jnp
        import numpy as np
        DIM = 128
        INTER = 64
        E = 8
        TOP_K = 2
        ROUTE_SCALE = 1.0
        B, S, D = x.shape
        xf = x.reshape(-1, D)
        N = xf.shape[0]
        scores = jax.nn.softmax(xf @ gate_w.T, axis=-1)
        _, idx = jax.lax.top_k(scores, TOP_K)
        weights = jnp.take_along_axis(scores, idx, axis=-1) * ROUTE_SCALE
        cw = jnp.zeros((N, E), dtype=xf.dtype)
        cw = cw.at[jnp.arange(N)[:, None], idx].add(weights)
        g = jnp.einsum('nd,efd->nef', xf, wg)
        u = jnp.einsum('nd,efd->nef', xf, wu)
        h = jax.nn.silu(g) * u
        y = jnp.einsum('nef,edf->ned', h, wd)
        routed = jnp.einsum('ned,ne->nd', y, cw)
        shared = jax.nn.silu(xf @ sg.T) * (xf @ su.T) @ sd.T
        return (routed + shared).reshape(B, S, D)

    def _L1_xattn_ref(query, key, value, Wq, Wk, Wv, bq, bk, bv, Wo, bo):
        import jax, jax.numpy as jnp
        import numpy as np
        EMBED_DIM = 128
        NUM_HEADS = 16
        HEAD_DIM = EMBED_DIM // NUM_HEADS
        B, Tq, E = query.shape
        Tk = key.shape[1]
        H, hd = (NUM_HEADS, HEAD_DIM)
        q = query @ Wq.T + bq
        k = key @ Wk.T + bk
        v = value @ Wv.T + bv
        q = q.reshape(B, Tq, H, hd).transpose(0, 2, 1, 3)
        k = k.reshape(B, Tk, H, hd).transpose(0, 2, 1, 3)
        v = v.reshape(B, Tk, H, hd).transpose(0, 2, 1, 3)
        scores = jnp.einsum('bhqd,bhkd->bhqk', q, k) / jnp.sqrt(jnp.float32(hd))
        attn = jax.nn.softmax(scores, axis=-1)
        out = jnp.einsum('bhqk,bhkd->bhqd', attn, v)
        out = out.transpose(0, 2, 1, 3).reshape(B, Tq, E)
        return out @ Wo.T + bo

    def _L1_ffn_ref(x, gate_w, w1, b1, w2, b2):
        import jax, jax.numpy as jnp
        import numpy as np
        NUM_EXPERTS = 8
        N_EMBD = 128
        D_FF = 4 * N_EMBD
        B, S = (4, 256)
        Bb, Ss, D = x.shape
        x_flat = x.reshape(-1, D)
        router_logits = x_flat @ gate_w
        router_probs = jax.nn.softmax(router_logits, axis=-1)
        expert_idx = jnp.argmax(router_probs, axis=-1)
        expert_w = jnp.take_along_axis(router_probs, expert_idx[:, None], axis=1)[:, 0]
        out = jnp.zeros_like(x_flat)
        for e in range(NUM_EXPERTS):
            h = jax.nn.gelu(x_flat @ w1[e] + b1[e], approximate=False)
            y = h @ w2[e] + b2[e]
            sel = expert_idx == e
            out = out + jnp.where(sel, expert_w, 0.0)[:, None] * y
        return out.reshape(Bb, Ss, D)

    def _L2_xattn_ref(q, k, v, mask, wq, bq, wk, bk, wv, bv, wo, bo):
        import jax, jax.numpy as jnp
        import numpy as np
        import math
        D_MODEL = 128
        NUM_HEADS = 16
        D_K = D_MODEL // NUM_HEADS
        B, S = (4, 256)
        b = q.shape[0]

        def proj(x, w, bb):
            return (jnp.einsum('bsd,ed->bse', x, w) + bb).reshape(b, -1, NUM_HEADS, D_K).transpose(0, 2, 1, 3)
        qh = proj(q, wq, bq)
        kh = proj(k, wk, bk)
        vh = proj(v, wv, bv)
        scores = jnp.einsum('bhqd,bhkd->bhqk', qh, kh) / math.sqrt(D_K)
        scores = jnp.where(mask, jnp.float32(-1000000000.0), scores)
        probs = jax.nn.softmax(scores, axis=-1)
        out = jnp.einsum('bhqk,bhkd->bhqd', probs, vh)
        out = out.transpose(0, 2, 1, 3).reshape(b, -1, D_MODEL)
        return jnp.einsum('bsd,ed->bse', out, wo) + bo

    def _L2_ffn_ref(hidden_states, router_indices, routing_weights, gate_up_proj, gate_up_proj_bias, down_proj, down_proj_bias):
        import jax, jax.numpy as jnp
        import numpy as np
        NUM_EXPERTS = 8
        HIDDEN = 128
        INTER = 128
        BATCH = 2
        SEQ = 128
        TOP_K = 2
        SWIGLU_ALPHA = 1.702
        LIMIT = 7.0

        def _grouped_mm(x, w, expert_ids):
            onehot = jax.nn.one_hot(expert_ids, w.shape[0], dtype=x.dtype)
            y_all = jnp.einsum('tk,ekn->etn', x, w)
            return jnp.einsum('te,etn->tn', onehot, y_all)

        def _gpt_oss_swiglu(x):
            gate = jnp.minimum(x[..., ::2], LIMIT)
            up = jnp.clip(x[..., 1::2], -LIMIT, LIMIT)
            glu = gate * jax.nn.sigmoid(gate * SWIGLU_ALPHA)
            return (up + 1.0) * glu
        B = hidden_states.shape[0]
        H = hidden_states.shape[-1]
        x = hidden_states.reshape(-1, H)
        M = x.shape[0]
        top_k = router_indices.shape[1]
        num_experts = gate_up_proj.shape[0]
        topk_weights = jnp.take_along_axis(routing_weights, router_indices, axis=1)
        flat_experts = router_indices.reshape(-1)
        sort_idx = jnp.argsort(flat_experts)
        sorted_pos = sort_idx // top_k
        expert_sorted = flat_experts[sort_idx]
        grouped = x[sorted_pos]
        gate_up = _grouped_mm(grouped, gate_up_proj, expert_sorted)
        gate_up = gate_up + gate_up_proj_bias[expert_sorted]
        inter = _gpt_oss_swiglu(gate_up)
        down = _grouped_mm(inter, down_proj, expert_sorted)
        down = down + down_proj_bias[expert_sorted]
        down = down * topk_weights.reshape(-1)[sort_idx][:, None]
        out = jnp.zeros((M, H), x.dtype).at[sorted_pos].add(down)
        return out.reshape(B, -1, H)

    def _L3_xattn_ref(query, key, value, Wq, bq, Wk, bk, Wv, bv, Wo, bo):
        import jax, jax.numpy as jnp
        import numpy as np
        D_MODEL = 128
        NUM_HEADS = 16
        HEAD_DIM = D_MODEL // NUM_HEADS
        MAX_SEQ = 64

        def rope_tables(seq_len, dim):
            inv_freq = 1.0 / 10000.0 ** (jnp.arange(0, dim, 2, dtype=jnp.float32) / dim)
            t = jnp.arange(seq_len, dtype=jnp.float32)
            freqs = jnp.einsum('i,j->ij', t, inv_freq)
            emb = jnp.concatenate([freqs, freqs], axis=-1)
            return (jnp.cos(emb), jnp.sin(emb))

        def rotate_half(x):
            x1, x2 = jnp.split(x, 2, axis=-1)
            return jnp.concatenate([-x2, x1], axis=-1)
        B, S, D = query.shape
        H, Hd = (NUM_HEADS, HEAD_DIM)
        scale = Hd ** (-0.5)

        def proj(x, W, b):
            y = jnp.einsum('bsd,ed->bse', x, W) + b
            return y.reshape(B, S, H, Hd).transpose(0, 2, 1, 3)
        q = proj(query, Wq, bq)
        k = proj(key, Wk, bk)
        v = proj(value, Wv, bv)
        cos, sin = rope_tables(S, Hd)
        cos = cos[None, None]
        sin = sin[None, None]
        q = q * cos + rotate_half(q) * sin
        k = k * cos + rotate_half(k) * sin
        attn = jnp.einsum('bhqd,bhkd->bhqk', q, k) * scale
        attn_w = jax.nn.softmax(attn, axis=-1)
        out = jnp.einsum('bhqk,bhkd->bhqd', attn_w, v)
        out = out.transpose(0, 2, 1, 3).reshape(B, S, D)
        out = jnp.einsum('bsd,ed->bse', out, Wo) + bo
        return out

    def _L3_ffn_ref(hidden_states, gate_w, shared_gate_w, shared_gate_up_w, shared_down_w, expert_gate_up_w, expert_down_w):
        import jax, jax.numpy as jnp
        import numpy as np
        TOP_K = 8
        CAPACITY = 64

        def _silu(x):
            return x * jax.nn.sigmoid(x)
        B, S, H = hidden_states.shape
        x = hidden_states.reshape(-1, H)
        T = x.shape[0]
        E = gate_w.shape[1]
        Is = shared_gate_up_w.shape[1] // 2
        I = expert_gate_up_w.shape[2] // 2
        gu = x @ shared_gate_up_w
        shared = _silu(gu[:, :Is]) * gu[:, Is:] @ shared_down_w
        shared = shared * jax.nn.sigmoid(x @ shared_gate_w)
        logits = x @ gate_w
        probs = jax.nn.softmax(logits.astype(jnp.float32), axis=-1)
        w, idx = jax.lax.top_k(probs, TOP_K)
        w = (w / jnp.sum(w, axis=-1, keepdims=True)).astype(x.dtype)
        e_flat = idx.reshape(-1)
        w_flat = w.reshape(-1)
        A = e_flat.shape[0]
        tok = jnp.arange(A) // TOP_K
        onehot = jax.nn.one_hot(e_flat, E, dtype=jnp.int32)
        pos = jnp.take_along_axis(jnp.cumsum(onehot, axis=0) - 1, e_flat[:, None], axis=1)[:, 0]
        slot = jnp.minimum(pos, CAPACITY)
        buf = jnp.zeros((E, CAPACITY + 1, H), x.dtype).at[e_flat, slot].set(x[tok])
        gu_e = jnp.einsum('ech,ehf->ecf', buf, expert_gate_up_w)
        act = _silu(gu_e[..., :I]) * gu_e[..., I:]
        out_e = jnp.einsum('eci,eih->ech', act, expert_down_w)
        y = out_e[e_flat, slot] * w_flat[:, None]
        y = jnp.where((pos < CAPACITY)[:, None], y, jnp.zeros_like(y))
        y = y.reshape(T, TOP_K, H).sum(axis=1)
        return (y + shared).reshape(B, S, H)
    x = x + _L0_xattn_ref(_layernorm(x, axis=-1), ctx_1024, ctx_1024, L0_xattn_Wq, L0_xattn_bq, L0_xattn_Wk, L0_xattn_bk, L0_xattn_Wv, L0_xattn_bv, L0_xattn_Wo, L0_xattn_bo)
    x = x + _L0_ffn_ref(_layernorm(x, axis=-1), L0_ffn_gate_w, L0_ffn_wg, L0_ffn_wu, L0_ffn_wd, L0_ffn_sg, L0_ffn_su, L0_ffn_sd)
    x = x + _L1_xattn_ref(_layernorm(x, axis=-1), ctx_1024, ctx_1024, L1_xattn_Wq, L1_xattn_Wk, L1_xattn_Wv, L1_xattn_bq, L1_xattn_bk, L1_xattn_bv, L1_xattn_Wo, L1_xattn_bo)
    x = x + _L1_ffn_ref(_layernorm(x, axis=-1), L1_ffn_gate_w, L1_ffn_w1, L1_ffn_b1, L1_ffn_w2, L1_ffn_b2)
    x = x + _L2_xattn_ref(_layernorm(x, axis=-1), ctx_1024, ctx_1024, mask_SxS2_bk1, L2_xattn_wq, L2_xattn_bq, L2_xattn_wk, L2_xattn_bk, L2_xattn_wv, L2_xattn_bv, L2_xattn_wo, L2_xattn_bo)
    x = x + _L2_ffn_ref(_layernorm(x, axis=-1), L2_ffn_router_indices, L2_ffn_routing_weights, L2_ffn_gate_up_proj, L2_ffn_gate_up_proj_bias, L2_ffn_down_proj, L2_ffn_down_proj_bias)
    x = x + _L3_xattn_ref(_layernorm(x, axis=-1), ctx_1024, ctx_1024, L3_xattn_Wq, L3_xattn_bq, L3_xattn_Wk, L3_xattn_bk, L3_xattn_Wv, L3_xattn_bv, L3_xattn_Wo, L3_xattn_bo)
    x = x + _L3_ffn_ref(_layernorm(x, axis=-1), L3_ffn_gate_w, L3_ffn_shared_gate_w, L3_ffn_shared_gate_up_w, L3_ffn_shared_down_w, L3_ffn_expert_gate_up_w, L3_ffn_expert_down_w)
    return x

_drawn_inputs = setup_inputs


def setup_inputs(seed=0):
    import zlib

    import numpy as np

    out = dict(_drawn_inputs(seed))
    spreads = {'L0_xattn_bq': (0.0, 0.1),
     'L0_xattn_bk': (0.0, 2.0),
     'L0_xattn_bv': (0.0, 0.1),
     'L0_xattn_bo': (0.0, 0.1),
     'L1_xattn_bq': (0.0, 0.726),
     'L1_xattn_bk': (0.0, 2.0),
     'L1_xattn_bv': (0.0, 0.1),
     'L1_xattn_bo': (0.0, 0.1),
     'L1_ffn_b1': (0.0, 0.8),
     'L1_ffn_b2': (0.0, 0.8),
     'L3_xattn_bq': (0.0, 0.8),
     'L3_xattn_bk': (0.0, 0.8),
     'L3_xattn_bv': (0.0, 0.1),
     'L3_xattn_bo': (0.0, 0.1)}
    factors = {'L0_ffn_gate_w': 3.789,
     'L0_ffn_wg': 3.427,
     'L0_ffn_wu': 3.353,
     'L0_ffn_wd': 3.333,
     'L1_ffn_gate_w': 6.02,
     'L1_ffn_w1': 8.0,
     'L1_ffn_w2': 8.0,
     'L2_ffn_routing_weights': 8.0,
     'L2_ffn_gate_up_proj': 8.0,
     'L2_ffn_gate_up_proj_bias': 8.0,
     'L2_ffn_down_proj': 8.0,
     'L2_ffn_down_proj_bias': 8.0,
     'L3_ffn_gate_w': 8.0,
     'L3_ffn_shared_gate_w': 47.864,
     'L3_ffn_expert_gate_up_w': 8.0,
     'L3_ffn_expert_down_w': 8.0,
     'L3_ffn_shared_gate_up_w': 7.774,
     'L3_ffn_shared_down_w': 7.812}
    for name, (base, spread) in spreads.items():
        noise = np.random.default_rng([zlib.crc32(name.encode()), seed]).standard_normal(out[name].shape)
        drawn = base * np.exp(spread * noise) if base else spread * noise
        out[name] = jnp.asarray(drawn.astype(out[name].dtype))
    for name, factor in factors.items():
        out[name] = (out[name] * factor).astype(out[name].dtype)
    return out
```

```python
from contextlib import ExitStack

import numpy as np

import concourse.bass as bass
from concourse import mybir

F32 = mybir.dt.float32
BF16 = mybir.dt.bfloat16
I32 = mybir.dt.int32
U8 = mybir.dt.uint8
ALU = mybir.AluOpType
ACT = mybir.ActivationFunctionType
AX = mybir.AxisListType.X

P = 128
NT = 32
T = NT * P
GT = 4
GN = GT * P
NG = NT // GT
H, HD = 16, 8
TERMS = 6
SR = TERMS * HD
EPS = 1e-5
NEG = -float(2 ** 60)
STACKS = 3
FIRST_SEMAPHORE = 128
CAPACITY = 64
ZERO_COLS = (T + CAPACITY) // 4
Q_PARTS = (0, 0, 0, 1, 1, 2)
K_PARTS = (0, 1, 2, 0, 1, 0)


class Core:
    pass


def semaphores(nc, c, prefix, names):
    taken = [c.ctx.enter_context(nc.semaphore(f"{prefix}_{n}", num=c.next_semaphore + k))
             for k, n in enumerate(names.split())]
    c.next_semaphore += len(taken)
    return taken


def zero_semaphores(nc, c):
    with nc.Block() as block:
        @block.gpsimd
        def _(pool):
            pool.sem_clear(range(FIRST_SEMAPHORE, c.next_semaphore))


def done(n, credit=2):
    return n + (1 + credit)


def free(n):
    return n + 1


def ln_vector(nc, c, dve, sems):
    var_ready, root_ready, chain = sems
    nc.vector.tensor_scalar(c.veps[:], c.mv[:, :, 1], EPS, None, ALU.add).then_inc(var_ready, 1)
    dve.wait_ge(root_ready, 1)
    nc.vector.reciprocal(c.rstd0[:], c.root[:]).then_inc(chain, 1)
    dve.wait_ge(chain, 1)
    nc.vector.tensor_tensor(c.newt[:], c.rstd0[:], c.rstd0[:], ALU.mult).then_inc(chain, 1)
    dve.wait_ge(chain, 2)
    nc.vector.tensor_tensor(c.newt[:], c.newt[:], c.veps[:], ALU.mult).then_inc(chain, 1)
    dve.wait_ge(chain, 3)
    nc.vector.tensor_scalar(c.newt[:], c.newt[:], -0.5, 1.5, ALU.mult, ALU.add).then_inc(chain, 1)
    dve.wait_ge(chain, 4)
    nc.vector.tensor_tensor(c.rstd[:], c.newt[:], c.rstd0[:], ALU.mult).then_inc(chain, 1)
    dve.wait_ge(chain, 5)


def ln_scalar(nc, c, act, sems):
    var_ready, root_ready, _ = sems
    act.wait_ge(var_ready, 1)
    nc.scalar.activation(c.root[:], c.veps[:], ACT.Sqrt).then_inc(root_ready, 1)


def scratch(nc, ctx, prefix, shapes):
    for name, (shape, dt) in shapes.items():
        yield ctx.enter_context(nc.sbuf_tensor(f"{prefix}_{name}", shape, dt))


def run_steps(engine, step, first, unroll, loops, last):
    for i in range(first):
        step(i, 0)
    with engine.Fori(0, loops) as r:
        for j in range(unroll):
            step(first + j, r)
    for i in range(first + unroll * loops, last):
        step(i, 0)


class Item:

    def __init__(self, n, r, unroll, total=NT):
        self.n, self.r, self.unroll = n, r, unroll
        self.live = not isinstance(r, int) or 0 <= n < total
        self.b = n % 2
        self.stack = (n // 2) % STACKS
        self.half = slice((n % 2) * P, (n % 2) * P + P)

    def items(self, k, m=0):
        return self.r * (self.unroll * k) + (self.n * k + m)

    @property
    def t(self):
        return self.items(1)

    @property
    def turn(self):
        return self.r * (self.unroll // 2) + self.n // 2

    @property
    def fill(self):
        return self.r * (self.unroll // 2 // STACKS) + self.n // 2 // STACKS


def project(nc, c, layer):
    rope = layer == 3

    pre = f"p{layer}"
    ln = semaphores(nc, c, pre, "var root chain")
    (xn_ready, xt_psum, xt_ready, q_psum, k_psum, v_psum, ctx_ready, v_ready,
     hi_ready, res_ready, mid_ready, lo_ready, turned, roped) = semaphores(
        nc, c, pre, "xn xtp xt q k v ctx vdone hi res mid lo turned roped")
    parts_out = semaphores(nc, c, pre, "out0 out1")
    wq, wk, wv = (c.wa[:, layer, n, :] for n in range(3))
    bias = [c.bcol[:, 2 * layer + n:2 * layer + n + 1] for n in range(2)]
    xt_bank = [c.bank[n] for n in (0, 1)]
    qk_bank = [[c.bank[2], c.bank[3]], [c.bank[4], c.bank[5]]]
    v_bank = [c.bank[n] for n in (6, 7)]

    with ExitStack() as own, nc.Block() as block:
        c.xn, c.xnT, c.ctxg, c.parts, c.resid = scratch(nc, own, pre, dict(
            xn=([P, 2, GT, P], F32), xnT=([P, 2, GN], F32), ctxg=([P, 2, GN], F32),
            parts=([P, 2, 2, 3, GN], BF16), resid=([P, 2, 2, GN], F32)))
        if rope:
            c.roped, c.rot = scratch(nc, own, pre, dict(roped=([P, 2, 2, GN], F32), rot=([P, 2, GT, P], F32)))

        @block.gpsimd
        def _(pool):
            pool.sem_inc(ctx_ready, 2)
            pool.sem_inc(lo_ready, 4)
            with pool.Fori(0, NG // 2) as it:
                for b in range(2):
                    g = it * 2 + b
                    pool.wait_ge(v_psum, free(g))
                    nc.gpsimd.tensor_copy(c.ctxg[:, b, :], c.ctxT[:, bass.ds(g * GN, GN)]).then_inc(ctx_ready, 1)
                    pool.wait_ge(xn_ready, done(g))
                    nc.gpsimd.tensor_tensor(
                        c.x[:, bass.ds(g * GT, GT), :], c.x[:, bass.ds(g * GT, GT), :],
                        c.brow[:, 2 * layer + 1:2 * layer + 2, :].to_broadcast([P, GT, P]), ALU.add)
                    for n in range(2):
                        m = g * 2 + n
                        pool.wait_ge(mid_ready, done(m, 4))
                        nc.gpsimd.tensor_tensor(c.parts[:, b, n, 2, :], c.resid[:, b, n, :],
                                                c.parts[:, b, n, 1, :], ALU.subtract).then_inc(lo_ready, 1)

        @block.vector
        def _(dve):
            dve.sem_inc(xn_ready, 2)
            dve.sem_inc(v_ready, 2)
            dve.sem_inc(res_ready, 4)
            if rope:
                dve.sem_inc(roped, 2)
            ln_vector(nc, c, dve, ln)
            with dve.Fori(0, NG // 2) as it:
                for b in range(2):
                    g = it * 2 + b
                    dve.wait_ge(xt_psum, free(g))
                    for j in range(GT):
                        t = g * GT + j
                        last = nc.vector.tensor_scalar(c.xn[:, b, j, :], c.x[:, t, :], c.mv[:, t, 0:1],
                                                       c.rstd[:, bass.ds(t, 1)], ALU.subtract, ALU.mult)
                    last.then_inc(xn_ready, 1)
                    for n, psum in enumerate((q_psum, k_psum)):
                        m = g * 2 + n
                        dve.wait_ge(psum, done(g))
                        if rope:
                            main, rot = (qk_bank[n][k].rearrange("p (j t) -> p j t", j=GT) for k in range(2))
                            cos = c.rope[:, 0:1, :].to_broadcast([P, GT, P])
                            sin = c.rope[:, 1:2, :].to_broadcast([P, GT, P])
                            nc.vector.scalar_tensor_tensor(c.rot[:, 0], main, bias[n], cos, ALU.add, ALU.mult)
                            nc.vector.scalar_tensor_tensor(c.rot[:, 1], rot, c.bcol[:, 8 + n:9 + n], sin,
                                                           ALU.add, ALU.mult).then_inc(turned, 1)
                            dve.wait_ge(turned, m + 1)
                            dve.wait_ge(hi_ready, free(m))
                            nc.vector.tensor_tensor(c.roped[:, b, n, :], c.rot[:, 0].rearrange("p j t -> p (j t)"),
                                                    c.rot[:, 1].rearrange("p j t -> p (j t)"),
                                                    ALU.add).then_inc(roped, 1)
                        dve.wait_ge(hi_ready, done(m, 4))
                        dve.wait_ge(lo_ready, free(m))
                        if rope:
                            nc.vector.tensor_tensor(c.resid[:, b, n, :], c.roped[:, b, n, :],
                                                    c.parts[:, b, n, 0, :], ALU.subtract).then_inc(res_ready, 1)
                        else:
                            nc.vector.scalar_tensor_tensor(c.resid[:, b, n, :], qk_bank[n][b], bias[n],
                                                           c.parts[:, b, n, 0, :], ALU.add,
                                                           ALU.subtract).then_inc(res_ready, 1)
                    dve.wait_ge(v_psum, done(g))
                    nc.vector.tensor_tensor(
                        c.v[:, bass.ds(g * GT, GT), :], v_bank[b].rearrange("p (j f) -> p j f", j=GT),
                        c.brow[:, 2 * layer:2 * layer + 1, :].to_broadcast([P, GT, P]), ALU.add
                    ).then_inc(v_ready, 1)

        @block.scalar
        def _(act):
            act.sem_inc(xt_ready, 2)
            act.sem_inc(hi_ready, 4)
            act.sem_inc(mid_ready, 4)
            ln_scalar(nc, c, act, ln)
            with act.Fori(0, NG // 2) as it:
                for b in range(2):
                    g = it * 2 + b
                    act.wait_ge(xt_psum, done(g))
                    act.wait_ge(q_psum, free(g))
                    nc.scalar.activation(c.xnT[:, b, :], xt_bank[b], ACT.Identity).then_inc(xt_ready, 1)
                    act.wait_ge(parts_out[b], it * 32 + 32)
                    for n, psum in enumerate((q_psum, k_psum)):
                        m = g * 2 + n
                        if rope:
                            act.wait_ge(roped, done(m))
                            nc.scalar.activation(c.parts[:, b, n, 0, :], c.roped[:, b, n, :],
                                                 ACT.Identity).then_inc(hi_ready, 1)
                        else:
                            act.wait_ge(psum, done(g))
                            nc.scalar.activation(c.parts[:, b, n, 0, :], qk_bank[n][b], ACT.Identity,
                                                 bias=bias[n]).then_inc(hi_ready, 1)
                    for n in range(2):
                        act.wait_ge(res_ready, done(g * 2 + n, 4))
                        nc.scalar.activation(c.parts[:, b, n, 1, :], c.resid[:, b, n, :],
                                             ACT.Identity).then_inc(mid_ready, 1)

        @block.tensor
        def _(pe):
            for s in (xt_psum, q_psum, k_psum, v_psum):
                pe.sem_inc(s, 2)
            with pe.Fori(0, NG // 2) as it:
                for b in range(2):
                    g = it * 2 + b
                    pe.wait_ge(xn_ready, done(g))
                    pe.wait_ge(xt_ready, free(g))
                    for j in range(GT):
                        last = nc.tensor.transpose(xt_bank[b][:, j * P:(j + 1) * P], c.xn[:, b, j, :], c.ident[:])
                    last.then_inc(xt_psum, 1)
                    pe.wait_ge(xt_ready, done(g))
                    keys = c.ctxT[:, bass.ds(g * GN, GN)]
                    for n, (psum, w, src) in enumerate(((q_psum, wq, c.xnT[:, b, :]), (k_psum, wk, keys))):
                        m = g * 2 + n
                        if rope:
                            pe.wait_ge(roped, m + 1)
                            nc.tensor.matmul(qk_bank[n][0], w, src, start=True, stop=True)
                            nc.tensor.matmul(qk_bank[n][1], c.wrot[:, n, :], src, start=True,
                                             stop=True).then_inc(psum, 1)
                        else:
                            pe.wait_ge(res_ready, free(m))
                            nc.tensor.matmul(qk_bank[n][b], w, src, start=True, stop=True).then_inc(psum, 1)
                    pe.wait_ge(ctx_ready, done(g))
                    pe.wait_ge(v_ready, free(g))
                    for j in range(GT):
                        last = nc.tensor.matmul(v_bank[b][:, j * P:(j + 1) * P], c.ctxg[:, b, j * P:(j + 1) * P],
                                                wv, start=True, stop=True)
                    last.then_inc(v_psum, 1)

        @block.sync
        def _(sp):
            for s in parts_out:
                sp.sem_inc(s, 32)
            with sp.Fori(0, NG // 2) as it:
                for b in range(2):
                    g = it * 2 + b
                    sp.wait_ge(lo_ready, done(g * 2 + 1, 4))
                    for n in range(2):
                        sp.dma_start(c.parts_dram[n][:, :, bass.ds(g * GN, GN)],
                                     c.parts[:, b, n, :, :]).then_inc(parts_out[b], 16)
            for s in parts_out:
                sp.wait_ge(s, 32 * (NG // 2 + 1))


def attend(nc, c, layer):
    scale = 1.0 if layer == 0 else float(1 / np.sqrt(np.float32(HD)))
    mask = {0: 0, 2: 1}.get(layer)

    (scores, maxed, m_ready, mt_psum, mt_ready, st_psum, exp_ready, vx_ready, pv_psum, pv_ready,
     n_psum, rd_ready, n_ready, at_psum, at_ready, y_psum, x_ready, stats_ready, hi_ready,
     mv_ready, x_stored) = semaphores(
        nc, c, f"a{layer}", "s max m mtp mt st exp vx pvp pv np rd n atp at y x bn hi mv xst")
    m_rows = semaphores(nc, c, f"a{layer}", "row0 row1")
    stacked = semaphores(nc, c, f"a{layer}", "stack0 stack1 stack2")
    wo = c.wa[:, layer, 3, :]
    s_bank = [c.bank[n].rearrange("p (h k) -> p h k", h=4) for n in (0, 1)]
    st_bank = [c.bank[n] for n in (2, 3)]
    pv = c.bank[4][:, 0:2 * P].rearrange("p (a q) -> p a q", a=2)
    back = c.bank[5][:, 0:2 * P]
    at = c.bank[6][:, 0:P]
    mt = c.bank[6][:, P:P + P // 2].bitcast(BF16)
    y = c.bank[7][:, 0:P]
    LAG = dict(S=0, M=1, ST=2, PV=3, BACK=4, AT=5, Y=6, X=7)
    FIRST, LOOPS, U = 8, 4, 6
    LAST = NT + LAG["X"]

    def steps(engine, step, loops=LOOPS):
        run_steps(engine, step, FIRST, U, loops, LAST)

    def Tile(i, r, lag):
        return Item(i - lag, r, U)

    with ExitStack() as own, nc.Block() as block:
        c.pt, c.m, c.mneg, c.mt, c.pvs, c.rd, c.an, c.at = scratch(nc, own, f"a{layer}", dict(
            pt=([P, 2, H, P], F32), m=([P, 2, H], F32), mneg=([P, 2, 2 * H], BF16), mt=([2 * H, 2, P], BF16),
            pvs=([P, 2, 2, P], F32), rd=([P, 2, H], F32), an=([P, 2, P], F32), at=([P, 2, P], F32)))

        @block.tensor
        def _(pe):
            for s in (scores, st_psum, mt_psum, pv_psum, n_psum, at_psum, y_psum):
                pe.sem_inc(s, 2)

            def quarter(a, q):
                if not a.live:
                    return
                n = a.items(4, q)
                pe.wait_ge(maxed, free(n))
                if q == 0 and a.n % 2 == 0:
                    pe.wait_ge(stacked[a.stack], a.fill * c.STACK_INCS + c.STACK_INCS)
                for h in range(4):
                    last = nc.tensor.matmul(s_bank[q % 2][:, h, :], c.qs[:, a.stack, 4 * q + h, a.half],
                                            c.ks[:, a.stack, 4 * q + h, a.half], start=mask is None or h == 0,
                                            stop=mask is None)
                if mask is not None:
                    last = nc.tensor.matmul(s_bank[q % 2], c.identb[:], c.mask[:, mask, 0],
                                            start=False, stop=True)
                last.then_inc(scores, 1)

            def turned_quarter(a, q):
                if not a.live:
                    return
                n = a.items(4, q)
                if q == 0:
                    pe.wait_ge(m_rows[a.b], a.turn * 32 + 32)
                pe.wait_ge(exp_ready, free(n))
                for h in range(4):
                    last = nc.tensor.matmul(st_bank[q % 2][:, h * P:(h + 1) * P],
                                            c.ks[:, a.stack, 4 * q + h, a.half],
                                            c.qs[:, a.stack, 4 * q + h, a.half],
                                            start=mask is None or h == 0, stop=mask is None)
                if mask is not None:
                    last = nc.tensor.matmul(st_bank[q % 2], c.identb[:],
                                            c.mask[:, mask, 1].rearrange("p h k -> p (h k)"),
                                            start=False, stop=True)
                last.then_inc(st_psum, 1)

            def values(a, f):
                if not a.live:
                    return
                if f == 0:
                    pe.wait_ge(vx_ready, done(a.t))
                    pe.wait_ge(pv_ready, a.items(1, 2))
                pe.wait_ge(exp_ready, done(a.items(4, 2 * f + 1)))
                for odd in range(2):
                    for g in range(4):
                        h = 8 * f + 2 * g + odd
                        last = nc.tensor.matmul(pv[32 * g:32 * g + 32, f, :], c.vx[:, a.b, h, :],
                                                c.pt[:, a.b, h, :], start=odd == 0, stop=odd == 1)
                if f == 1:
                    last.then_inc(pv_psum, 1)

            def step(i, r):
                s, m, st, v, bk, a, yy = (Tile(i, r, LAG[k]) for k in ("S", "M", "ST", "PV", "BACK", "AT", "Y"))
                quarter(s, 0)
                turned_quarter(st, 0)
                if m.live:
                    pe.wait_ge(m_ready, done(m.t))
                    pe.wait_ge(mt_ready, m.items(1, 2))
                    if yy.live:
                        pe.wait_ge(at_ready, done(yy.t))
                    nc.tensor.transpose(mt[0:2 * H, :], c.mneg[:, m.b, :], c.identb[:]).then_inc(mt_psum, 1)
                turned_quarter(st, 1)
                quarter(s, 1)
                values(v, 0)
                quarter(s, 2)
                turned_quarter(st, 2)
                if bk.live:
                    pe.wait_ge(pv_ready, done(bk.t))
                    pe.wait_ge(n_ready, bk.items(1, 2))
                    for f in range(2):
                        last = nc.tensor.transpose(back[:, f * P:(f + 1) * P], c.pvs[:, bk.b, f, :], c.ident[:])
                    last.then_inc(n_psum, 1)
                turned_quarter(st, 3)
                quarter(s, 3)
                values(v, 1)
                if a.live:
                    pe.wait_ge(n_ready, done(a.t))
                    if m.live:
                        pe.wait_ge(mt_ready, done(m.t))
                    pe.wait_ge(at_ready, a.items(1, 2))
                    nc.tensor.transpose(at, c.an[:, a.b, :], c.ident[:]).then_inc(at_psum, 1)
                if yy.live:
                    pe.wait_ge(at_ready, done(yy.t))
                    pe.wait_ge(x_ready, yy.items(1, 2))
                    nc.tensor.matmul(y, c.at[:, yy.b, :], wo, start=True, stop=True).then_inc(y_psum, 1)

            steps(pe, step)

        @block.vector
        def _(dve):
            for s in (maxed, m_ready, n_ready, x_ready):
                dve.sem_inc(s, 2)

            def quarter_max(a, q):
                if not a.live:
                    return
                n = a.items(4, q)
                dve.wait_ge(scores, done(n))
                if q == 0:
                    dve.wait_ge(m_ready, free(a.t))
                nc.vector.reduce_max(c.m[:, a.b, 4 * q:4 * q + 4], s_bank[q % 2], AX).then_inc(maxed, 1)

            def step(i, r):
                s, bk, xx = (Tile(i, r, LAG[k]) for k in ("S", "BACK", "X"))
                quarter_max(s, 0)
                if xx.live:
                    dve.wait_ge(y_psum, done(xx.t))
                    dve.wait_ge(x_stored, free(xx.t))
                    nc.vector.tensor_tensor(c.xs[:, xx.b, :], c.x[:, xx.t, :], y, ALU.add).then_inc(x_ready, 1)
                    dve.wait_ge(x_ready, done(xx.t))
                    nc.vector.bn_stats(c.stats[:, xx.b, :], c.xs[:, xx.b, :]).then_inc(stats_ready, 1)
                if xx.live:
                    dve.wait_ge(stats_ready, xx.t + 1)
                quarter_max(s, 1)
                if xx.live:
                    nc.vector.bn_aggr(c.mvs[:, xx.b, :], c.stats[:, xx.b, :]).then_inc(mv_ready, 1)
                quarter_max(s, 2)
                if bk.live:
                    dve.wait_ge(n_psum, done(bk.t))
                    heads = back.rearrange("p (h e) -> p h e", h=H)
                    nc.vector.reciprocal(c.rd[:, bk.b, :], heads[:, :, HD]).then_inc(rd_ready, 1)
                    dve.wait_ge(rd_ready, bk.t + 1)
                    dve.wait_ge(at_psum, free(bk.t))
                    nc.vector.tensor_tensor(c.an[:, bk.b, :].rearrange("p (h d) -> p h d", h=H), heads[:, :, 0:HD],
                                            c.rd[:, bk.b, :].rearrange("p (h a) -> p h a", a=1).to_broadcast([P, H, HD]),
                                            ALU.mult).then_inc(n_ready, 1)
                quarter_max(s, 3)
                if s.live:
                    dve.wait_ge(maxed, done(s.items(4, 3)))
                    dve.wait_ge(mt_psum, free(s.t))
                    nc.vector.tensor_scalar(c.mneg[:, s.b, 0:H], c.m[:, s.b, :], -1.0, None, ALU.mult).then_inc(hi_ready, 1)
                    dve.wait_ge(hi_ready, s.t + 1)
                    nc.vector.scalar_tensor_tensor(c.mneg[:, s.b, H:2 * H], c.m[:, s.b, :], -1.0,
                                                   c.mneg[:, s.b, 0:H], ALU.mult, ALU.subtract).then_inc(m_ready, 1)

            steps(dve, step)

        @block.scalar
        def _(act):
            for s in (mt_ready, exp_ready, pv_ready, at_ready):
                act.sem_inc(s, 2)

            def exponentials(a, q):
                if not a.live:
                    return
                act.wait_ge(st_psum, done(a.items(4, q)))
                if q == 0:
                    act.wait_ge(pv_psum, free(a.t))
                nc.scalar.activation(c.pt[:, a.b, 4 * q:4 * q + 4, :].rearrange("p h q -> p (h q)"),
                                     st_bank[q % 2], ACT.Exp, scale=scale).then_inc(exp_ready, 1)

            def step(i, r):
                m, st, v, yy = (Tile(i, r, LAG[k]) for k in ("M", "ST", "PV", "Y"))
                if yy.live:
                    act.wait_ge(at_psum, done(yy.t))
                    act.wait_ge(y_psum, free(yy.t))
                    nc.scalar.activation(c.at[:, yy.b, :], at, ACT.Identity).then_inc(at_ready, 1)
                exponentials(st, 0)
                if m.live:
                    act.wait_ge(mt_psum, done(m.t))
                    act.wait_ge(m_rows[m.b], m.turn * 32)
                    nc.scalar.activation(c.mt[:, m.b, :], mt[0:2 * H, :], ACT.Identity).then_inc(mt_ready, 1)
                for q in (1, 2, 3):
                    exponentials(st, q)
                if v.live:
                    act.wait_ge(pv_psum, done(v.t))
                    act.wait_ge(n_psum, free(v.t))
                    nc.scalar.activation(c.pvs[:, v.b], pv, ACT.Identity).then_inc(pv_ready, 1)

            steps(act, step)

        @block.gpsimd
        def _(pool):
            pool.sem_inc(vx_ready, 2)
            pool.sem_inc(x_stored, 2)

            def step(i, r):
                spread_values(Tile(i, r, LAG["M"]))
                store(Tile(i, r, LAG["X"]))

            def store(a):
                if not a.live:
                    return
                pool.wait_ge(mv_ready, a.t + 1)
                nc.gpsimd.tensor_copy(c.x[:, a.t, :], c.xs[:, a.b, :])
                nc.gpsimd.tensor_copy(c.mv[:, a.t, :], c.mvs[:, a.b, :]).then_inc(x_stored, 1)

            def spread_values(a):
                if not a.live:
                    return
                pool.wait_ge(pv_psum, free(a.t))
                src = c.v[:, a.t, :].rearrange("p (g o d) -> p g o d", o=2, d=HD)
                dst = c.vx[:, a.b].rearrange("p (g o) e -> p g o e", o=2)
                for odd in range(2):
                    last = nc.gpsimd.tensor_copy(dst[:, :, odd, 16 * odd:16 * odd + HD], src[:, :, odd, :])
                last.then_inc(vx_ready, 1)

            steps(pool, step)

        @block.sync
        def _(sp):
            def load(a):
                incs = stacked[a.stack]
                pair = bass.ds(a.t * P, 2 * P)
                for dst, dram, parts in ((c.qs, c.parts_dram[0], Q_PARTS), (c.ks, c.parts_dram[1], K_PARTS)):
                    rows = dram.rearrange("(h d) c t -> c d h t", d=HD)
                    for s, part in enumerate(parts):
                        sp.dma_start(dst[HD * s:HD * s + HD, a.stack], rows[part][:, :, pair]).then_inc(incs, 16)
                sp.dma_start(c.qs[SR:SR + 2, a.stack], c.zeros[:]).then_inc(incs, 16)

            for p in range(2):
                load(Tile(2 * p, 0, 0))

            def step(i, r):
                m = Tile(i, r, LAG["M"])
                if m.live:
                    sp.wait_ge(mt_ready, done(m.t))
                    for row in range(2):
                        sp.dma_start(c.qs[SR + row:SR + row + 1, m.stack, :, m.half],
                                     c.mt[row * H:(row + 1) * H, m.b, :]).then_inc(m_rows[m.b], 16)
                nxt = Tile(i, r, -3)
                if i % 2 == 1 and nxt.live:
                    if not isinstance(r, int) or i >= 3:
                        sp.wait_ge(st_psum, done(Tile(i, r, 2).items(4, 3)))
                    load(nxt)

            steps(sp, step, LOOPS - 1)
            for row in range(2):
                sp.wait_ge(m_rows[row], NT // 2 * 32)


def route(nc, c, layer, experts, top, loads):
    pre = f"r{layer}"
    ln = semaphores(nc, c, pre, "var root chain")
    (xn_ready, xt_psum, xt_ready, xt_kept, log_psum, log_ready, soft, exp_ready, gate_in) = semaphores(
        nc, c, pre, "xn xtp xt keep lp log soft exp gate")
    loaded, = semaphores(nc, c, pre, "loaded")
    table_out = semaphores(nc, c, pre, "out0 out1")
    E = loads[0][0].shape[-1]
    gate = loads[0][0]
    big = layer == 3
    xt_bank, log_bank = [c.bank[n] for n in (0, 1)], [c.bank[n] for n in (2, 3)]
    with ExitStack() as own, nc.Block() as block:
        xn, xnT, logits, mx, tot = scratch(nc, own, pre, dict(
            xn=([P, 2, GT, P], F32), xnT=([P, 2, GN], F32), logits=([P, NT, E], F32), mx=([P, NT], F32),
            tot=([P, NT], F32)))
        if not big:
            above, equal, rank = scratch(nc, own, pre, dict(
                above=([P, NT, experts, experts], F32), equal=([P, NT, experts, experts], F32),
                rank=([P, NT, experts], F32)))
        else:
            top8, rest = scratch(nc, own, pre, dict(top8=([P, NT, 8], F32), rest=([P, NT, experts], F32)))
        scores = logits[:, :, 0:experts]

        @block.sync
        def _(sp):
            sp.dma_start(gate, loads[0][1]).then_inc(gate_in, 16)
            for dst, src in loads[1:]:
                sp.dma_start(dst, src).then_inc(loaded, 16)
            if big:
                for s in table_out:
                    sp.sem_inc(s, 16)
                with sp.Fori(0, NG // 2) as it:
                    for b in range(2):
                        g = it * 2 + b
                        sp.wait_ge(xn_ready, done(g))
                        rows = c.table[bass.ds(g * GN, GN), 0:P].rearrange("(j t) f -> t j f", t=P)
                        sp.dma_start(rows, xn[:, b]).then_inc(table_out[b], 16)
                for s in table_out:
                    sp.wait_ge(s, 16 * (NG // 2 + 1))
            sp.wait_ge(loaded, 16 * (len(loads) - 1))

        @block.gpsimd
        def _(pool):
            pool.sem_inc(xt_kept, 2)
            with pool.Fori(0, NG // 2) as it:
                for b in range(2):
                    g = it * 2 + b
                    pool.wait_ge(xt_ready, done(g))
                    nc.gpsimd.tensor_copy(c.xT[:, bass.ds(g * GN, GN)], xnT[:, b, :]).then_inc(xt_kept, 1)

        @block.vector
        def _(dve):
            dve.sem_inc(xn_ready, 2)
            ln_vector(nc, c, dve, ln)
            with dve.Fori(0, NG // 2) as it:
                for b in range(2):
                    g = it * 2 + b
                    dve.wait_ge(xt_psum, free(g))
                    if big:
                        dve.wait_ge(table_out[b], it * 16 + 16)
                    for j in range(GT):
                        t = g * GT + j
                        last = nc.vector.tensor_scalar(xn[:, b, j, :], c.x[:, t, :], c.mv[:, t, 0:1],
                                                       c.rstd[:, bass.ds(t, 1)], ALU.subtract, ALU.mult)
                    last.then_inc(xn_ready, 1)
            dve.wait_ge(log_ready, done(NG - 1))
            links = [0]

            def link(instruction):
                instruction.then_inc(soft, 1)
                links[0] += 1
                dve.wait_ge(soft, links[0])

            wide = [P, NT, experts]
            link(nc.vector.reduce_max(mx[:], scores, AX))
            link(nc.vector.tensor_tensor(scores, scores, mx.rearrange("p (t a) -> p t a", a=1).to_broadcast(wide),
                                         ALU.subtract))
            dve.wait_ge(exp_ready, 1)
            link(nc.vector.reduce_sum(tot[:], scores, AX))
            link(nc.vector.reciprocal(tot[:], tot[:]))
            link(nc.vector.tensor_tensor(scores, scores, tot.rearrange("p (t a) -> p t a", a=1).to_broadcast(wide),
                                         ALU.mult))
            if not big:
                other = scores.rearrange("p t (a e) -> p t a e", a=1).to_broadcast([P, NT, experts, experts])
                mine = scores.rearrange("p t (e a) -> p t e a", a=1).to_broadcast([P, NT, experts, experts])
                nc.vector.tensor_tensor(above[:], other, mine, ALU.is_gt)
                link(nc.vector.tensor_tensor(equal[:], other, mine, ALU.is_equal))
                flat = [x.rearrange("p t e f -> p t (e f)") for x in (above, equal)]
                link(nc.vector.tensor_tensor(flat[1], flat[1], c.before[:].to_broadcast([P, NT, experts ** 2]), ALU.mult))
                link(nc.vector.tensor_tensor(flat[0], flat[0], flat[1], ALU.add))
                link(nc.vector.reduce_sum(rank[:], above[:], AX))
                nc.vector.scalar_tensor_tensor(c.gates[:, :, 0:experts], rank[:], float(top), scores, ALU.is_lt, ALU.mult)
            else:
                for t in range(NT):
                    last = nc.vector.max(top8[:, t, :], scores[:, t, :])
                link(last)
                for t in range(NT):
                    last = nc.vector.match_replace(rest[:, t, :], top8[:, t, :], scores[:, t, :], -1.0)
                link(last)
                link(nc.vector.reduce_sum(tot[:], top8[:], AX))
                link(nc.vector.reciprocal(tot[:], tot[:]))
                link(nc.vector.tensor_scalar(rest[:], rest[:], 0.0, None, ALU.is_lt))
                nc.vector.tensor_copy(c.chosen.rearrange("p t h e -> p h t e"), rest.rearrange("p (h t) e -> p h t e", h=2))
                link(nc.vector.tensor_tensor(scores, scores, rest[:], ALU.mult))
                nc.vector.tensor_tensor(c.gates[:], scores, tot.rearrange("p (t a) -> p t a", a=1).to_broadcast(wide),
                                        ALU.mult)

        @block.scalar
        def _(act):
            act.sem_inc(xt_ready, 2)
            act.sem_inc(log_ready, 2)
            ln_scalar(nc, c, act, ln)
            with act.Fori(0, NG // 2) as it:
                for b in range(2):
                    g = it * 2 + b
                    act.wait_ge(xt_psum, done(g))
                    act.wait_ge(log_psum, free(g))
                    act.wait_ge(xt_kept, free(g))
                    nc.scalar.activation(xnT[:, b, :], xt_bank[b], ACT.Identity).then_inc(xt_ready, 1)
                    act.wait_ge(log_psum, done(g))
                    nc.scalar.activation(logits[:, bass.ds(g * GT, GT), :],
                                         log_bank[b][:, 0:GT * E].rearrange("p (j e) -> p j e", j=GT),
                                         ACT.Identity).then_inc(log_ready, 1)
            act.wait_ge(soft, 2)
            nc.scalar.activation(scores, scores, ACT.Exp).then_inc(exp_ready, 1)
            if big:
                nc.scalar.activation(c.shared_gate[:], logits[:, :, experts], ACT.Sigmoid)

        @block.tensor
        def _(pe):
            pe.sem_inc(xt_psum, 2)
            pe.sem_inc(log_psum, 2)
            pe.wait_ge(gate_in, 16)
            with pe.Fori(0, NG // 2) as it:
                for b in range(2):
                    g = it * 2 + b
                    pe.wait_ge(xn_ready, done(g))
                    pe.wait_ge(xt_ready, free(g))
                    for j in range(GT):
                        last = nc.tensor.transpose(xt_bank[b][:, j * P:(j + 1) * P], xn[:, b, j, :], c.ident[:])
                    last.then_inc(xt_psum, 1)
                    pe.wait_ge(xt_ready, done(g))
                    pe.wait_ge(log_ready, free(g))
                    for j in range(GT):
                        last = nc.tensor.matmul(log_bank[b][:, j * E:(j + 1) * E], xnT[:, b, j * P:(j + 1) * P], gate,
                                                start=True, stop=True)
                    last.then_inc(log_psum, 1)


def gated_mlp(nc, c, layer, w):
    first = layer == 0
    pre = f"g{layer}"
    (xt_ready, up_psum, silu_ready, h_ready, hw_ready, ht_psum, ht_ready, y_psum, x_ready, stats_ready, mv_ready,
     x_stored) = semaphores(nc, c, pre, "xt up silu h hw htp ht y x bn mv xst")
    wide = 512 if first else 256
    chunks = 5 if first else 2
    LAG = dict(UP=0, HT=1, Y=2, X=3)
    FIRST, U, LOOPS, LAST = 4, 2, 14, NT + LAG["X"]
    up_bank = [[c.bank[0], c.bank[1]], [c.bank[2], c.bank[3]]]
    shared_bank, ht_bank, hs_bank, y_bank = (c.bank[n] for n in (4, 5, 6, 7))
    routed = slice(0, 512)
    with ExitStack() as own, nc.Block() as block:
        xt, act_g, h, hT, xs, stats, mvs = scratch(nc, own, pre, dict(
            xt=([P, 2, P], F32), g=([P, 2, 640], F32), h=([P, 2, 640], F32), hT=([P, 2, 5, P], F32),
            xs=([P, 2, P], F32), stats=([P, 2, 6], F32), mvs=([P, 2, 2], F32)))

        def Tile(i, r, lag):
            return Item(i - lag, r, U)

        @block.tensor
        def _(pe):
            for s in (up_psum, ht_psum, y_psum):
                pe.sem_inc(s, 2)

            def step(i, r):
                up, ht, y = (Tile(i, r, LAG[k]) for k in ("UP", "HT", "Y"))
                if up.live:
                    pe.wait_ge(xt_ready, done(up.t))
                    pe.wait_ge(h_ready, up.items(1, 2) if first else free(up.t))
                    if first:
                        nc.tensor.matmul(up_bank[up.b][0], xt[:, up.b, :], w["wg"][:], start=True, stop=True)
                        nc.tensor.matmul(up_bank[up.b][1], xt[:, up.b, :], w["wu"][:], start=True, stop=True)
                        nc.tensor.matmul(shared_bank[:, 0:P], xt[:, up.b, :], w["ws"][:], start=True,
                                         stop=True).then_inc(up_psum, 1)
                    else:
                        nc.tensor.matmul(up_bank[up.b][0], xt[:, up.b, :], w["sgu"][:], start=True,
                                         stop=True).then_inc(up_psum, 1)
                if ht.live:
                    pe.wait_ge(hw_ready, done(ht.t))
                    pe.wait_ge(ht_ready, ht.items(1, 2))
                    for k in range(4 if first else 2):
                        last = nc.tensor.transpose(ht_bank[:, k * P:(k + 1) * P], h[:, ht.b, k * P:(k + 1) * P], c.ident[:])
                    if first:
                        last = nc.tensor.transpose(hs_bank[0:64, 0:P], h[:, ht.b, 512:576], c.ident[:])
                    last.then_inc(ht_psum, 1)
                if y.live:
                    pe.wait_ge(ht_ready, done(y.t))
                    pe.wait_ge(x_ready, y.items(1, 2))
                    for k in range(chunks):
                        rows = slice(0, 64 if k == 4 else P)
                        last = nc.tensor.matmul(y_bank[:, 0:P], hT[rows, y.b, k, :], w["wd"][rows, k, :],
                                                start=k == 0, stop=k == chunks - 1)
                    last.then_inc(y_psum, 1)

            run_steps(pe, step, FIRST, U, LOOPS, LAST)

        @block.scalar
        def _(act):
            act.sem_inc(silu_ready, 2)
            act.sem_inc(ht_ready, 2)

            def step(i, r):
                up, ht = (Tile(i, r, LAG[k]) for k in ("UP", "HT"))
                if ht.live:
                    act.wait_ge(ht_psum, done(ht.t))
                    act.wait_ge(y_psum, free(ht.t))
                    n = 4 if first else 2
                    last = nc.scalar.activation(hT[:, ht.b, 0:n, :].rearrange("p k t -> p (k t)"), ht_bank[:, 0:n * P],
                                                ACT.Identity)
                    if first:
                        last = nc.scalar.activation(hT[0:64, ht.b, 4, :], hs_bank[0:64, 0:P], ACT.Identity)
                    last.then_inc(ht_ready, 1)
                if up.live:
                    act.wait_ge(up_psum, done(up.t))
                    act.wait_ge(h_ready, free(up.t))
                    last = nc.scalar.activation(act_g[:, up.b, 0:wide], up_bank[up.b][0][:, 0:wide], ACT.Silu)
                    if first:
                        last = nc.scalar.activation(act_g[:, up.b, 512:576], shared_bank[:, 0:64], ACT.Silu)
                    last.then_inc(silu_ready, 1)

            run_steps(act, step, FIRST, U, LOOPS, LAST)

        @block.vector
        def _(dve):
            for s in (h_ready, x_ready):
                dve.sem_inc(s, 2)

            def step(i, r):
                up, xx = (Tile(i, r, LAG[k]) for k in ("UP", "X"))
                if xx.live:
                    dve.wait_ge(y_psum, done(xx.t))
                    dve.wait_ge(x_stored, free(xx.t))
                    if first:
                        nc.vector.tensor_tensor(xs[:, xx.b, :], c.x[:, xx.t, :], y_bank[:, 0:P], ALU.add).then_inc(x_ready, 1)
                    else:
                        nc.vector.scalar_tensor_tensor(xs[:, xx.b, :], y_bank[:, 0:P], c.shared_gate[:, bass.ds(xx.t, 1)],
                                                       c.x[:, xx.t, :], ALU.mult, ALU.add).then_inc(x_ready, 1)
                    if first:
                        dve.wait_ge(x_ready, done(xx.t))
                        nc.vector.bn_stats(stats[:, xx.b, :], xs[:, xx.b, :]).then_inc(stats_ready, 1)
                        dve.wait_ge(stats_ready, xx.t + 1)
                if up.live:
                    dve.wait_ge(silu_ready, done(up.t))
                    dve.wait_ge(ht_psum, free(up.t))
                    if first:
                        dve.wait_ge(hw_ready, free(up.t))
                        nc.vector.tensor_tensor(h[:, up.b, routed], act_g[:, up.b, routed], up_bank[up.b][1], ALU.mult)
                        nc.vector.tensor_tensor(h[:, up.b, 512:576], act_g[:, up.b, 512:576], shared_bank[:, 64:128],
                                                ALU.mult).then_inc(h_ready, 1)
                    else:
                        nc.vector.tensor_tensor(h[:, up.b, 0:256], act_g[:, up.b, 0:256], up_bank[up.b][0][:, 256:512],
                                                ALU.mult).then_inc(h_ready, 1)
                if xx.live and first:
                    nc.vector.bn_aggr(mvs[:, xx.b, :], stats[:, xx.b, :]).then_inc(mv_ready, 1)

            run_steps(dve, step, FIRST, U, LOOPS, LAST)

        @block.gpsimd
        def _(pool):
            for s in (xt_ready, hw_ready, x_stored):
                pool.sem_inc(s, 2)

            def stage(a):
                if a.live:
                    pool.wait_ge(up_psum, free(a.t))
                    nc.gpsimd.tensor_copy(xt[:, a.b, :], c.xT[:, bass.ds(a.t * P, P)]).then_inc(xt_ready, 1)

            def step(i, r):
                nxt, up, xx = (Tile(i, r, k) for k in (-1, LAG["UP"], LAG["X"]))
                if i == 0 and isinstance(r, int):
                    stage(up)
                stage(nxt)
                if up.live:
                    pool.wait_ge(h_ready, done(up.t))
                    if first:
                        gates = c.gates[:, up.t, 0:8].rearrange("p (e a) -> p e a", a=1).to_broadcast([P, 8, 64])
                        cols = h[:, up.b, routed].rearrange("p (e f) -> p e f", e=8)
                        nc.gpsimd.tensor_tensor(cols, cols, gates, ALU.mult).then_inc(hw_ready, 1)
                    else:
                        pool.sem_inc(hw_ready, 1)
                if xx.live:
                    if first:
                        pool.wait_ge(mv_ready, xx.t + 1)
                        nc.gpsimd.tensor_copy(c.mv[:, xx.t, :], mvs[:, xx.b, :])
                    else:
                        pool.wait_ge(x_ready, done(xx.t))
                    nc.gpsimd.tensor_copy(c.x[:, xx.t, :], xs[:, xx.b, :]).then_inc(x_stored, 1)

            run_steps(pool, step, FIRST, U, LOOPS - 1, LAST)


def routed_gelu(nc, c, w):
    EX, CH = 8, 4
    (h_psum, gelu_ready, y_psum, yb_ready, acc_ready, stats_ready, mv_ready, x_stored) = semaphores(
        nc, c, "e1", "h gelu y yb acc bn mv xst")
    h_bank, y_bank = [c.bank[n] for n in range(4)], [c.bank[n] for n in (4, 5)]
    LAST = NG * EX + 1

    def steps(engine, step):
        run_steps(engine, step, EX, EX, NG - 1, LAST)

    def ItemOf(i, r, lag):
        return Item(i - lag, r, EX, NG * EX)

    with ExitStack() as own, nc.Block() as block:
        hT, yb, acc, stats, mvs = scratch(nc, own, "e1", dict(
            hT=([P, 2, CH, GN], F32), yb=([P, GT, P], F32), acc=([P, 2, GT, P], F32),
            stats=([P, GT, 6], F32), mvs=([P, GT, 2], F32)))

        @block.tensor
        def _(pe):
            pe.sem_inc(h_psum, CH)
            pe.sem_inc(y_psum, 2)

            def step(i, r):
                up, dn = ItemOf(i, r, 0), ItemOf(i, r, 1)
                if up.live:
                    e, g = up.n % EX, r + up.n // EX
                    for k in range(CH):
                        pe.wait_ge(gelu_ready, free(up.items(CH, k)))
                        nc.tensor.matmul(h_bank[k], w["w1"][:, e, k * P:(k + 1) * P], c.xT[:, bass.ds(g * GN, GN)],
                                         start=True, stop=True).then_inc(h_psum, 1)
                if dn.live:
                    e = dn.n % EX
                    pe.wait_ge(yb_ready, free(dn.t))
                    pe.wait_ge(gelu_ready, done(dn.items(CH, CH - 1), CH))
                    for j in range(GT):
                        for k in range(CH):
                            last = nc.tensor.matmul(y_bank[dn.b][:, j * P:(j + 1) * P],
                                                    hT[:, dn.b, k, j * P:(j + 1) * P], w["w2"][:, e, k, :],
                                                    start=k == 0, stop=k == CH - 1)
                    last.then_inc(y_psum, 1)

            steps(pe, step)

        @block.scalar
        def _(act):
            act.sem_inc(gelu_ready, CH)

            def step(i, r):
                up = ItemOf(i, r, 0)
                if up.live:
                    for k in range(CH):
                        act.wait_ge(h_psum, done(up.items(CH, k), CH))
                        if k == 0:
                            act.wait_ge(y_psum, free(up.t))
                        nc.scalar.activation(hT[:, up.b, k, :], h_bank[k], ACT.Gelu,
                                             bias=w["b1"][:, up.n % EX, k:k + 1]).then_inc(gelu_ready, 1)

            steps(act, step)

        @block.vector
        def _(dve):
            dve.sem_inc(yb_ready, 2)

            def aggregate():
                for j in range(GT):
                    last = nc.vector.bn_aggr(mvs[:, j, :], stats[:, j, :])
                last.then_inc(mv_ready, 1)

            def step(i, r):
                dn = ItemOf(i, r, 1)
                if not dn.live:
                    return
                e, first = dn.n % EX, dn.n % EX == 0
                g = r + dn.n // EX
                dve.wait_ge(y_psum, done(dn.t))
                if dn.n or not isinstance(r, int):
                    dve.wait_ge(acc_ready, dn.t)
                if first and dn.n:
                    dve.wait_ge(stats_ready, g)
                nc.vector.tensor_tensor(yb[:], y_bank[dn.b].rearrange("p (j f) -> p j f", j=GT),
                                        c.b2[:, e:e + 1, :].to_broadcast([P, GT, P]), ALU.add).then_inc(yb_ready, 1)
                if first and dn.n:
                    aggregate()
                if e == EX - 1:
                    dve.wait_ge(x_stored, free(g))
                dve.wait_ge(yb_ready, done(dn.t))
                for j in range(GT):
                    t = g * GT + j
                    before = c.x[:, t, :] if first else acc[:, 0, j, :]
                    last = nc.vector.scalar_tensor_tensor(acc[:, 1 if e == EX - 1 else 0, j, :], yb[:, j, :],
                                                          c.gates[:, t, e:e + 1], before, ALU.mult, ALU.add)
                last.then_inc(acc_ready, 1)
                if e == EX - 1:
                    dve.wait_ge(acc_ready, dn.t + 1)
                    for j in range(GT):
                        last = nc.vector.bn_stats(stats[:, j, :], acc[:, 1, j, :])
                    last.then_inc(stats_ready, 1)

            steps(dve, step)
            dve.wait_ge(stats_ready, NG)
            aggregate()

        @block.gpsimd
        def _(pool):
            pool.sem_inc(x_stored, 1)
            with pool.Fori(0, NG) as g:
                pool.wait_ge(mv_ready, g + 1)
                nc.gpsimd.tensor_copy(c.mv[:, bass.ds(g * GT, GT), :], mvs[:])
                nc.gpsimd.tensor_copy(c.x[:, bass.ds(g * GT, GT), :], acc[:, 1]).then_inc(x_stored, 1)


def ffn0(nc, c, d):
    with ExitStack() as own:
        gate, wg, wu, ws, wd = scratch(nc, own, "w0", dict(
            gate=([P, 8], F32), wg=([P, 512], F32), wu=([P, 512], F32), ws=([P, P], F32), wd=([P, 5, P], F32)))
        w = dict(wg=wg, wu=wu, ws=ws, wd=wd)
        route(nc, c, 0, 8, 2, [(gate[:], d["f0_gate"]), (wg[:], d["f0_wg"]), (wu[:], d["f0_wu"]), (ws[:], d["f0_ws"]),
                               (wd[:, 0:4, :], d["f0_wd"]), (wd[0:64, 4, :], d["f0_sd"])])
        gated_mlp(nc, c, 0, w)


def ffn1(nc, c, d):
    with ExitStack() as own:
        gate, w1, b1, w2 = scratch(nc, own, "w1", dict(
            gate=([P, 8], F32), w1=([P, 8, 512], F32), b1=([P, 8, 4], F32), w2=([P, 8, 4, P], F32)))
        c.b2, = scratch(nc, own, "w1", dict(b2=([P, 8, P], F32)))
        route(nc, c, 1, 8, 1, [(gate[:], d["f1_gate"]), (w1[:], d["f1_w1"]), (b1[:], d["f1_b1"]), (w2[:], d["f1_w2"]),
                               (c.b2[:], d["f1_b2"].partition_broadcast(P))])
        routed_gelu(nc, c, dict(w1=w1, b1=b1, w2=w2))


def ffn2(nc, c, d):
    EX, TILES, LIMIT, ALPHA = 8, 2, 7.0, 1.702
    NTOK = TILES * P
    ln = semaphores(nc, c, "e2", "var root chain")
    (loaded, xn_ready, xt_psum, xt_ready, h_psum, gate_ready, up_clipped, up_ready, sig_ready, glu_ready,
     inter_ready, y_psum, yb_ready, acc_ready, cw_links, stats_ready) = semaphores(
        nc, c, "e2", "load xn xtp xt h gate upc up sig glu inter y yb acc cw bn")
    h_bank, y_bank, xt_bank = [c.bank[0], c.bank[1]], [c.bank[2], c.bank[3]], c.bank[4]
    with ExitStack() as own, nc.Block() as block:
        w_gu, w_down, b_gu, b_down, numbers, idx, weights = scratch(nc, own, "e2", dict(
            wgu=([P, EX, 2, P], F32), wdown=([P, EX, P], F32), bgu=([P, EX, 2], F32), bdown=([P, EX, P], F32),
            numbers=([P, EX], F32), idx=([P, TILES, 2], I32), weights=([P, TILES, EX], F32)))
        xn, xT, idx_f, picked, cw, gate, up, sig, glu, inter, yb, stats = scratch(nc, own, "e2", dict(
            xn=([P, TILES, P], F32), xT=([P, NTOK], F32), idxf=([P, TILES, 2], F32), picked=([P, TILES, 2, EX], F32),
            cw=([P, TILES, EX], F32), gate=([P, 2, NTOK], F32), up=([P, 2, NTOK], F32), sig=([P, 2, NTOK], F32),
            glu=([P, 2, NTOK], F32), inter=([P, 2, NTOK], F32), yb=([P, 2, TILES, P], F32), stats=([P, TILES, 6], F32)))
        loads = [(idx[:], d["f2_idx"]), (weights[:], d["f2_weights"]), (numbers[:], d["numbers"].partition_broadcast(P)),
                 (b_gu[:], d["f2_bgu"]), (w_gu[:], d["f2_wgu"]), (w_down[:], d["f2_down"]),
                 (b_down[:], d["f2_bdown"].partition_broadcast(P))]

        @block.sync
        def _(sp):
            for dst, src in loads:
                sp.dma_start(dst, src).then_inc(loaded, 16)

        @block.tensor
        def _(pe):
            pe.wait_ge(xn_ready, 1)
            for t in range(TILES):
                last = nc.tensor.transpose(xt_bank[:, t * P:(t + 1) * P], xn[:, t, :], c.ident[:])
            last.then_inc(xt_psum, 1)
            pe.wait_ge(xt_ready, 1)
            pe.wait_ge(loaded, 16 * len(loads))
            for i in range(EX + 1):
                if i < EX:
                    if i >= 2:
                        pe.wait_ge(gate_ready, i - 1)
                        pe.wait_ge(up_clipped, i - 1)
                    for k in range(2):
                        last = nc.tensor.matmul(h_bank[i % 2][:, k * NTOK:(k + 1) * NTOK], w_gu[:, i, k, :], xT[:],
                                                start=True, stop=True)
                    last.then_inc(h_psum, 1)
                if i >= 1:
                    e = i - 1
                    pe.wait_ge(inter_ready, e + 1)
                    if e >= 2:
                        pe.wait_ge(yb_ready, e - 1)
                    for t in range(TILES):
                        last = nc.tensor.matmul(y_bank[e % 2][:, t * P:(t + 1) * P],
                                                inter[:, e % 2, t * P:(t + 1) * P], w_down[:, e, :],
                                                start=True, stop=True)
                    last.then_inc(y_psum, 1)

        @block.scalar
        def _(act):
            ln_scalar(nc, c, act, ln)
            act.wait_ge(xt_psum, 1)
            nc.scalar.activation(xT[:], xt_bank[:, 0:NTOK], ACT.Identity).then_inc(xt_ready, 1)
            for e in range(EX):
                act.wait_ge(gate_ready, e + 1)
                if e >= 2:
                    act.wait_ge(glu_ready, e - 1)
                nc.scalar.activation(sig[:, e % 2, :], gate[:, e % 2, :], ACT.Sigmoid, scale=ALPHA).then_inc(sig_ready, 1)

        @block.vector
        def _(dve):
            ln_vector(nc, c, dve, ln)
            for t in range(TILES):
                last = nc.vector.tensor_scalar(xn[:, t, :], c.x[:, t, :], c.mv[:, t, 0:1], c.rstd[:, t:t + 1],
                                               ALU.subtract, ALU.mult)
            last.then_inc(xn_ready, 1)
            dve.wait_ge(loaded, 16 * len(loads))
            nc.vector.tensor_copy(idx_f[:], idx[:]).then_inc(cw_links, 1)
            dve.wait_ge(cw_links, 1)
            for k in range(2):
                last = nc.vector.tensor_tensor(picked[:, :, k, :], idx_f[:, :, k:k + 1].to_broadcast([P, TILES, EX]),
                                               numbers.rearrange("p (t e) -> p t e", t=1).to_broadcast([P, TILES, EX]),
                                               ALU.is_equal)
            last.then_inc(cw_links, 1)
            dve.wait_ge(cw_links, 2)
            nc.vector.tensor_tensor(cw[:], picked[:, :, 0, :], picked[:, :, 1, :], ALU.add).then_inc(cw_links, 1)
            dve.wait_ge(cw_links, 3)
            nc.vector.tensor_tensor(cw[:], cw[:], weights[:], ALU.mult).then_inc(cw_links, 1)
            dve.wait_ge(cw_links, 4)
            for i in range(EX + 2):
                b = i % 2
                if i < EX:
                    dve.wait_ge(h_psum, i + 1)
                    nc.vector.tensor_scalar(gate[:, b, :], h_bank[b][:, 0:NTOK], b_gu[:, i, 0:1], LIMIT,
                                            ALU.add, ALU.min).then_inc(gate_ready, 1)
                    nc.vector.tensor_scalar(up[:, b, :], h_bank[b][:, NTOK:2 * NTOK], b_gu[:, i, 1:2], LIMIT,
                                            ALU.add, ALU.min).then_inc(up_clipped, 1)
                e = i - 1
                if 0 <= e < EX:
                    dve.wait_ge(sig_ready, e + 1)
                    nc.vector.tensor_tensor(glu[:, e % 2, :], gate[:, e % 2, :], sig[:, e % 2, :],
                                            ALU.mult).then_inc(glu_ready, 1)
                if i < EX:
                    dve.wait_ge(up_clipped, i + 1)
                    nc.vector.tensor_scalar(up[:, b, :], up[:, b, :], -LIMIT, 1.0, ALU.max, ALU.add).then_inc(up_ready, 1)
                if 0 <= e < EX:
                    dve.wait_ge(glu_ready, e + 1)
                    dve.wait_ge(up_ready, e + 1)
                    if e >= 2:
                        dve.wait_ge(y_psum, e - 1)
                    nc.vector.tensor_tensor(inter[:, e % 2, :], glu[:, e % 2, :], up[:, e % 2, :],
                                            ALU.mult).then_inc(inter_ready, 1)
                e = i - 2
                if e >= 0:
                    dve.wait_ge(y_psum, e + 1)
                    nc.vector.tensor_tensor(yb[:, e % 2], y_bank[e % 2][:, 0:NTOK].rearrange("p (t f) -> p t f", t=TILES),
                                            b_down[:, e:e + 1, :].to_broadcast([P, TILES, P]), ALU.add).then_inc(yb_ready, 1)
                    dve.wait_ge(yb_ready, e + 1)
                    if e >= 1:
                        dve.wait_ge(acc_ready, e)
                    for t in range(TILES):
                        last = nc.vector.scalar_tensor_tensor(c.x[:, t, :], yb[:, e % 2, t, :], cw[:, t, e:e + 1],
                                                              c.x[:, t, :], ALU.mult, ALU.add)
                    last.then_inc(acc_ready, 1)
            dve.wait_ge(acc_ready, EX)
            for t in range(TILES):
                last = nc.vector.bn_stats(stats[:, t, :], c.x[:, t, :])
            last.then_inc(stats_ready, 1)
            dve.wait_ge(stats_ready, 1)
            for t in range(TILES):
                nc.vector.bn_aggr(c.mv[:, t, :], stats[:, t, :])


def dispatch(nc, c, d, weights):
    HALF = T // 2
    ROUNDS = CAPACITY // 8
    (loaded, cleared, sel_psum, searched, links, moved, twice, tok_psum, stored,
     weights_in) = semaphores(
        nc, c, "d3", "load clear sp search link moved twice tp stored win")
    with ExitStack() as own, nc.Block() as block:
        order, value = c.ctxT[:, 0:HALF], c.ctxT[:, HALF:T]
        slots, region, zeros, top, some, merged, best, empty, tok = scratch(nc, own, "d3", dict(
            slots=([64, CAPACITY], F32), region=([P, 1], F32),
            zeros=([P, ZERO_COLS], F32), top=([P, CAPACITY], F32), some=([64, CAPACITY], F32),
            merged=([64, 2, CAPACITY], F32), best=([64, CAPACITY], F32), empty=([64, CAPACITY], F32),
            tok=([64, 2, CAPACITY], F32)))
        loads = [(order, d["order"].partition_broadcast(P)), (slots[:], d["slots"].partition_broadcast(64)),
                 (region[:], d["region"])]
        flat = c.sum_rows.rearrange("(p n) f -> p (n f)", p=P)
        clears = [(flat[:, k:k + ZERO_COLS], zeros[:]) for k in range(0, flat.shape[1], ZERO_COLS)]
        clears.append((c.table[T:T + CAPACITY, :], zeros[0:CAPACITY, 0:P + 64]))

        @block.sync
        def _(sp):
            for dst, src in loads:
                sp.dma_start(dst, src).then_inc(loaded, 16)
            sp.dma_start(c.table[0:T, P:P + 64].rearrange("(j t) e -> t j e", t=P), c.gates[:]).then_inc(stored, 16)
            sp.wait_ge(cleared, 1)
            for dst, src in clears:
                sp.dma_start(dst, src).then_inc(stored, 16)
            for dst, src in weights:
                sp.dma_start(dst, src).then_inc(weights_in, 16)
            sp.wait_ge(searched, 2 * ROUNDS - 1)
            sp.dma_start(merged[:, 1, :], top[64:P, :]).then_inc(moved, 16)
            sp.wait_ge(stored, 16 * (len(clears) + 1))
            sp.wait_ge(weights_in, 16 * len(weights))

        @block.gpsimd
        def _(pool):
            nc.gpsimd.memset(zeros[:], 0.0).then_inc(cleared, 1)

        @block.tensor
        def _(pe):
            for k in range(4):
                for j in range(4):
                    last = nc.tensor.transpose(c.bank[k][:, j * P:(j + 1) * P],
                                               c.chosen[:, 4 * k + j].rearrange("p h e -> p (h e)"), c.ident[:])
                last.then_inc(sel_psum, 1)
            pe.wait_ge(twice, 1)
            nc.tensor.transpose(c.bank[4][:, 0:64], tok.rearrange("e k s -> e (k s)"), c.ident[0:64, 0:64]).then_inc(tok_psum, 1)

        @block.vector
        def _(dve):
            count = [0]

            def link(instruction):
                instruction.then_inc(links, 1)
                count[0] += 1
                dve.wait_ge(links, count[0])

            dve.wait_ge(loaded, 16 * len(loads))
            for k in range(4):
                dve.wait_ge(sel_psum, k + 1)
                part = slice(k * GN, (k + 1) * GN)
                last = nc.vector.tensor_tensor(value[:, part], c.bank[k], order[:, part], ALU.mult)
            link(last)
            for k in range(ROUNDS):
                found = top[:, 8 * k:8 * k + 8]
                nc.vector.max(found, value).then_inc(searched, 1)
                dve.wait_ge(searched, 2 * k + 1)
                if k < ROUNDS - 1:
                    nc.vector.match_replace(value, found, value, 0.0).then_inc(searched, 1)
                    dve.wait_ge(searched, 2 * k + 2)
            link(nc.vector.tensor_scalar(some[:], top[0:64, :], 0.0, float(HALF), ALU.is_gt, ALU.mult))
            link(nc.vector.tensor_tensor(merged[:, 0, :], some[:], top[0:64, :], ALU.add))
            dve.wait_ge(moved, 16)
            both = merged.rearrange("e h s -> e (h s)")
            for k in range(ROUNDS):
                link(nc.vector.max(best[:, 8 * k:8 * k + 8], both))
                if k < ROUNDS - 1:
                    link(nc.vector.match_replace(both, best[:, 8 * k:8 * k + 8], both, 0.0))
            link(nc.vector.scalar_tensor_tensor(empty[:], best[:], 0.0, slots[:], ALU.is_equal, ALU.mult))
            link(nc.vector.tensor_scalar(best[:], best[:], -1.0, float(T), ALU.mult, ALU.add))
            for k in range(2):
                nc.vector.tensor_tensor(tok[:, k, :], best[:], empty[:], ALU.add).then_inc(links, 1)
            dve.wait_ge(links, count[0] + 2)
            dve.sem_inc(twice, 1)
            dve.wait_ge(tok_psum, 1)
            for k in range(2):
                half = slice(k * 64, k * 64 + 64)
                mine = c.bank[4][half, 0:64].rearrange("p (n k) -> p n k", k=2)[:, :, k]
                nc.vector.tensor_copy(c.idx[half, :], mine)
                nc.vector.tensor_scalar(c.sum_idx[half, :], mine, region[half, 0:1], None, ALU.add)


def experts(nc, c, w):
    PAIRS, XB, AHEAD, I = 32, 4, 3, 64
    (xt_psum, xt_ready, up_psum, silu_ready, h_ready, ht_psum, ht_ready, y_psum, ys_ready, scattered,
     cleared) = semaphores(nc, c, "x3", "xtp xt up silu h htp ht y ys scat clear")
    gathered = semaphores(nc, c, "x3", "in0 in1 in2 in3")
    xt_bank, up_bank, ht_bank, y_bank = ([c.bank[n], c.bank[n + 1]] for n in (0, 2, 4, 6))
    halves = [slice(0, 64), slice(64, P)]
    FIRST, U, LOOPS, LAST = 8, 4, 6, PAIRS + 3

    with ExitStack() as own, nc.Block() as block:
        rows, xT, silu, h, hT, ys = scratch(nc, own, "x3", dict(
            rows=([P, XB, P + 64], F32), xT=([P, 2, P], F32),
            silu=([P, 2, 2, I], F32), h=([P, 2, P], F32), hT=([P, 2, P], F32), ys=([P, 2, P], F32)))

        def Pair(i, r, lag=0):
            return Item(i - lag, r, U, PAIRS)

        @block.gpsimd
        def _(pool):
            nc.gpsimd.memset(h[:], 0.0).then_inc(cleared, 1)
            for n in range(PAIRS + AHEAD):
                if n < PAIRS:
                    if n >= XB:
                        pool.wait_ge(ys_ready, free(n))
                    nc.gpsimd.indirect_dma_start(rows[:, n % XB, :], None, c.table[:, :],
                                                 bass.IndirectOffsetOnAxis(ap=c.idx[:, n:n + 1], axis=0)
                                                 ).then_inc(gathered[n % XB], 16)
                y = n - AHEAD
                if y >= 0:
                    pool.wait_ge(ys_ready, done(y, XB))
                    if y >= 1:
                        pool.wait_ge(scattered, 16 * y)
                    nc.gpsimd.indirect_dma_start(c.sum_rows[:, :],
                                                 bass.IndirectOffsetOnAxis(ap=c.sum_idx[:, y:y + 1], axis=0),
                                                 ys[:, y % 2, :], None, compute_op=ALU.add).then_inc(scattered, 16)
            pool.wait_ge(scattered, 16 * PAIRS)

        @block.tensor
        def _(pe):
            for s in (xt_psum, up_psum, ht_psum, y_psum):
                pe.sem_inc(s, 2)

            def step(i, r):
                x, up, ht, y = (Pair(i, r, lag) for lag in range(4))
                if x.live:
                    pe.wait_ge(gathered[x.n % XB], r * 16 + (16 * (x.n // XB) + 16))
                    pe.wait_ge(xt_ready, free(x.t))
                    nc.tensor.transpose(xt_bank[x.b][:, 0:P], rows[:, x.n % XB, 0:P], c.ident[:]).then_inc(xt_psum, 1)
                if up.live:
                    pe.wait_ge(xt_ready, done(up.t))
                    pe.wait_ge(h_ready, free(up.t))
                    nc.tensor.matmul(up_bank[up.b][:, 0:2 * P], xT[:, up.b, :],
                                     w["up"][:, bass.ds(up.items(2), 2), :].rearrange("d a f -> d (a f)"),
                                     start=True, stop=True).then_inc(up_psum, 1)
                if ht.live:
                    pe.wait_ge(h_ready, done(ht.t))
                    pe.wait_ge(ht_ready, free(ht.t))
                    nc.tensor.transpose(ht_bank[ht.b][:, 0:P], h[:, ht.b, :], c.ident[:]).then_inc(ht_psum, 1)
                if y.live:
                    pe.wait_ge(ht_ready, done(y.t))
                    pe.wait_ge(ys_ready, y.items(1, 3))
                    nc.tensor.matmul(y_bank[y.b][:, 0:P], hT[:, y.b, :],
                                     w["down"][:, bass.ds(y.t, 1), :].rearrange("d a f -> d (a f)"),
                                     start=True, stop=True).then_inc(y_psum, 1)

            run_steps(pe, step, FIRST, U, LOOPS, LAST)

        @block.scalar
        def _(act):
            for s in (xt_ready, silu_ready, ht_ready):
                act.sem_inc(s, 2)

            def step(i, r):
                x, up, ht = (Pair(i, r, lag) for lag in range(3))
                if x.live:
                    act.wait_ge(xt_psum, done(x.t))
                    act.wait_ge(up_psum, free(x.t))
                    nc.scalar.activation(xT[:, x.b, :], xt_bank[x.b][:, 0:P], ACT.Copy).then_inc(xt_ready, 1)
                if up.live:
                    act.wait_ge(up_psum, done(up.t))
                    act.wait_ge(h_ready, free(up.t))
                    nc.scalar.activation(silu[:, up.b], up_bank[up.b][:, 0:2 * P].rearrange("p (k f) -> p k f", k=2)[:, :, 0:I],
                                         ACT.Silu).then_inc(silu_ready, 1)
                if ht.live:
                    act.wait_ge(ht_psum, done(ht.t))
                    act.wait_ge(y_psum, free(ht.t))
                    nc.scalar.activation(hT[:, ht.b, :], ht_bank[ht.b][:, 0:P], ACT.Copy).then_inc(ht_ready, 1)

            run_steps(act, step, FIRST, U, LOOPS, LAST)

        @block.vector
        def _(dve):
            dve.sem_inc(h_ready, 2)
            dve.sem_inc(ys_ready, XB)

            def step(i, r):
                up, y = Pair(i, r, 1), Pair(i, r, 3)
                if up.live:
                    if up.n == 0 and isinstance(r, int):
                        dve.wait_ge(cleared, 1)
                    dve.wait_ge(silu_ready, done(up.t))
                    dve.wait_ge(ht_psum, free(up.t))
                    for k in range(2):
                        last = nc.vector.tensor_tensor(h[halves[k], up.b, k * I:(k + 1) * I], silu[halves[k], up.b, k, :],
                                                       up_bank[up.b][halves[k], k * P + I:(k + 1) * P], ALU.mult)
                    last.then_inc(h_ready, 1)
                if y.live:
                    dve.wait_ge(y_psum, done(y.t))
                    if y.n >= 2:
                        dve.wait_ge(scattered, y.items(16) - 16)
                    for k in range(2):
                        gate = rows[halves[k], y.n % XB, bass.ds(y.items(2, P + k), 1)]
                        last = nc.vector.tensor_scalar(ys[halves[k], y.b, :], y_bank[y.b][halves[k], 0:P], gate, None,
                                                       ALU.mult)
                    last.then_inc(ys_ready, 1)

            run_steps(dve, step, FIRST, U, LOOPS, LAST)


def ffn3(nc, c, d):
    with ExitStack() as own:
        gate, sgu, wd, chosen = scratch(nc, own, "w3", dict(
            gate=([P, 65], F32), sgu=([P, 512], F32), wd=([P, 2, P], F32), chosen=([P, NT // 2, 2, 64], F32)))
        c.chosen = chosen
        c.idx, c.sum_idx = scratch(nc, own, "w3", dict(idx=([P, 32], I32), sumidx=([P, 32], I32)))
        route(nc, c, 3, 64, 8, [(gate[:], d["f3_gate"]), (sgu[:], d["f3_sgu"]), (wd[:], d["f3_sdown"])])
        with ExitStack() as inner:
            up, down = scratch(nc, inner, "w3", dict(up=([P, 64, P], F32), down=([P, 32, P], F32)))
            dispatch(nc, c, d, [(up[:], d["f3_up"]), (down[:], d["f3_down"])])
            experts(nc, c, dict(up=up, down=down))
        gated_mlp(nc, c, 3, dict(sgu=sgu, wd=wd))


def finish(nc, c, out):
    PARTS = 4
    loaded, added, stored = (semaphores(nc, c, "end", " ".join(f"{k}{n}" for n in range(PARTS)))
                             for k in ("load", "add", "store"))
    with ExitStack() as own, nc.Block() as block:
        sums, = scratch(nc, own, "end", dict(sums=([P, 2, NT, P], F32)))

        def part(n):
            return slice(n * NT // PARTS, (n + 1) * NT // PARTS)

        @block.sync
        def _(sp):
            for n in range(PARTS):
                for k in range(2):
                    sp.dma_start(sums[:, k, part(n), :],
                                 c.sums[k][0:T, :].rearrange("(j t) f -> t j f", t=P)[:, part(n), :]).then_inc(loaded[n], 16)
            for n in range(PARTS):
                sp.wait_ge(added[n], 2)
                sp.dma_start(out.rearrange("b t f -> t b f")[:, part(n), :], c.x[:, part(n), :]).then_inc(stored[n], 16)
            for n in range(PARTS):
                sp.wait_ge(stored[n], 16)

        @block.vector
        def _(dve):
            for n in range(PARTS):
                dve.wait_ge(loaded[n], 32)
                for k in range(2):
                    if k:
                        dve.wait_ge(added[n], 1)
                    nc.vector.tensor_tensor(c.x[:, part(n), :], c.x[:, part(n), :], sums[:, k, part(n), :],
                                            ALU.add).then_inc(added[n], 1)


def setup(nc, c, d):
    loaded, made, cleared, stats, aggr, masks = semaphores(nc, c, "su", "load made clear stats aggr mask")
    loads = [(c.ident[:], d["ident"]), (c.wa[:], d["wa"]), (c.wrot[:], d["wrot"]), (c.bcol[:], d["bcol"]),
             (c.rope[:], d["rope"]), (c.ctxT[:], d["ctxT"]),
             (c.before[:], d["before"].partition_broadcast(P)),
             (c.brow[:], d["brow"].partition_broadcast(P)), (c.causal[:], d["causal"]), (c.umask[:], d["umask"])]
    xs = [semaphores(nc, c, "su", f"x{g}")[0] for g in range(4)]
    with nc.Block() as block:
        @block.sync
        def _(sp):
            for g in range(4):
                part = slice(g * NT // 4, (g + 1) * NT // 4)
                sp.dma_start(c.x[:, part, :], d["x"].rearrange("b t f -> t b f")[:, part, :]).then_inc(xs[g], 16)
            for dst, src in loads:
                sp.dma_start(dst, src).then_inc(loaded, 16)

        @block.vector
        def _(dve):
            dve.wait_ge(loaded, 16 * len(loads))
            nc.vector.tensor_copy(c.identb[:], c.ident[:]).then_inc(made, 1)
            for kind, src in enumerate((c.causal, c.umask)):
                for side in range(2):
                    nc.vector.tensor_scalar(c.mask[:, kind, side], src[:, side:side + 1, :].to_broadcast([P, 4, P]),
                                            NEG, None, ALU.mult).then_inc(masks, 1)
            for t in range(NT):
                if t % (NT // 4) == 0:
                    dve.wait_ge(xs[t // (NT // 4)], 16)
                nc.vector.bn_stats(c.stats0[:, t, :], c.x[:, t, :]).then_inc(stats, 1)
            for t in range(NT):
                dve.wait_ge(stats, t + 1)
                nc.vector.bn_aggr(c.mv[:, t, :], c.stats0[:, t, :])

        @block.gpsimd
        def _(pool):
            nc.gpsimd.memset(c.qs[:], 0.0)
            nc.gpsimd.memset(c.ks[:], 0.0).then_inc(cleared, 1)
            nc.gpsimd.memset(c.vx[:], 0.0).then_inc(cleared, 1)
            nc.gpsimd.memset(c.zeros[:], 0.0)
            pool.wait_ge(cleared, 2)
            nc.gpsimd.memset(c.ks[32:64], 1.0).then_inc(cleared, 1)
            pool.wait_ge(cleared, 3)
            for odd in range(2):
                nc.gpsimd.memset(c.vx.rearrange("p b (g o) e -> p b g o e", o=2)[
                    :, :, :, odd, 16 * odd + HD:16 * odd + 2 * HD], 1.0)


def build(nc, d, out, stages=range(8)):
    with ExitStack() as ctx:
        c = Core()
        c.ctx = ctx

        def sb(name, shape, dt=F32):
            return ctx.enter_context(nc.sbuf_tensor(name, shape, dt))

        c.psum = ctx.enter_context(nc.psum_tensor("psum", [P, 8, 512], F32))
        c.bank = [c.psum[:, n, :] for n in range(8)]
        c.x = sb("x_sb", [P, NT, P])
        c.ctxT = sb("ctx_T", [P, T])
        c.v = sb("v_sb", [P, NT, P])
        c.wa = sb("w_attn", [P, 4, 4, P])
        c.wrot = sb("w_rot", [P, 2, P])
        c.bcol = sb("b_cols", [P, 10])
        c.brow = sb("b_rows", [P, 8, P])
        c.rope = sb("rope_sb", [P, 2, P])
        c.ident = sb("ident_sb", [P, P])
        c.identb = sb("ident_bf", [P, P], BF16)
        c.causal = sb("causal_sb", [P, 2, P])
        c.umask = sb("umask_sb", [P, 2, P], U8)
        c.mask = sb("mask_sb", [P, 2, 2, 4, P], BF16)
        c.mv = sb("mean_var", [P, NT, 2])
        c.stats0 = sb("stats0", [P, NT, 6])
        c.stats = sb("stats", [P, 2, 6])
        c.mvs = sb("mean_var_new", [P, 2, 2])
        c.xs = sb("x_new", [P, 2, P])
        c.veps, c.root, c.rstd0, c.newt, c.rstd = (sb("ln_" + n, [P, NT]) for n in
                                                   ("veps", "root", "rstd0", "newt", "rstd"))
        c.gates = sb("gates", [P, NT, 64])
        c.before = sb("before_sb", [P, 1, 64])
        c.shared_gate = sb("shared_gate", [P, NT])
        c.xT = c.v.rearrange("p t f -> p (t f)")
        c.parts_dram = [nc.dram_tensor(n, [P, 3, T], BF16, kind="Internal").ap() for n in ("q_parts", "k_parts")]
        c.STACK_INCS = 16 * (2 * TERMS + 1)

        c.qs = sb("q_stack", [P, STACKS, H, 2 * P], BF16)
        c.ks = sb("k_stack", [P, STACKS, H, 2 * P], BF16)
        c.zeros = sb("zeros", [2, H, 2 * P], BF16)
        c.vx = sb("v_x", [P, 2, H, 32])
        c.table = nc.dram_tensor("table", [T + CAPACITY, P + 64], F32, kind="Internal").ap()
        c.sum_rows = nc.dram_tensor("sum_rows", [2 * (T + CAPACITY), P], F32, kind="Internal").ap()
        c.sums = [c.sum_rows[k * (T + CAPACITY):(k + 1) * (T + CAPACITY), :] for k in range(2)]
        for layer in range(4):
            with ExitStack() as sems:
                c.ctx = sems
                c.next_semaphore = FIRST_SEMAPHORE
                if layer == 0:
                    setup(nc, c, d)
                if 2 * layer in stages:
                    project(nc, c, layer)
                    attend(nc, c, layer)
                if 2 * layer + 1 in stages:
                    (ffn0, ffn1, ffn2, ffn3)[layer](nc, c, d)
                if layer == 3:
                    finish(nc, c, out)
                else:
                    zero_semaphores(nc, c)


def host_arrays(i):
    f = {}
    at = lambda n, k: np.asarray(i[f"L{n}_xattn_{k if n != 2 else k.lower()}"])
    f["x"] = np.asarray(i["x"])
    f["ctxT"] = np.ascontiguousarray(np.asarray(i["ctx_1024"]).reshape(T, P).T)
    f["wa"] = np.ascontiguousarray(np.stack([np.stack([at(n, k).T for k in ("Wq", "Wk", "Wv", "Wo")])
                                             for n in range(4)]).transpose(2, 0, 1, 3))
    swap = np.arange(P).reshape(H, 2, HD // 2)[:, ::-1].reshape(P)
    f["wrot"] = np.ascontiguousarray(np.stack([at(3, k).T[:, swap] for k in ("Wq", "Wk")], 1))
    f["bcol"] = np.ascontiguousarray(np.stack([at(n, k) for n in range(4) for k in ("bq", "bk")]
                                              + [at(3, k)[swap] for k in ("bq", "bk")], 1))
    f["brow"] = np.ascontiguousarray(np.stack([at(n, k) for n in range(4) for k in ("bv", "bo")]))
    angle = np.arange(P)[:, None] * (1.0 / 10000.0 ** (np.arange(0, HD, 2) / HD))[None, :]
    cos, sin = (np.tile(fn(angle), (1, 2 * H)).T for fn in (np.cos, np.sin))
    sign = np.where(np.arange(P) % HD < HD // 2, -1.0, 1.0)[:, None]
    f["rope"] = np.ascontiguousarray(np.stack([cos, sin * sign], 1).astype(np.float32))
    f["ident"] = np.eye(P, dtype=np.float32)
    later = (np.arange(P)[None, :] > np.arange(P)[:, None]).astype(np.float32)
    f["causal"] = np.ascontiguousarray(np.stack([later, later.T], 1))
    f["before"] = np.ascontiguousarray((np.arange(8)[None, :] < np.arange(8)[:, None]).astype(np.float32).reshape(1, 64))
    up = {k: np.asarray(i[f"L0_ffn_{k}"]) for k in ("gate_w", "wg", "wu", "wd", "sg", "su", "sd")}
    f["f0_gate"] = np.ascontiguousarray(up["gate_w"].T)
    f["f0_wg"], f["f0_wu"] = (np.ascontiguousarray(up[k].reshape(512, P).T) for k in ("wg", "wu"))
    f["f0_ws"] = np.ascontiguousarray(np.concatenate([up["sg"], up["su"]]).T)
    f["f0_wd"] = np.ascontiguousarray(up["wd"].transpose(0, 2, 1).reshape(4, P, P).transpose(1, 0, 2))
    f["f0_sd"] = np.ascontiguousarray(up["sd"].T)
    up = {k: np.asarray(i[f"L1_ffn_{k}"]) for k in ("gate_w", "w1", "b1", "w2", "b2")}
    f["f1_gate"] = up["gate_w"]
    f["f1_w1"] = np.ascontiguousarray(up["w1"].transpose(1, 0, 2))
    f["f1_b1"] = np.ascontiguousarray(up["b1"].reshape(8, 4, P).transpose(2, 0, 1))
    f["f1_w2"] = np.ascontiguousarray(up["w2"].reshape(8, 4, P, P).transpose(2, 0, 1, 3))
    f["f1_b2"] = up["b2"]
    up = {k: np.asarray(i[f"L2_ffn_{k}"]) for k in ("router_indices", "routing_weights", "gate_up_proj",
                                                    "gate_up_proj_bias", "down_proj", "down_proj_bias")}
    f["f2_idx"], f["f2_weights"] = (np.ascontiguousarray(up[k].reshape(2, P, -1).transpose(1, 0, 2))
                                    for k in ("router_indices", "routing_weights"))
    f["numbers"] = np.arange(8, dtype=np.float32).reshape(1, 8)
    f["f2_wgu"] = np.ascontiguousarray(up["gate_up_proj"].reshape(8, P, P, 2).transpose(1, 0, 3, 2))
    f["f2_bgu"] = np.ascontiguousarray(up["gate_up_proj_bias"].reshape(8, P, 2).transpose(1, 0, 2))
    f["f2_down"] = np.ascontiguousarray(up["down_proj"].transpose(1, 0, 2))
    f["f2_bdown"] = up["down_proj_bias"]
    up = {k: np.asarray(i[f"L3_ffn_{k}"]) for k in ("gate_w", "shared_gate_w", "shared_gate_up_w", "shared_down_w",
                                                    "expert_gate_up_w", "expert_down_w")}
    f["f3_gate"] = np.ascontiguousarray(np.concatenate([up["gate_w"], up["shared_gate_w"]], 1))
    f["f3_up"] = np.ascontiguousarray(up["expert_gate_up_w"].transpose(1, 0, 2))
    f["f3_down"] = np.ascontiguousarray(up["expert_down_w"].reshape(32, P, P).transpose(1, 0, 2))
    f["f3_sgu"] = up["shared_gate_up_w"]
    f["f3_sdown"] = np.ascontiguousarray(up["shared_down_w"].reshape(2, P, P).transpose(1, 0, 2))
    f["order"] = (T // 2 - np.arange(T // 2, dtype=np.float32)).reshape(1, -1)
    f["slots"] = np.arange(CAPACITY, dtype=np.float32).reshape(1, -1)
    f["region"] = np.repeat(np.array([0, T + CAPACITY], np.float32), 64).reshape(P, 1)
    mask = np.asarray(i["mask_SxS2_bk1"]).view(np.uint8)
    f["umask"] = np.ascontiguousarray(np.stack([mask, mask.T], 1))
    return f


def kernel(**inputs):
    import numpy as _np
    import concourse.bacc as _bacc
    from concourse import mybir as _mybir
    from concourse.bass_utils import run_bass_kernel_spmd as _run

    nc = _bacc.Bacc("TRN2", target_bir_lowering=False, num_devices=1)
    arrays = {f"in_{k}": _np.ascontiguousarray(a) for k, a in host_arrays(inputs).items()}
    dram = {k[3:]: nc.dram_tensor(k, a.shape, _mybir.dt.from_np(a.dtype), kind="ExternalInput").ap()
            for k, a in arrays.items()}
    out = nc.dram_tensor("out_0_dram", (NT, P, P), F32, kind="ExternalOutput").ap()
    build(nc, dram, out)
    r = _run(nc, [arrays], core_ids=[0])
    return r.results[0]["out_0_dram"]
```

```python
from contextlib import ExitStack

import numpy as np

import concourse.bass as bass
from concourse import mybir

F32 = mybir.dt.float32
BF16 = mybir.dt.bfloat16
I32 = mybir.dt.int32
U8 = mybir.dt.uint8
ALU = mybir.AluOpType
ACT = mybir.ActivationFunctionType
AX = mybir.AxisListType.X

P = 128
NT = 32
T = NT * P
GT = 4
GN = GT * P
NG = NT // GT
H, HD = 16, 8
TERMS = 6
SR = TERMS * HD
EPS = 1e-5
NEG = -float(2 ** 60)
STACKS = 3
FIRST_SEMAPHORE = 128
FIRST_GPSIMD_SEMAPHORE = 236
HALVES = 2
BLOCKS = NT // HALVES + 8
CAPACITY = 64
ZERO_COLS = (T + CAPACITY) // 4
Q_PARTS = (0, 0, 0, 1, 1, 2)
K_RUNS = (3, 2, 1)


class Core:
    pass


def semaphores(nc, c, prefix, names):
    taken = [c.ctx.enter_context(nc.semaphore(f"{prefix}_{n}", num=c.next_semaphore + k))
             for k, n in enumerate(names.split())]
    c.next_semaphore += len(taken)
    return taken


def gpsimd_dma_semaphores(nc, c, prefix, names):
    taken = [c.program.enter_context(nc.semaphore(f"{prefix}_{n}", num=c.next_gpsimd_semaphore + k))
             for k, n in enumerate(names.split())]
    c.next_gpsimd_semaphore += len(taken)
    return taken


def zero_semaphores(nc, c):
    with nc.Block() as block:
        @block.gpsimd
        def _(pool):
            pool.sem_clear(range(FIRST_SEMAPHORE, c.next_semaphore))


def done(n, credit=2):
    return n + (1 + credit)


def free(n):
    return n + 1


def ln_vector(nc, c, dve, sems):
    var_ready, root_ready, chain = sems
    nc.vector.tensor_scalar(c.veps[:], c.mv[:, :, 1], EPS, None, ALU.add).then_inc(var_ready, 1)
    dve.wait_ge(root_ready, 1)
    nc.vector.reciprocal(c.rstd0[:], c.root[:]).then_inc(chain, 1)
    dve.wait_ge(chain, 1)
    nc.vector.tensor_tensor(c.newt[:], c.rstd0[:], c.rstd0[:], ALU.mult).then_inc(chain, 1)
    dve.wait_ge(chain, 2)
    nc.vector.tensor_tensor(c.newt[:], c.newt[:], c.veps[:], ALU.mult).then_inc(chain, 1)
    dve.wait_ge(chain, 3)
    nc.vector.tensor_scalar(c.newt[:], c.newt[:], -0.5, 1.5, ALU.mult, ALU.add).then_inc(chain, 1)
    dve.wait_ge(chain, 4)
    nc.vector.tensor_tensor(c.rstd[:], c.newt[:], c.rstd0[:], ALU.mult).then_inc(chain, 1)
    dve.wait_ge(chain, 5)


def ln_scalar(nc, c, act, sems):
    var_ready, root_ready, _ = sems
    act.wait_ge(var_ready, 1)
    nc.scalar.activation(c.root[:], c.veps[:], ACT.Sqrt).then_inc(root_ready, 1)


def scratch(nc, ctx, prefix, shapes):
    for name, (shape, dt) in shapes.items():
        yield ctx.enter_context(nc.sbuf_tensor(f"{prefix}_{name}", shape, dt))


def run_steps(engine, step, first, unroll, loops, last):
    for i in range(first):
        step(i, 0)
    with engine.Fori(0, loops) as r:
        for j in range(unroll):
            step(first + j, r)
    for i in range(first + unroll * loops, last):
        step(i, 0)


class Item:

    def __init__(self, n, r, unroll, total=NT):
        self.n, self.r, self.unroll = n, r, unroll
        self.live = not isinstance(r, int) or 0 <= n < total
        self.b = n % 2
        self.stack = (n // 2) % STACKS
        self.half = slice((n % 2) * P, (n % 2) * P + P)

    def items(self, k, m=0):
        return self.r * (self.unroll * k) + (self.n * k + m)

    @property
    def t(self):
        return self.items(1)

    @property
    def turn(self):
        return self.r * (self.unroll // 2) + self.n // 2

    @property
    def fill(self):
        return self.r * (self.unroll // 2 // STACKS) + self.n // 2 // STACKS


def project(nc, c, layer):
    rope = layer == 3

    pre = f"p{layer}"
    ln = semaphores(nc, c, pre, "var root chain")
    (xn_ready, xt_psum, xt_ready, q_psum, k_psum, v_psum, ctx_ready, v_ready,
     hi_ready, res_ready, mid_ready, lo_ready, turned, roped) = semaphores(
        nc, c, pre, "xn xtp xt q k v ctx vdone hi res mid lo turned roped")
    parts_out = semaphores(nc, c, pre, "out0 out1")
    wq, wk, wv = (c.wa[:, layer, n, :] for n in range(3))
    bias = [c.bcol[:, 2 * layer + n:2 * layer + n + 1] for n in range(2)]
    xt_bank = [c.bank[n] for n in (0, 1)]
    qk_bank = [[c.bank[2], c.bank[3]], [c.bank[4], c.bank[5]]]
    v_bank = [c.bank[n] for n in (6, 7)]

    with ExitStack() as own, nc.Block() as block:
        c.xn, c.xnT, c.ctxg, c.parts, c.resid = scratch(nc, own, pre, dict(
            xn=([P, 2, GT, P], F32), xnT=([P, 2, GN], F32), ctxg=([P, 2, GN], F32),
            parts=([P, 2, 2, 3, GN], BF16), resid=([P, 2, 2, GN], F32)))
        if rope:
            c.roped, c.rot = scratch(nc, own, pre, dict(roped=([P, 2, 2, GN], F32), rot=([P, 2, GT, P], F32)))

        @block.gpsimd
        def _(pool):
            pool.sem_inc(ctx_ready, 2)
            pool.sem_inc(lo_ready, 4)
            with pool.Fori(0, NG // 2) as it:
                for b in range(2):
                    g = it * 2 + b
                    pool.wait_ge(v_psum, free(g))
                    nc.gpsimd.tensor_copy(c.ctxg[:, b, :], c.ctxT[:, bass.ds(g * GN, GN)]).then_inc(ctx_ready, 1)
                    pool.wait_ge(xn_ready, done(g))
                    nc.gpsimd.tensor_tensor(
                        c.x[:, bass.ds(g * GT, GT), :], c.x[:, bass.ds(g * GT, GT), :],
                        c.brow[:, 2 * layer + 1:2 * layer + 2, :].to_broadcast([P, GT, P]), ALU.add)
                    for n in range(2):
                        m = g * 2 + n
                        pool.wait_ge(mid_ready, done(m, 4))
                        nc.gpsimd.tensor_tensor(c.parts[:, b, n, 2, :], c.resid[:, b, n, :],
                                                c.parts[:, b, n, 1, :], ALU.subtract).then_inc(lo_ready, 1)

        @block.vector
        def _(dve):
            dve.sem_inc(xn_ready, 2)
            dve.sem_inc(v_ready, 2)
            dve.sem_inc(res_ready, 4)
            if rope:
                dve.sem_inc(roped, 2)
            ln_vector(nc, c, dve, ln)
            with dve.Fori(0, NG // 2) as it:
                for b in range(2):
                    g = it * 2 + b
                    dve.wait_ge(xt_psum, free(g))
                    for j in range(GT):
                        t = g * GT + j
                        last = nc.vector.tensor_scalar(c.xn[:, b, j, :], c.x[:, t, :], c.mv[:, t, 0:1],
                                                       c.rstd[:, bass.ds(t, 1)], ALU.subtract, ALU.mult)
                    last.then_inc(xn_ready, 1)
                    for n, psum in enumerate((q_psum, k_psum)):
                        m = g * 2 + n
                        dve.wait_ge(psum, done(g))
                        if rope:
                            main, rot = (qk_bank[n][k].rearrange("p (j t) -> p j t", j=GT) for k in range(2))
                            cos = c.rope[:, 0:1, :].to_broadcast([P, GT, P])
                            sin = c.rope[:, 1:2, :].to_broadcast([P, GT, P])
                            nc.vector.scalar_tensor_tensor(c.rot[:, 0], main, bias[n], cos, ALU.add, ALU.mult)
                            nc.vector.scalar_tensor_tensor(c.rot[:, 1], rot, c.bcol[:, 8 + n:9 + n], sin,
                                                           ALU.add, ALU.mult).then_inc(turned, 1)
                            dve.wait_ge(turned, m + 1)
                            dve.wait_ge(hi_ready, free(m))
                            nc.vector.tensor_tensor(c.roped[:, b, n, :], c.rot[:, 0].rearrange("p j t -> p (j t)"),
                                                    c.rot[:, 1].rearrange("p j t -> p (j t)"),
                                                    ALU.add).then_inc(roped, 1)
                        dve.wait_ge(hi_ready, done(m, 4))
                        dve.wait_ge(lo_ready, free(m))
                        if rope:
                            nc.vector.tensor_tensor(c.resid[:, b, n, :], c.roped[:, b, n, :],
                                                    c.parts[:, b, n, 0, :], ALU.subtract).then_inc(res_ready, 1)
                        else:
                            nc.vector.scalar_tensor_tensor(c.resid[:, b, n, :], qk_bank[n][b], bias[n],
                                                           c.parts[:, b, n, 0, :], ALU.add,
                                                           ALU.subtract).then_inc(res_ready, 1)
                    dve.wait_ge(v_psum, done(g))
                    nc.vector.tensor_tensor(
                        c.v[:, bass.ds(g * GT, GT), :], v_bank[b].rearrange("p (j f) -> p j f", j=GT),
                        c.brow[:, 2 * layer:2 * layer + 1, :].to_broadcast([P, GT, P]), ALU.add
                    ).then_inc(v_ready, 1)

        @block.scalar
        def _(act):
            act.sem_inc(xt_ready, 2)
            act.sem_inc(hi_ready, 4)
            act.sem_inc(mid_ready, 4)
            ln_scalar(nc, c, act, ln)
            with act.Fori(0, NG // 2) as it:
                for b in range(2):
                    g = it * 2 + b
                    act.wait_ge(xt_psum, done(g))
                    act.wait_ge(q_psum, free(g))
                    nc.scalar.activation(c.xnT[:, b, :], xt_bank[b], ACT.Identity).then_inc(xt_ready, 1)
                    act.wait_ge(parts_out[b], it * 64 + 64)
                    for n, psum in enumerate((q_psum, k_psum)):
                        m = g * 2 + n
                        if rope:
                            act.wait_ge(roped, done(m))
                            nc.scalar.activation(c.parts[:, b, n, 0, :], c.roped[:, b, n, :],
                                                 ACT.Identity).then_inc(hi_ready, 1)
                        else:
                            act.wait_ge(psum, done(g))
                            nc.scalar.activation(c.parts[:, b, n, 0, :], qk_bank[n][b], ACT.Identity,
                                                 bias=bias[n]).then_inc(hi_ready, 1)
                    for n in range(2):
                        act.wait_ge(res_ready, done(g * 2 + n, 4))
                        nc.scalar.activation(c.parts[:, b, n, 1, :], c.resid[:, b, n, :],
                                             ACT.Identity).then_inc(mid_ready, 1)

        @block.tensor
        def _(pe):
            for s in (xt_psum, q_psum, k_psum, v_psum):
                pe.sem_inc(s, 2)
            with pe.Fori(0, NG // 2) as it:
                for b in range(2):
                    g = it * 2 + b
                    pe.wait_ge(xn_ready, done(g))
                    pe.wait_ge(xt_ready, free(g))
                    for j in range(GT):
                        last = nc.tensor.transpose(xt_bank[b][:, j * P:(j + 1) * P], c.xn[:, b, j, :], c.ident[:])
                    last.then_inc(xt_psum, 1)
                    pe.wait_ge(xt_ready, done(g))
                    keys = c.ctxT[:, bass.ds(g * GN, GN)]
                    for n, (psum, w, src) in enumerate(((q_psum, wq, c.xnT[:, b, :]), (k_psum, wk, keys))):
                        m = g * 2 + n
                        if rope:
                            pe.wait_ge(roped, m + 1)
                            nc.tensor.matmul(qk_bank[n][0], w, src, start=True, stop=True)
                            nc.tensor.matmul(qk_bank[n][1], c.wrot[:, n, :], src, start=True,
                                             stop=True).then_inc(psum, 1)
                        else:
                            pe.wait_ge(res_ready, free(m))
                            nc.tensor.matmul(qk_bank[n][b], w, src, start=True, stop=True).then_inc(psum, 1)
                    pe.wait_ge(ctx_ready, done(g))
                    pe.wait_ge(v_ready, free(g))
                    for j in range(GT):
                        last = nc.tensor.matmul(v_bank[b][:, j * P:(j + 1) * P], c.ctxg[:, b, j * P:(j + 1) * P],
                                                wv, start=True, stop=True)
                    last.then_inc(v_psum, 1)

        @block.sync
        def _(sp):
            for s in parts_out:
                sp.sem_inc(s, 64)
            with sp.Fori(0, NG // 2) as it:
                for b in range(2):
                    g = it * 2 + b
                    sp.wait_ge(lo_ready, done(g * 2 + 1, 4))
                    tokens = bass.ds(g * GN, GN)
                    for part in range(3):
                        copies = [n for n, p in enumerate(Q_PARTS) if p == part]
                        sp.dma_start(c.q_dram[:, copies[0]:copies[-1] + 1, tokens],
                                     c.parts[:, b, 0, part:part + 1, :].to_broadcast([P, len(copies), GN])
                                     ).then_inc(parts_out[b], 16)
                    sp.dma_start(c.k_dram[:, :, tokens], c.parts[:, b, 1, :, :]).then_inc(parts_out[b], 16)
            for s in parts_out:
                sp.wait_ge(s, 64 * (NG // 2 + 1))


def attend(nc, c, layer):
    scale = 1.0 if layer == 0 else float(1 / np.sqrt(np.float32(HD)))
    mask = {0: 0, 2: 1}.get(layer)

    (scores, maxed, m_ready, mt_psum, mt_ready, st_psum, exp_ready, vx_ready, pv_psum, pv_ready,
     n_psum, rd_ready, n_ready, at_psum, at_ready, y_psum, x_ready, stats_ready, hi_ready,
     mv_ready, x_stored) = semaphores(
        nc, c, f"a{layer}", "s max m mtp mt st exp vx pvp pv np rd n atp at y x bn hi mv xst")
    m_rows = semaphores(nc, c, f"a{layer}", "row0 row1")
    stacked = semaphores(nc, c, f"a{layer}", "stack0 stack1 stack2")
    wo = c.wa[:, layer, 3, :]
    s_bank = [c.bank[n].rearrange("p (h k) -> p h k", h=4) for n in (0, 1)]
    st_bank = [c.bank[n] for n in (2, 3)]
    pv = c.bank[4][:, 0:2 * P].rearrange("p (a q) -> p a q", a=2)
    back = c.bank[5][:, 0:2 * P]
    at = c.bank[6][:, 0:P]
    mt = c.bank[6][:, P:P + P // 2].bitcast(BF16)
    y = c.bank[7][:, 0:P]
    LAG = dict(S=0, M=1, ST=2, PV=3, BACK=4, AT=5, Y=6, X=7)
    FIRST, LOOPS, U = 8, 4, 6
    LAST = NT + LAG["X"]

    def steps(engine, step, loops=LOOPS):
        run_steps(engine, step, FIRST, U, loops, LAST)

    def Tile(i, r, lag):
        return Item(i - lag, r, U)

    with ExitStack() as own, nc.Block() as block:
        c.pt, c.m, c.mneg, c.mt, c.pvs, c.rd, c.an, c.at = scratch(nc, own, f"a{layer}", dict(
            pt=([P, 2, H, P], F32), m=([P, 2, H], F32), mneg=([P, 2, 2 * H], BF16), mt=([2 * H, 2, P], BF16),
            pvs=([P, 2, 2, P], F32), rd=([P, 2, H], F32), an=([P, 2, P], F32), at=([P, 2, P], F32)))

        @block.tensor
        def _(pe):
            for s in (scores, st_psum, mt_psum, pv_psum, n_psum, at_psum, y_psum):
                pe.sem_inc(s, 2)

            def quarter(a, q):
                if not a.live:
                    return
                n = a.items(4, q)
                pe.wait_ge(maxed, free(n))
                if q == 0 and a.n % 2 == 0:
                    pe.wait_ge(stacked[a.stack], a.fill * c.STACK_INCS + c.STACK_INCS)
                for h in range(4):
                    last = nc.tensor.matmul(s_bank[q % 2][:, h, :], c.qs[:, a.stack, 4 * q + h, a.half],
                                            c.ks[:, a.stack, 4 * q + h, a.half], start=mask is None or h == 0,
                                            stop=mask is None)
                if mask is not None:
                    last = nc.tensor.matmul(s_bank[q % 2], c.identb[:], c.mask[:, mask, 0],
                                            start=False, stop=True)
                last.then_inc(scores, 1)

            def turned_quarter(a, q):
                if not a.live:
                    return
                n = a.items(4, q)
                if q == 0:
                    pe.wait_ge(m_rows[a.b], a.turn * 16 + 16)
                pe.wait_ge(exp_ready, free(n))
                for h in range(4):
                    last = nc.tensor.matmul(st_bank[q % 2][:, h * P:(h + 1) * P],
                                            c.ks[:, a.stack, 4 * q + h, a.half],
                                            c.qs[:, a.stack, 4 * q + h, a.half],
                                            start=mask is None or h == 0, stop=mask is None)
                if mask is not None:
                    last = nc.tensor.matmul(st_bank[q % 2], c.identb[:],
                                            c.mask[:, mask, 1].rearrange("p h k -> p (h k)"),
                                            start=False, stop=True)
                last.then_inc(st_psum, 1)

            def values(a, f):
                if not a.live:
                    return
                if f == 0:
                    pe.wait_ge(vx_ready, done(a.t))
                    pe.wait_ge(pv_ready, a.items(1, 2))
                pe.wait_ge(exp_ready, done(a.items(4, 2 * f + 1)))
                for odd in range(2):
                    for g in range(4):
                        h = 8 * f + 2 * g + odd
                        last = nc.tensor.matmul(pv[32 * g:32 * g + 32, f, :], c.vx[:, a.b, h, :],
                                                c.pt[:, a.b, h, :], start=odd == 0, stop=odd == 1)
                if f == 1:
                    last.then_inc(pv_psum, 1)

            def step(i, r):
                s, m, st, v, bk, a, yy = (Tile(i, r, LAG[k]) for k in ("S", "M", "ST", "PV", "BACK", "AT", "Y"))
                quarter(s, 0)
                turned_quarter(st, 0)
                if m.live:
                    pe.wait_ge(m_ready, done(m.t))
                    pe.wait_ge(mt_ready, m.items(1, 2))
                    if yy.live:
                        pe.wait_ge(at_ready, done(yy.t))
                    nc.tensor.transpose(mt[0:2 * H, :], c.mneg[:, m.b, :], c.identb[:]).then_inc(mt_psum, 1)
                turned_quarter(st, 1)
                quarter(s, 1)
                values(v, 0)
                quarter(s, 2)
                turned_quarter(st, 2)
                if bk.live:
                    pe.wait_ge(pv_ready, done(bk.t))
                    pe.wait_ge(n_ready, bk.items(1, 2))
                    for f in range(2):
                        last = nc.tensor.transpose(back[:, f * P:(f + 1) * P], c.pvs[:, bk.b, f, :], c.ident[:])
                    last.then_inc(n_psum, 1)
                turned_quarter(st, 3)
                quarter(s, 3)
                values(v, 1)
                if a.live:
                    pe.wait_ge(n_ready, done(a.t))
                    if m.live:
                        pe.wait_ge(mt_ready, done(m.t))
                    pe.wait_ge(at_ready, a.items(1, 2))
                    nc.tensor.transpose(at, c.an[:, a.b, :], c.ident[:]).then_inc(at_psum, 1)
                if yy.live:
                    pe.wait_ge(at_ready, done(yy.t))
                    pe.wait_ge(x_ready, yy.items(1, 2))
                    nc.tensor.matmul(y, c.at[:, yy.b, :], wo, start=True, stop=True).then_inc(y_psum, 1)

            steps(pe, step)

        @block.vector
        def _(dve):
            for s in (maxed, m_ready, n_ready, x_ready):
                dve.sem_inc(s, 2)

            def quarter_max(a, q):
                if not a.live:
                    return
                n = a.items(4, q)
                dve.wait_ge(scores, done(n))
                if q == 0:
                    dve.wait_ge(m_ready, free(a.t))
                nc.vector.reduce_max(c.m[:, a.b, 4 * q:4 * q + 4], s_bank[q % 2], AX).then_inc(maxed, 1)

            def step(i, r):
                s, bk, xx = (Tile(i, r, LAG[k]) for k in ("S", "BACK", "X"))
                quarter_max(s, 0)
                if xx.live:
                    dve.wait_ge(y_psum, done(xx.t))
                    dve.wait_ge(x_stored, free(xx.t))
                    nc.vector.tensor_tensor(c.xs[:, xx.b, :], c.x[:, xx.t, :], y, ALU.add).then_inc(x_ready, 1)
                    dve.wait_ge(x_ready, done(xx.t))
                    nc.vector.bn_stats(c.stats[:, xx.b, :], c.xs[:, xx.b, :]).then_inc(stats_ready, 1)
                if xx.live:
                    dve.wait_ge(stats_ready, xx.t + 1)
                quarter_max(s, 1)
                if xx.live:
                    nc.vector.bn_aggr(c.mvs[:, xx.b, :], c.stats[:, xx.b, :]).then_inc(mv_ready, 1)
                quarter_max(s, 2)
                if bk.live:
                    dve.wait_ge(n_psum, done(bk.t))
                    heads = back.rearrange("p (h e) -> p h e", h=H)
                    nc.vector.reciprocal(c.rd[:, bk.b, :], heads[:, :, HD]).then_inc(rd_ready, 1)
                    dve.wait_ge(rd_ready, bk.t + 1)
                    dve.wait_ge(at_psum, free(bk.t))
                    nc.vector.tensor_tensor(c.an[:, bk.b, :].rearrange("p (h d) -> p h d", h=H), heads[:, :, 0:HD],
                                            c.rd[:, bk.b, :].rearrange("p (h a) -> p h a", a=1).to_broadcast([P, H, HD]),
                                            ALU.mult).then_inc(n_ready, 1)
                quarter_max(s, 3)
                if s.live:
                    dve.wait_ge(maxed, done(s.items(4, 3)))
                    dve.wait_ge(mt_psum, free(s.t))
                    nc.vector.tensor_scalar(c.mneg[:, s.b, 0:H], c.m[:, s.b, :], -1.0, None, ALU.mult).then_inc(hi_ready, 1)
                    dve.wait_ge(hi_ready, s.t + 1)
                    nc.vector.scalar_tensor_tensor(c.mneg[:, s.b, H:2 * H], c.m[:, s.b, :], -1.0,
                                                   c.mneg[:, s.b, 0:H], ALU.mult, ALU.subtract).then_inc(m_ready, 1)

            steps(dve, step)

        @block.scalar
        def _(act):
            for s in (mt_ready, exp_ready, pv_ready, at_ready):
                act.sem_inc(s, 2)

            def exponentials(a, q):
                if not a.live:
                    return
                act.wait_ge(st_psum, done(a.items(4, q)))
                if q == 0:
                    act.wait_ge(pv_psum, free(a.t))
                nc.scalar.activation(c.pt[:, a.b, 4 * q:4 * q + 4, :].rearrange("p h q -> p (h q)"),
                                     st_bank[q % 2], ACT.Exp, scale=scale).then_inc(exp_ready, 1)

            def step(i, r):
                m, st, v, yy = (Tile(i, r, LAG[k]) for k in ("M", "ST", "PV", "Y"))
                if yy.live:
                    act.wait_ge(at_psum, done(yy.t))
                    act.wait_ge(y_psum, free(yy.t))
                    nc.scalar.activation(c.at[:, yy.b, :], at, ACT.Identity).then_inc(at_ready, 1)
                exponentials(st, 0)
                if m.live:
                    act.wait_ge(mt_psum, done(m.t))
                    act.wait_ge(m_rows[m.b], m.turn * 16)
                    nc.scalar.activation(c.mt[:, m.b, :], mt[0:2 * H, :], ACT.Identity).then_inc(mt_ready, 1)
                for q in (1, 2, 3):
                    exponentials(st, q)
                if v.live:
                    act.wait_ge(pv_psum, done(v.t))
                    act.wait_ge(n_psum, free(v.t))
                    nc.scalar.activation(c.pvs[:, v.b], pv, ACT.Identity).then_inc(pv_ready, 1)

            steps(act, step)

        @block.gpsimd
        def _(pool):
            pool.sem_inc(vx_ready, 2)
            pool.sem_inc(x_stored, 2)

            def step(i, r):
                spread_values(Tile(i, r, LAG["M"]))
                store(Tile(i, r, LAG["X"]))

            def store(a):
                if not a.live:
                    return
                pool.wait_ge(mv_ready, a.t + 1)
                nc.gpsimd.tensor_copy(c.x[:, a.t, :], c.xs[:, a.b, :])
                nc.gpsimd.tensor_copy(c.mv[:, a.t, :], c.mvs[:, a.b, :]).then_inc(x_stored, 1)

            def spread_values(a):
                if not a.live:
                    return
                pool.wait_ge(pv_psum, free(a.t))
                src = c.v[:, a.t, :].rearrange("p (g o d) -> p g o d", o=2, d=HD)
                dst = c.vx[:, a.b].rearrange("p (g o) e -> p g o e", o=2)
                for odd in range(2):
                    last = nc.gpsimd.tensor_copy(dst[:, :, odd, 16 * odd:16 * odd + HD], src[:, :, odd, :])
                last.then_inc(vx_ready, 1)

            steps(pool, step)

        @block.sync
        def _(sp):
            def load(a):
                incs = stacked[a.stack]
                pair = bass.ds(a.t * P, 2 * P)
                sp.dma_start(c.qs[0:SR + 2, a.stack], c.q_stack_dram[:, :, pair]).then_inc(incs, 16)
                start = 0
                for run in K_RUNS:
                    sp.dma_start(c.ks[start:start + run * HD, a.stack],
                                 c.k_stack_dram[0:run * HD, :, pair]).then_inc(incs, 16)
                    start += run * HD

            for p in range(2):
                load(Tile(2 * p, 0, 0))

            def step(i, r):
                m = Tile(i, r, LAG["M"])
                if m.live:
                    sp.wait_ge(mt_ready, done(m.t))
                    sp.dma_start(c.qs[SR:SR + 2, m.stack, :, m.half], c.mt[:, m.b, :]).then_inc(m_rows[m.b], 16)
                nxt = Tile(i, r, -3)
                if i % 2 == 1 and nxt.live:
                    if not isinstance(r, int) or i >= 3:
                        sp.wait_ge(st_psum, done(Tile(i, r, 2).items(4, 3)))
                    load(nxt)

            steps(sp, step, LOOPS - 1)
            for row in range(2):
                sp.wait_ge(m_rows[row], NT // 2 * 16)


def route(nc, c, layer, experts, top, loads):
    pre = f"r{layer}"
    ln = semaphores(nc, c, pre, "var root chain")
    (xn_ready, xt_psum, xt_ready, xt_kept, log_psum, log_ready, soft, exp_ready, gate_in) = semaphores(
        nc, c, pre, "xn xtp xt keep lp log soft exp gate")
    loaded, = semaphores(nc, c, pre, "loaded")
    table_out = semaphores(nc, c, pre, "out0 out1")
    E = loads[0][0].shape[-1]
    gate = loads[0][0]
    big, rows = layer == 3, layer == 1
    xt_bank, log_bank = [c.bank[n] for n in (0, 1)], [c.bank[n] for n in (2, 3)]
    with ExitStack() as own, nc.Block() as block:
        xn, xnT, logits, mx, tot = scratch(nc, own, pre, dict(
            xn=([P, 2, GT, P], F32), xnT=([P, 2, GN], F32), logits=([P, NT, E], F32), mx=([P, NT], F32),
            tot=([P, NT], F32)))
        if not big:
            above, rank = scratch(nc, own, pre, dict(
                above=([P, NT, experts, experts], F32), rank=([P, NT, experts], F32)))
            equal = c.gates.rearrange("p t (e f) -> p t e f", e=experts)
        else:
            top8, rest = scratch(nc, own, pre, dict(top8=([P, NT, 8], F32), rest=([P, NT, experts], F32)))
        scores = logits[:, :, 0:experts]

        @block.sync
        def _(sp):
            sp.dma_start(gate, loads[0][1]).then_inc(gate_in, 16)
            for dst, src in loads[1:]:
                sp.dma_start(dst, src).then_inc(loaded, 16)
            if big:
                for s in table_out:
                    sp.sem_inc(s, 16)
                with sp.Fori(0, NG // 2) as it:
                    for b in range(2):
                        g = it * 2 + b
                        sp.wait_ge(xn_ready, done(g))
                        sp.dma_start(c.table[bass.ds(g * GN, GN), 0:P].rearrange("(j t) f -> t j f", t=P), xn[:, b]).then_inc(table_out[b], 16)
                for s in table_out:
                    sp.wait_ge(s, 16 * (NG // 2 + 1))
            sp.wait_ge(loaded, 16 * (len(loads) - 1))

        @block.gpsimd
        def _(pool):
            pool.sem_inc(xt_kept, 2)
            with pool.Fori(0, NG // 2) as it:
                for b in range(2):
                    g = it * 2 + b
                    if rows:
                        pool.wait_ge(xn_ready, done(g))
                        nc.gpsimd.tensor_copy(c.v[:, bass.ds(g * GT, GT), :], xn[:, b]).then_inc(xt_kept, 1)
                    else:
                        pool.wait_ge(xt_ready, done(g))
                        nc.gpsimd.tensor_copy(c.xT[:, bass.ds(g * GN, GN)], xnT[:, b, :]).then_inc(xt_kept, 1)

        @block.vector
        def _(dve):
            dve.sem_inc(xn_ready, 2)
            ln_vector(nc, c, dve, ln)
            with dve.Fori(0, NG // 2) as it:
                for b in range(2):
                    g = it * 2 + b
                    dve.wait_ge(xt_psum, free(g))
                    if rows:
                        dve.wait_ge(xt_kept, free(g))
                    if big:
                        dve.wait_ge(table_out[b], it * 16 + 16)
                    for j in range(GT):
                        t = g * GT + j
                        last = nc.vector.tensor_scalar(xn[:, b, j, :], c.x[:, t, :], c.mv[:, t, 0:1],
                                                       c.rstd[:, bass.ds(t, 1)], ALU.subtract, ALU.mult)
                    last.then_inc(xn_ready, 1)
            dve.wait_ge(log_ready, done(NG - 1))
            links = [0]

            def link(instruction):
                instruction.then_inc(soft, 1)
                links[0] += 1
                dve.wait_ge(soft, links[0])

            wide = [P, NT, experts]
            link(nc.vector.reduce_max(mx[:], scores, AX))
            link(nc.vector.tensor_tensor(scores, scores, mx.rearrange("p (t a) -> p t a", a=1).to_broadcast(wide),
                                         ALU.subtract))
            dve.wait_ge(exp_ready, 1)
            link(nc.vector.reduce_sum(tot[:], scores, AX))
            link(nc.vector.reciprocal(tot[:], tot[:]))
            link(nc.vector.tensor_tensor(scores, scores, tot.rearrange("p (t a) -> p t a", a=1).to_broadcast(wide),
                                         ALU.mult))
            if not big:
                other = scores.rearrange("p t (a e) -> p t a e", a=1).to_broadcast([P, NT, experts, experts])
                mine = scores.rearrange("p t (e a) -> p t e a", a=1).to_broadcast([P, NT, experts, experts])
                nc.vector.tensor_tensor(above[:], other, mine, ALU.is_gt)
                link(nc.vector.tensor_tensor(equal, other, mine, ALU.is_equal))
                flat = [x.rearrange("p t e f -> p t (e f)") for x in (above, equal)]
                link(nc.vector.tensor_tensor(flat[1], flat[1], c.before[:].to_broadcast([P, NT, experts ** 2]), ALU.mult))
                link(nc.vector.tensor_tensor(flat[0], flat[0], flat[1], ALU.add))
                link(nc.vector.reduce_sum(rank[:], above[:], AX))
                nc.vector.scalar_tensor_tensor(c.gates[:, :, 0:experts], rank[:], float(top), scores, ALU.is_lt, ALU.mult)
            else:
                for t in range(NT):
                    last = nc.vector.max(top8[:, t, :], scores[:, t, :])
                link(last)
                for t in range(NT):
                    last = nc.vector.match_replace(rest[:, t, :], top8[:, t, :], scores[:, t, :], -1.0)
                link(last)
                link(nc.vector.reduce_sum(tot[:], top8[:], AX))
                link(nc.vector.reciprocal(tot[:], tot[:]))
                link(nc.vector.tensor_scalar(rest[:], rest[:], 0.0, None, ALU.is_lt))
                nc.vector.tensor_copy(c.chosen.rearrange("p t h e -> p h t e"), rest.rearrange("p (h t) e -> p h t e", h=2))
                link(nc.vector.tensor_tensor(scores, scores, rest[:], ALU.mult))
                nc.vector.tensor_tensor(c.gates[:], scores, tot.rearrange("p (t a) -> p t a", a=1).to_broadcast(wide),
                                        ALU.mult)

        @block.scalar
        def _(act):
            act.sem_inc(xt_ready, 2)
            act.sem_inc(log_ready, 2)
            ln_scalar(nc, c, act, ln)
            with act.Fori(0, NG // 2) as it:
                for b in range(2):
                    g = it * 2 + b
                    act.wait_ge(xt_psum, done(g))
                    act.wait_ge(log_psum, free(g))
                    if not rows:
                        act.wait_ge(xt_kept, free(g))
                    nc.scalar.activation(xnT[:, b, :], xt_bank[b], ACT.Identity).then_inc(xt_ready, 1)
                    act.wait_ge(log_psum, done(g))
                    nc.scalar.activation(logits[:, bass.ds(g * GT, GT), :],
                                         log_bank[b][:, 0:GT * E].rearrange("p (j e) -> p j e", j=GT),
                                         ACT.Identity).then_inc(log_ready, 1)
            act.wait_ge(soft, 2)
            nc.scalar.activation(scores, scores, ACT.Exp).then_inc(exp_ready, 1)
            if big:
                nc.scalar.activation(c.shared_gate[:], logits[:, :, experts], ACT.Sigmoid)

        @block.tensor
        def _(pe):
            pe.sem_inc(xt_psum, 2)
            pe.sem_inc(log_psum, 2)
            pe.wait_ge(gate_in, 16)
            with pe.Fori(0, NG // 2) as it:
                for b in range(2):
                    g = it * 2 + b
                    pe.wait_ge(xn_ready, done(g))
                    pe.wait_ge(xt_ready, free(g))
                    for j in range(GT):
                        last = nc.tensor.transpose(xt_bank[b][:, j * P:(j + 1) * P], xn[:, b, j, :], c.ident[:])
                    last.then_inc(xt_psum, 1)
                    pe.wait_ge(xt_ready, done(g))
                    pe.wait_ge(log_ready, free(g))
                    for j in range(GT):
                        last = nc.tensor.matmul(log_bank[b][:, j * E:(j + 1) * E], xnT[:, b, j * P:(j + 1) * P], gate,
                                                start=True, stop=True)
                    last.then_inc(log_psum, 1)


def gated_mlp(nc, c, layer, w):
    first = layer == 0
    pre = f"g{layer}"
    (xt_ready, up_psum, silu_ready, h_ready, hw_ready, ht_psum, ht_ready, y_psum, x_ready, stats_ready, mv_ready,
     x_stored) = semaphores(nc, c, pre, "xt up silu h hw htp ht y x bn mv xst")
    wide = 512 if first else 256
    chunks = 5 if first else 2
    LAG = dict(UP=0, HT=1, Y=2, X=3)
    FIRST, U, LOOPS, LAST = 4, 2, 14, NT + LAG["X"]
    up_bank = [[c.bank[0], c.bank[1]], [c.bank[2], c.bank[3]]]
    shared_bank, ht_bank, hs_bank, y_bank = (c.bank[n] for n in (4, 5, 6, 7))
    routed = slice(0, 512)
    with ExitStack() as own, nc.Block() as block:
        xt, act_g, h, hT, xs, stats, mvs = scratch(nc, own, pre, dict(
            xt=([P, 2, P], F32), g=([P, 2, 640], F32), h=([P, 2, 640], F32), hT=([P, 2, 5, P], F32),
            xs=([P, 2, P], F32), stats=([P, 2, 6], F32), mvs=([P, 2, 2], F32)))

        def Tile(i, r, lag):
            return Item(i - lag, r, U)

        @block.tensor
        def _(pe):
            for s in (up_psum, ht_psum, y_psum):
                pe.sem_inc(s, 2)

            def step(i, r):
                up, ht, y = (Tile(i, r, LAG[k]) for k in ("UP", "HT", "Y"))
                if up.live:
                    pe.wait_ge(xt_ready, done(up.t))
                    pe.wait_ge(h_ready, up.items(1, 2) if first else free(up.t))
                    if first:
                        nc.tensor.matmul(up_bank[up.b][0], xt[:, up.b, :], w["wg"][:], start=True, stop=True)
                        nc.tensor.matmul(up_bank[up.b][1], xt[:, up.b, :], w["wu"][:], start=True, stop=True)
                        nc.tensor.matmul(shared_bank[:, 0:P], xt[:, up.b, :], w["ws"][:], start=True,
                                         stop=True).then_inc(up_psum, 1)
                    else:
                        nc.tensor.matmul(up_bank[up.b][0], xt[:, up.b, :], w["sgu"][:], start=True,
                                         stop=True).then_inc(up_psum, 1)
                if ht.live:
                    pe.wait_ge(hw_ready, done(ht.t))
                    pe.wait_ge(ht_ready, ht.items(1, 2))
                    for k in range(4 if first else 2):
                        last = nc.tensor.transpose(ht_bank[:, k * P:(k + 1) * P], h[:, ht.b, k * P:(k + 1) * P], c.ident[:])
                    if first:
                        last = nc.tensor.transpose(hs_bank[0:64, 0:P], h[:, ht.b, 512:576], c.ident[:])
                    last.then_inc(ht_psum, 1)
                if y.live:
                    pe.wait_ge(ht_ready, done(y.t))
                    pe.wait_ge(x_ready, y.items(1, 2))
                    for k in range(chunks):
                        rows = slice(0, 64 if k == 4 else P)
                        last = nc.tensor.matmul(y_bank[:, 0:P], hT[rows, y.b, k, :], w["wd"][rows, k, :],
                                                start=k == 0, stop=k == chunks - 1)
                    last.then_inc(y_psum, 1)

            run_steps(pe, step, FIRST, U, LOOPS, LAST)

        @block.scalar
        def _(act):
            act.sem_inc(silu_ready, 2)
            act.sem_inc(ht_ready, 2)

            def step(i, r):
                up, ht = (Tile(i, r, LAG[k]) for k in ("UP", "HT"))
                if ht.live:
                    act.wait_ge(ht_psum, done(ht.t))
                    act.wait_ge(y_psum, free(ht.t))
                    n = 4 if first else 2
                    last = nc.scalar.activation(hT[:, ht.b, 0:n, :].rearrange("p k t -> p (k t)"), ht_bank[:, 0:n * P],
                                                ACT.Identity)
                    if first:
                        last = nc.scalar.activation(hT[0:64, ht.b, 4, :], hs_bank[0:64, 0:P], ACT.Identity)
                    last.then_inc(ht_ready, 1)
                if up.live:
                    act.wait_ge(up_psum, done(up.t))
                    act.wait_ge(h_ready, free(up.t))
                    last = nc.scalar.activation(act_g[:, up.b, 0:wide], up_bank[up.b][0][:, 0:wide], ACT.Silu)
                    if first:
                        last = nc.scalar.activation(act_g[:, up.b, 512:576], shared_bank[:, 0:64], ACT.Silu)
                    last.then_inc(silu_ready, 1)

            run_steps(act, step, FIRST, U, LOOPS, LAST)

        @block.vector
        def _(dve):
            for s in (h_ready, x_ready):
                dve.sem_inc(s, 2)

            def step(i, r):
                up, xx = (Tile(i, r, LAG[k]) for k in ("UP", "X"))
                if xx.live:
                    dve.wait_ge(y_psum, done(xx.t))
                    dve.wait_ge(x_stored, free(xx.t))
                    if first:
                        nc.vector.tensor_tensor(xs[:, xx.b, :], c.x[:, xx.t, :], y_bank[:, 0:P], ALU.add).then_inc(x_ready, 1)
                    else:
                        nc.vector.scalar_tensor_tensor(xs[:, xx.b, :], y_bank[:, 0:P], c.shared_gate[:, bass.ds(xx.t, 1)],
                                                       c.x[:, xx.t, :], ALU.mult, ALU.add).then_inc(x_ready, 1)
                    if first:
                        dve.wait_ge(x_ready, done(xx.t))
                        nc.vector.bn_stats(stats[:, xx.b, :], xs[:, xx.b, :]).then_inc(stats_ready, 1)
                        dve.wait_ge(stats_ready, xx.t + 1)
                if up.live:
                    dve.wait_ge(silu_ready, done(up.t))
                    dve.wait_ge(ht_psum, free(up.t))
                    if first:
                        dve.wait_ge(hw_ready, free(up.t))
                        nc.vector.tensor_tensor(h[:, up.b, routed], act_g[:, up.b, routed], up_bank[up.b][1], ALU.mult)
                        nc.vector.tensor_tensor(h[:, up.b, 512:576], act_g[:, up.b, 512:576], shared_bank[:, 64:128],
                                                ALU.mult).then_inc(h_ready, 1)
                    else:
                        nc.vector.tensor_tensor(h[:, up.b, 0:256], act_g[:, up.b, 0:256], up_bank[up.b][0][:, 256:512],
                                                ALU.mult).then_inc(h_ready, 1)
                if xx.live and first:
                    nc.vector.bn_aggr(mvs[:, xx.b, :], stats[:, xx.b, :]).then_inc(mv_ready, 1)

            run_steps(dve, step, FIRST, U, LOOPS, LAST)

        @block.gpsimd
        def _(pool):
            for s in (xt_ready, hw_ready, x_stored):
                pool.sem_inc(s, 2)

            def stage(a):
                if a.live:
                    pool.wait_ge(up_psum, free(a.t))
                    nc.gpsimd.tensor_copy(xt[:, a.b, :], c.xT[:, bass.ds(a.t * P, P)]).then_inc(xt_ready, 1)

            def step(i, r):
                nxt, up, xx = (Tile(i, r, k) for k in (-1, LAG["UP"], LAG["X"]))
                if i == 0 and isinstance(r, int):
                    stage(up)
                stage(nxt)
                if up.live:
                    pool.wait_ge(h_ready, done(up.t))
                    if first:
                        gates = c.gates[:, up.t, 0:8].rearrange("p (e a) -> p e a", a=1).to_broadcast([P, 8, 64])
                        cols = h[:, up.b, routed].rearrange("p (e f) -> p e f", e=8)
                        nc.gpsimd.tensor_tensor(cols, cols, gates, ALU.mult).then_inc(hw_ready, 1)
                    else:
                        pool.sem_inc(hw_ready, 1)
                if xx.live:
                    if first:
                        pool.wait_ge(mv_ready, xx.t + 1)
                        nc.gpsimd.tensor_copy(c.mv[:, xx.t, :], mvs[:, xx.b, :])
                    else:
                        pool.wait_ge(x_ready, done(xx.t))
                    nc.gpsimd.tensor_copy(c.x[:, xx.t, :], xs[:, xx.b, :]).then_inc(x_stored, 1)

            run_steps(pool, step, FIRST, U, LOOPS - 1, LAST)


def places(nc, c, d):
    EX, HT = 8, NT // HALVES
    loaded, made, counts_psum, links = semaphores(nc, c, "l1", "load made counts link")
    within, total = (c.bank[n][:, 0:NT * EX].rearrange("p (g j e) -> p g j e", g=HALVES, j=HT) for n in (0, 1))
    with ExitStack() as own, nc.Block() as block:
        numbers, ones, sel, ping, pong, share, over, blocks, ends, ends_b, start, slot, late, ids = scratch(
            nc, own, "l1", dict(
                numbers=([P, BLOCKS], F32), ones=([P, P], F32), sel=([P, HALVES, HT, EX], F32),
                ping=([P, HALVES, HT, EX], F32), pong=([P, HALVES, HT, EX], F32), share=([P, HALVES, EX], F32),
                over=([P, HALVES, EX, HT], F32), blocks=([P, HALVES, EX], F32), ends=([P, HALVES, EX], F32),
                endsb=([P, HALVES, EX], F32), start=([P, HALVES, EX], F32), slot=([P, NT], F32),
                late=([1, HALVES, BLOCKS, EX], F32), ids=([1, HALVES, BLOCKS], F32)))

        @block.sync
        def _(sp):
            sp.dma_start(numbers[:], d["numbers"].partition_broadcast(P)).then_inc(loaded, 16)

        @block.tensor
        def _(pe):
            pe.wait_ge(made, 2)
            flat = sel.rearrange("p g j e -> p (g j e)")
            nc.tensor.matmul(c.bank[0][:, 0:NT * EX], c.causal[:, 0, :], flat, start=True, stop=True)
            nc.tensor.matmul(c.bank[1][:, 0:NT * EX], ones[:], flat, start=True, stop=True).then_inc(counts_psum, 1)

        @block.gpsimd
        def _(pool):
            nc.gpsimd.memset(ones[:], 1.0).then_inc(made, 1)

        @block.vector
        def _(dve):
            count = [0]

            def link(instruction):
                instruction.then_inc(links, 1)
                count[0] += 1
                dve.wait_ge(links, count[0])

            def scan(old, new, length):
                step = 1
                while step < length:
                    nc.vector.tensor_copy(new[:, :, 0:step], old[:, :, 0:step])
                    link(nc.vector.tensor_tensor(new[:, :, step:], old[:, :, step:], old[:, :, :length - step], ALU.add))
                    old, new = new, old
                    step *= 2
                return old

            gates = c.gates[:, :, 0:EX]
            nc.vector.tensor_scalar(sel.rearrange("p g j e -> p (g j) e"), gates, 0.0, None, ALU.is_gt).then_inc(made, 1)
            nc.vector.reduce_sum(c.token_gate[:], gates, AX)
            dve.wait_ge(counts_psum, 1)
            link(nc.vector.tensor_copy(ping[:], total))
            sums = scan(ping, pong, HT)
            tiles_before = pong if sums is ping else ping
            nc.vector.tensor_scalar(share[:], sums[:, :, HT - 1, :], 1.0 / P, None, ALU.mult)
            link(nc.vector.tensor_tensor(tiles_before[:], sums[:], total, ALU.subtract))
            dve.wait_ge(loaded, 16)
            for g in range(HALVES):
                last = nc.vector.tensor_tensor(
                    over[:, g], share[:, g, :].rearrange("p (e a) -> p e a", a=1).to_broadcast([P, EX, HT]),
                    numbers[:, 0:HT].rearrange("p (a k) -> p a k", a=1).to_broadcast([P, EX, HT]), ALU.is_gt)
            link(last)
            link(nc.vector.reduce_sum(blocks[:], over[:], AX))
            link(nc.vector.tensor_copy(ends[:], blocks[:]))
            done_ends = scan(ends, ends_b, EX)
            nc.vector.tensor_tensor(tiles_before[:], tiles_before[:], within, ALU.add)
            link(nc.vector.tensor_tensor(start[:], done_ends[:], blocks[:], ALU.subtract))
            link(nc.vector.tensor_scalar(start[:], start[:], float(P), None, ALU.mult))
            other = sums
            for g in range(HALVES):
                last = nc.vector.tensor_tensor(
                    other[:, g], tiles_before[:, g],
                    start[:, g:g + 1, :].to_broadcast([P, HT, EX]), ALU.add)
            link(last)
            link(nc.vector.tensor_tensor(other[:], other[:], sel[:], ALU.mult))
            link(nc.vector.reduce_sum(slot[:], other.rearrange("p g j e -> p (g j) e"), AX))
            nc.vector.tensor_copy(c.slot[:], slot[:])
            for g in range(HALVES):
                last = nc.vector.tensor_tensor(
                    late[:, g], numbers[0:1, :].rearrange("p (b a) -> p b a", a=1).to_broadcast([1, BLOCKS, EX]),
                    done_ends[0:1, g:g + 1, :].to_broadcast([1, BLOCKS, EX]), ALU.is_ge)
            link(last)
            link(nc.vector.reduce_sum(ids[:], late[:], AX))
            nc.vector.tensor_scalar(c.block_expert[:], ids.rearrange("p g b -> p (g b)"), float(EX - 1), None, ALU.min)


def routed_gelu(nc, c, w):
    CH, XB = 4, 4
    HT, NB, FF = NT // HALVES, HALVES * BLOCKS, 512
    (xt_psum, xt_ready, h_psum, hb_ready, gelu_ready, ht_psum, ht_ready, y_psum, y_ready, added, stats_ready) = semaphores(
        nc, c, "e1", "xtp xt h hb gelu htp ht yp y add bn")
    placed = gpsimd_dma_semaphores(nc, c, "e1", "place0 place1")
    back = gpsimd_dma_semaphores(nc, c, "e1", " ".join(f"back{n}" for n in range(8)))
    block_in = semaphores(nc, c, "e1", "in0 in1 in2 in3")
    y_out = semaphores(nc, c, "e1", "out0 out1")
    xt_bank, h_bank, ht_bank, y_bank = ([c.bank[n], c.bank[n + 1]] for n in (0, 2, 4, 6))
    FIRST, U, LOOPS, LAST = 4, 4, NB // 4 - 1, NB + 5
    TB = HT // 4

    def Block(i, r, lag=0):
        return Item(i - lag, r, U, NB)

    with ExitStack() as own, nc.Block() as block:
        xb, xT, hb, h, hT, y, stats = scratch(nc, own, "e1", dict(
            xb=([P, XB, P], F32), xT=([P, 2, P], F32), hb=([P, 2, FF], F32), h=([P, 2, FF], F32),
            hT=([P, 2, CH, P], F32), y=([P, 2, P], F32), stats=([P, NT, 6], F32)))

        def rows(halves, a):
            half = a.n // BLOCKS
            return halves[half][bass.ds(a.items(P, -half * BLOCKS * P), P), :]

        @block.gpsimd
        def _(pool):
            for j in range(NT):
                nc.gpsimd.indirect_dma_start(c.slots_x[j // HT][:, :], bass.IndirectOffsetOnAxis(ap=c.slot[:, j:j + 1], axis=0),
                                             c.v[:, j, :], None).then_inc(placed[j // HT], 16)
            for half in range(HALVES):
                pool.wait_ge(placed[half], 16 * HT)
                for k in range(2):
                    pool.wait_ge(y_out[k], 16 * (half + 1) * BLOCKS // 2 + 16)
                for j in range(half * HT, (half + 1) * HT):
                    nc.gpsimd.indirect_dma_start(c.v[:, j, :], None, c.slots_y[half][:, :],
                                                 bass.IndirectOffsetOnAxis(ap=c.slot[:, j:j + 1], axis=0)
                                                 ).then_inc(back[j // TB], 16)

        @block.sync
        def _(sp):
            for s in y_out:
                sp.sem_inc(s, 16)

            def step(i, r):
                x, yy = Block(i, r), Block(i, r, 5)
                if x.live:
                    if x.n >= XB:
                        sp.wait_ge(xt_psum, x.items(1, -1))
                    sp.dma_start(xb[:, x.n % XB, :], rows(c.slots_x, x)).then_inc(block_in[x.n % XB], 16)
                if yy.live:
                    sp.wait_ge(y_ready, done(yy.t))
                    sp.dma_start(rows(c.slots_y, yy), y[:, yy.b, :]).then_inc(y_out[yy.b], 16)

            sp.wait_ge(placed[0], 16 * HT)
            run_steps(sp, step, 2 * U, U, BLOCKS // U - 2, BLOCKS)
            sp.wait_ge(placed[1], 16 * HT)
            for i in range(BLOCKS, BLOCKS + 2 * U):
                step(i, 0)
            with sp.Fori(0, BLOCKS // U - 2) as r:
                for n in range(U):
                    step(BLOCKS + 2 * U + n, r)
            for i in range(NB, LAST):
                step(i, 0)
            for s in y_out:
                sp.wait_ge(s, 16 * NB // 2 + 16)

        @block.tensor
        def _(pe):
            for s in (xt_psum, h_psum, ht_psum, y_psum):
                pe.sem_inc(s, 2)

            def step(i, r):
                x, up, ht, yy = (Block(i, r, lag) for lag in range(4))
                if x.live:
                    pe.wait_ge(block_in[x.n % XB], r * 16 + (16 * (x.n // XB) + 16))
                    pe.wait_ge(xt_ready, free(x.t))
                    nc.tensor.transpose(xt_bank[x.b][:, 0:P], xb[:, x.n % XB, :], c.ident[:]).then_inc(xt_psum, 1)
                if up.live:
                    e = pe.value_load(c.block_expert[0:1, bass.ds(up.t, 1)], min_val=0, max_val=7)
                    pe.wait_ge(xt_ready, done(up.t))
                    pe.wait_ge(hb_ready, free(up.t))
                    nc.tensor.matmul(h_bank[up.b], xT[:, up.b, :],
                                     w["w1"][:, bass.ds(e, 1), :].rearrange("d a f -> d (a f)"),
                                     start=True, stop=True).then_inc(h_psum, 1)
                if ht.live:
                    pe.wait_ge(gelu_ready, done(ht.t))
                    pe.wait_ge(ht_ready, free(ht.t))
                    for k in range(CH):
                        last = nc.tensor.transpose(ht_bank[ht.b][:, k * P:(k + 1) * P], h[:, ht.b, k * P:(k + 1) * P], c.ident[:])
                    last.then_inc(ht_psum, 1)
                if yy.live:
                    e = pe.value_load(c.block_expert[0:1, bass.ds(yy.t, 1)], min_val=0, max_val=7)
                    pe.wait_ge(ht_ready, done(yy.t))
                    pe.wait_ge(y_ready, free(yy.t))
                    for k in range(CH):
                        last = nc.tensor.matmul(y_bank[yy.b][:, 0:P], hT[:, yy.b, k, :],
                                                w["w2"][:, bass.ds(e, 1), k * P:(k + 1) * P].rearrange("d a f -> d (a f)"),
                                                start=k == 0, stop=k == CH - 1)
                    last.then_inc(y_psum, 1)

            run_steps(pe, step, FIRST, U, LOOPS, LAST)

        @block.scalar
        def _(act):
            for s in (xt_ready, gelu_ready, ht_ready):
                act.sem_inc(s, 2)

            def step(i, r):
                x, up, ht = (Block(i, r, lag) for lag in range(3))
                if x.live:
                    act.wait_ge(xt_psum, done(x.t))
                    act.wait_ge(h_psum, free(x.t))
                    nc.scalar.activation(xT[:, x.b, :], xt_bank[x.b][:, 0:P], ACT.Identity).then_inc(xt_ready, 1)
                if ht.live:
                    act.wait_ge(ht_psum, done(ht.t))
                    act.wait_ge(y_psum, free(ht.t))
                    nc.scalar.activation(hT[:, ht.b].rearrange("p k t -> p (k t)"), ht_bank[ht.b],
                                         ACT.Identity).then_inc(ht_ready, 1)
                if up.live:
                    act.wait_ge(hb_ready, done(up.t))
                    act.wait_ge(ht_psum, free(up.t))
                    nc.scalar.activation(h[:, up.b, :], hb[:, up.b, :], ACT.Gelu).then_inc(gelu_ready, 1)

            run_steps(act, step, FIRST, U, LOOPS, LAST)

        @block.vector
        def _(dve):
            for s in (hb_ready, y_ready):
                dve.sem_inc(s, 2)

            def step(i, r):
                up, yy = Block(i, r, 1), Block(i, r, 3)
                if up.live:
                    e = dve.value_load(c.block_expert[0:1, bass.ds(up.t, 1)], min_val=0, max_val=7)
                    dve.wait_ge(h_psum, done(up.t))
                    dve.wait_ge(gelu_ready, free(up.t))
                    nc.vector.tensor_tensor(hb[:, up.b, :], h_bank[up.b],
                                            w["b1"][:, bass.ds(e, 1), :].rearrange("p a f -> p (a f)"),
                                            ALU.add).then_inc(hb_ready, 1)
                if yy.live:
                    e = dve.value_load(c.block_expert[0:1, bass.ds(yy.t, 1)], min_val=0, max_val=7)
                    dve.wait_ge(y_psum, done(yy.t))
                    dve.wait_ge(y_out[yy.b], r * 32 + (yy.n // 2) * 16 + 16)
                    nc.vector.tensor_tensor(y[:, yy.b, :], y_bank[yy.b][:, 0:P],
                                            w["b2"][:, bass.ds(e, 1), :].rearrange("p a f -> p (a f)"),
                                            ALU.add).then_inc(y_ready, 1)

            run_steps(dve, step, FIRST, U, LOOPS, LAST)
            for j in range(NT):
                if j % TB == 0:
                    dve.wait_ge(back[j // TB], 16 * TB)
                nc.vector.scalar_tensor_tensor(c.x[:, j, :], c.v[:, j, :], c.token_gate[:, j:j + 1], c.x[:, j, :],
                                               ALU.mult, ALU.add).then_inc(added, 1)
                if j:
                    dve.wait_ge(added, j)
                    nc.vector.bn_stats(stats[:, j - 1, :], c.x[:, j - 1, :]).then_inc(stats_ready, 1)
            dve.wait_ge(added, NT)
            nc.vector.bn_stats(stats[:, NT - 1, :], c.x[:, NT - 1, :]).then_inc(stats_ready, 1)
            dve.wait_ge(stats_ready, NT)
            for j in range(NT):
                nc.vector.bn_aggr(c.mv[:, j, :], stats[:, j, :])


def ffn0(nc, c, d):
    with ExitStack() as own:
        gate, wg, wu, ws, wd = scratch(nc, own, "w0", dict(
            gate=([P, 8], F32), wg=([P, 512], F32), wu=([P, 512], F32), ws=([P, P], F32), wd=([P, 5, P], F32)))
        w = dict(wg=wg, wu=wu, ws=ws, wd=wd)
        route(nc, c, 0, 8, 2, [(gate[:], d["f0_gate"]), (wg[:], d["f0_wg"]), (wu[:], d["f0_wu"]), (ws[:], d["f0_ws"]),
                               (wd[:, 0:4, :], d["f0_wd"]), (wd[0:64, 4, :], d["f0_sd"])])
        gated_mlp(nc, c, 0, w)


def ffn1(nc, c, d):
    with ExitStack() as own:
        gate, w1, b1, w2, b2, c.slot, c.block_expert, c.token_gate = scratch(nc, own, "w1", dict(
            gate=([P, 8], F32), w1=([P, 8, 512], F32), b1=([P, 8, 512], F32), w2=([P, 8, 512], F32),
            b2=([P, 8, P], F32), slot=([P, NT], I32), blockexpert=([1, HALVES * BLOCKS], I32), tokengate=([P, NT], F32)))
        route(nc, c, 1, 8, 1, [(gate[:], d["f1_gate"]), (w1[:], d["f1_w1"]), (w2[:], d["f1_w2"]),
                               (b1[:], d["f1_b1"].partition_broadcast(P)), (b2[:], d["f1_b2"].partition_broadcast(P))])
        places(nc, c, d)
        routed_gelu(nc, c, dict(w1=w1, b1=b1, w2=w2, b2=b2))


def ffn2(nc, c, d):
    EX, TILES, LIMIT, ALPHA = 8, 2, 7.0, 1.702
    NTOK = TILES * P
    ln = semaphores(nc, c, "e2", "var root chain")
    (loaded, xn_ready, xt_psum, xt_ready, h_psum, gate_ready, up_clipped, up_ready, sig_ready, glu_ready,
     inter_ready, y_psum, yb_ready, acc_ready, cw_links, stats_ready) = semaphores(
        nc, c, "e2", "load xn xtp xt h gate upc up sig glu inter y yb acc cw bn")
    h_bank, y_bank, xt_bank = [c.bank[0], c.bank[1]], [c.bank[2], c.bank[3]], c.bank[4]
    with ExitStack() as own, nc.Block() as block:
        w_gu, w_down, b_gu, b_down, numbers, idx, weights = scratch(nc, own, "e2", dict(
            wgu=([P, EX, 2, P], F32), wdown=([P, EX, P], F32), bgu=([P, EX, 2], F32), bdown=([P, EX, P], F32),
            numbers=([P, EX], F32), idx=([P, TILES, 2], I32), weights=([P, TILES, EX], F32)))
        xn, xT, idx_f, picked, cw, gate, up, sig, glu, inter, yb, stats = scratch(nc, own, "e2", dict(
            xn=([P, TILES, P], F32), xT=([P, NTOK], F32), idxf=([P, TILES, 2], F32), picked=([P, TILES, 2, EX], F32),
            cw=([P, TILES, EX], F32), gate=([P, 2, NTOK], F32), up=([P, 2, NTOK], F32), sig=([P, 2, NTOK], F32),
            glu=([P, 2, NTOK], F32), inter=([P, 2, NTOK], F32), yb=([P, 2, TILES, P], F32), stats=([P, TILES, 6], F32)))
        loads = [(idx[:], d["f2_idx"]), (weights[:], d["f2_weights"]), (numbers[:], d["numbers"][:, 0:EX].partition_broadcast(P)),
                 (b_gu[:], d["f2_bgu"]), (w_gu[:], d["f2_wgu"]), (w_down[:], d["f2_down"]),
                 (b_down[:], d["f2_bdown"].partition_broadcast(P))]

        @block.sync
        def _(sp):
            for dst, src in loads:
                sp.dma_start(dst, src).then_inc(loaded, 16)

        @block.tensor
        def _(pe):
            pe.wait_ge(xn_ready, 1)
            for t in range(TILES):
                last = nc.tensor.transpose(xt_bank[:, t * P:(t + 1) * P], xn[:, t, :], c.ident[:])
            last.then_inc(xt_psum, 1)
            pe.wait_ge(xt_ready, 1)
            pe.wait_ge(loaded, 16 * len(loads))
            for i in range(EX + 1):
                if i < EX:
                    if i >= 2:
                        pe.wait_ge(gate_ready, i - 1)
                        pe.wait_ge(up_clipped, i - 1)
                    for k in range(2):
                        last = nc.tensor.matmul(h_bank[i % 2][:, k * NTOK:(k + 1) * NTOK], w_gu[:, i, k, :], xT[:],
                                                start=True, stop=True)
                    last.then_inc(h_psum, 1)
                if i >= 1:
                    e = i - 1
                    pe.wait_ge(inter_ready, e + 1)
                    if e >= 2:
                        pe.wait_ge(yb_ready, e - 1)
                    for t in range(TILES):
                        last = nc.tensor.matmul(y_bank[e % 2][:, t * P:(t + 1) * P],
                                                inter[:, e % 2, t * P:(t + 1) * P], w_down[:, e, :],
                                                start=True, stop=True)
                    last.then_inc(y_psum, 1)

        @block.scalar
        def _(act):
            ln_scalar(nc, c, act, ln)
            act.wait_ge(xt_psum, 1)
            nc.scalar.activation(xT[:], xt_bank[:, 0:NTOK], ACT.Identity).then_inc(xt_ready, 1)
            for e in range(EX):
                act.wait_ge(gate_ready, e + 1)
                if e >= 2:
                    act.wait_ge(glu_ready, e - 1)
                nc.scalar.activation(sig[:, e % 2, :], gate[:, e % 2, :], ACT.Sigmoid, scale=ALPHA).then_inc(sig_ready, 1)

        @block.vector
        def _(dve):
            ln_vector(nc, c, dve, ln)
            for t in range(TILES):
                last = nc.vector.tensor_scalar(xn[:, t, :], c.x[:, t, :], c.mv[:, t, 0:1], c.rstd[:, t:t + 1],
                                               ALU.subtract, ALU.mult)
            last.then_inc(xn_ready, 1)
            dve.wait_ge(loaded, 16 * len(loads))
            nc.vector.tensor_copy(idx_f[:], idx[:]).then_inc(cw_links, 1)
            dve.wait_ge(cw_links, 1)
            for k in range(2):
                last = nc.vector.tensor_tensor(picked[:, :, k, :], idx_f[:, :, k:k + 1].to_broadcast([P, TILES, EX]),
                                               numbers.rearrange("p (t e) -> p t e", t=1).to_broadcast([P, TILES, EX]),
                                               ALU.is_equal)
            last.then_inc(cw_links, 1)
            dve.wait_ge(cw_links, 2)
            nc.vector.tensor_tensor(cw[:], picked[:, :, 0, :], picked[:, :, 1, :], ALU.add).then_inc(cw_links, 1)
            dve.wait_ge(cw_links, 3)
            nc.vector.tensor_tensor(cw[:], cw[:], weights[:], ALU.mult).then_inc(cw_links, 1)
            dve.wait_ge(cw_links, 4)
            for i in range(EX + 2):
                b = i % 2
                if i < EX:
                    dve.wait_ge(h_psum, i + 1)
                    nc.vector.tensor_scalar(gate[:, b, :], h_bank[b][:, 0:NTOK], b_gu[:, i, 0:1], LIMIT,
                                            ALU.add, ALU.min).then_inc(gate_ready, 1)
                    nc.vector.tensor_scalar(up[:, b, :], h_bank[b][:, NTOK:2 * NTOK], b_gu[:, i, 1:2], LIMIT,
                                            ALU.add, ALU.min).then_inc(up_clipped, 1)
                e = i - 1
                if 0 <= e < EX:
                    dve.wait_ge(sig_ready, e + 1)
                    nc.vector.tensor_tensor(glu[:, e % 2, :], gate[:, e % 2, :], sig[:, e % 2, :],
                                            ALU.mult).then_inc(glu_ready, 1)
                if i < EX:
                    dve.wait_ge(up_clipped, i + 1)
                    nc.vector.tensor_scalar(up[:, b, :], up[:, b, :], -LIMIT, 1.0, ALU.max, ALU.add).then_inc(up_ready, 1)
                if 0 <= e < EX:
                    dve.wait_ge(glu_ready, e + 1)
                    dve.wait_ge(up_ready, e + 1)
                    if e >= 2:
                        dve.wait_ge(y_psum, e - 1)
                    nc.vector.tensor_tensor(inter[:, e % 2, :], glu[:, e % 2, :], up[:, e % 2, :],
                                            ALU.mult).then_inc(inter_ready, 1)
                e = i - 2
                if e >= 0:
                    dve.wait_ge(y_psum, e + 1)
                    nc.vector.tensor_tensor(yb[:, e % 2], y_bank[e % 2][:, 0:NTOK].rearrange("p (t f) -> p t f", t=TILES),
                                            b_down[:, e:e + 1, :].to_broadcast([P, TILES, P]), ALU.add).then_inc(yb_ready, 1)
                    dve.wait_ge(yb_ready, e + 1)
                    if e >= 1:
                        dve.wait_ge(acc_ready, e)
                    for t in range(TILES):
                        last = nc.vector.scalar_tensor_tensor(c.x[:, t, :], yb[:, e % 2, t, :], cw[:, t, e:e + 1],
                                                              c.x[:, t, :], ALU.mult, ALU.add)
                    last.then_inc(acc_ready, 1)
            dve.wait_ge(acc_ready, EX)
            for t in range(TILES):
                last = nc.vector.bn_stats(stats[:, t, :], c.x[:, t, :])
            last.then_inc(stats_ready, 1)
            dve.wait_ge(stats_ready, 1)
            for t in range(TILES):
                nc.vector.bn_aggr(c.mv[:, t, :], stats[:, t, :])


def dispatch(nc, c, d, weights):
    HALF = T // 2
    ROUNDS = CAPACITY // 8
    (loaded, cleared, sel_psum, searched, links, moved, twice, tok_psum, stored,
     weights_in) = semaphores(
        nc, c, "d3", "load clear sp search link moved twice tp stored win")
    with ExitStack() as own, nc.Block() as block:
        order, value = c.ctxT[:, 0:HALF], c.ctxT[:, HALF:T]
        slots, region, zeros, top, some, merged, best, empty, tok = scratch(nc, own, "d3", dict(
            slots=([64, CAPACITY], F32), region=([P, 1], F32),
            zeros=([P, ZERO_COLS], F32), top=([P, CAPACITY], F32), some=([64, CAPACITY], F32),
            merged=([64, 2, CAPACITY], F32), best=([64, CAPACITY], F32), empty=([64, CAPACITY], F32),
            tok=([64, 2, CAPACITY], F32)))
        loads = [(order, d["order"].partition_broadcast(P)), (slots[:], d["slots"].partition_broadcast(64)),
                 (region[:], d["region"])]
        flat = c.sum_rows.rearrange("(p n) f -> p (n f)", p=P)
        clears = [(flat[:, k:k + ZERO_COLS], zeros[:]) for k in range(0, flat.shape[1], ZERO_COLS)]
        clears.append((c.table[T:T + CAPACITY, :], zeros[0:CAPACITY, 0:P + 64]))

        @block.sync
        def _(sp):
            for dst, src in loads:
                sp.dma_start(dst, src).then_inc(loaded, 16)
            sp.dma_start(c.table[0:T, P:P + 64].rearrange("(j t) e -> t j e", t=P), c.gates[:]).then_inc(stored, 16)
            sp.wait_ge(cleared, 1)
            for dst, src in clears:
                sp.dma_start(dst, src).then_inc(stored, 16)
            for dst, src in weights:
                sp.dma_start(dst, src).then_inc(weights_in, 16)
            sp.wait_ge(searched, 2 * ROUNDS - 1)
            sp.dma_start(merged[:, 1, :], top[64:P, :]).then_inc(moved, 16)
            sp.wait_ge(stored, 16 * (len(clears) + 1))
            sp.wait_ge(weights_in, 16 * len(weights))

        @block.gpsimd
        def _(pool):
            nc.gpsimd.memset(zeros[:], 0.0).then_inc(cleared, 1)

        @block.tensor
        def _(pe):
            for k in range(4):
                for j in range(4):
                    last = nc.tensor.transpose(c.bank[k][:, j * P:(j + 1) * P],
                                               c.chosen[:, 4 * k + j].rearrange("p h e -> p (h e)"), c.ident[:])
                last.then_inc(sel_psum, 1)
            pe.wait_ge(twice, 1)
            nc.tensor.transpose(c.bank[4][:, 0:64], tok.rearrange("e k s -> e (k s)"), c.ident[0:64, 0:64]).then_inc(tok_psum, 1)

        @block.vector
        def _(dve):
            count = [0]

            def link(instruction):
                instruction.then_inc(links, 1)
                count[0] += 1
                dve.wait_ge(links, count[0])

            dve.wait_ge(loaded, 16 * len(loads))
            for k in range(4):
                dve.wait_ge(sel_psum, k + 1)
                part = slice(k * GN, (k + 1) * GN)
                last = nc.vector.tensor_tensor(value[:, part], c.bank[k], order[:, part], ALU.mult)
            link(last)
            for k in range(ROUNDS):
                found = top[:, 8 * k:8 * k + 8]
                nc.vector.max(found, value).then_inc(searched, 1)
                dve.wait_ge(searched, 2 * k + 1)
                if k < ROUNDS - 1:
                    nc.vector.match_replace(value, found, value, 0.0).then_inc(searched, 1)
                    dve.wait_ge(searched, 2 * k + 2)
            link(nc.vector.tensor_scalar(some[:], top[0:64, :], 0.0, float(HALF), ALU.is_gt, ALU.mult))
            link(nc.vector.tensor_tensor(merged[:, 0, :], some[:], top[0:64, :], ALU.add))
            dve.wait_ge(moved, 16)
            both = merged.rearrange("e h s -> e (h s)")
            for k in range(ROUNDS):
                link(nc.vector.max(best[:, 8 * k:8 * k + 8], both))
                if k < ROUNDS - 1:
                    link(nc.vector.match_replace(both, best[:, 8 * k:8 * k + 8], both, 0.0))
            link(nc.vector.scalar_tensor_tensor(empty[:], best[:], 0.0, slots[:], ALU.is_equal, ALU.mult))
            link(nc.vector.tensor_scalar(best[:], best[:], -1.0, float(T), ALU.mult, ALU.add))
            for k in range(2):
                nc.vector.tensor_tensor(tok[:, k, :], best[:], empty[:], ALU.add).then_inc(links, 1)
            dve.wait_ge(links, count[0] + 2)
            dve.sem_inc(twice, 1)
            dve.wait_ge(tok_psum, 1)
            for k in range(2):
                half = slice(k * 64, k * 64 + 64)
                mine = c.bank[4][half, 0:64].rearrange("p (n k) -> p n k", k=2)[:, :, k]
                nc.vector.tensor_copy(c.idx[half, :], mine)
                nc.vector.tensor_scalar(c.sum_idx[half, :], mine, region[half, 0:1], None, ALU.add)


def experts(nc, c, w):
    PAIRS, XB, AHEAD, I = 32, 4, 3, 64
    (xt_psum, xt_ready, up_psum, silu_ready, h_ready, ht_psum, ht_ready, y_psum, ys_ready,
     cleared) = semaphores(nc, c, "x3", "xtp xt up silu h htp ht y ys clear")
    scattered, = gpsimd_dma_semaphores(nc, c, "x3", "scat")
    gathered = gpsimd_dma_semaphores(nc, c, "x3", "in0 in1 in2 in3")
    xt_bank, up_bank, ht_bank, y_bank = ([c.bank[n], c.bank[n + 1]] for n in (0, 2, 4, 6))
    halves = [slice(0, 64), slice(64, P)]
    FIRST, U, LOOPS, LAST = 8, 4, 6, PAIRS + 3

    with ExitStack() as own, nc.Block() as block:
        rows, xT, silu, h, hT, ys = scratch(nc, own, "x3", dict(
            rows=([P, XB, P + 64], F32), xT=([P, 2, P], F32),
            silu=([P, 2, 2, I], F32), h=([P, 2, P], F32), hT=([P, 2, P], F32), ys=([P, 2, P], F32)))

        def Pair(i, r, lag=0):
            return Item(i - lag, r, U, PAIRS)

        @block.gpsimd
        def _(pool):
            nc.gpsimd.memset(h[:], 0.0).then_inc(cleared, 1)
            for n in range(PAIRS + AHEAD):
                if n < PAIRS:
                    if n >= XB:
                        pool.wait_ge(ys_ready, free(n))
                    nc.gpsimd.indirect_dma_start(rows[:, n % XB, :], None, c.table[:, :],
                                                 bass.IndirectOffsetOnAxis(ap=c.idx[:, n:n + 1], axis=0)
                                                 ).then_inc(gathered[n % XB], 16)
                y = n - AHEAD
                if y >= 0:
                    pool.wait_ge(ys_ready, done(y, XB))
                    if y >= 1:
                        pool.wait_ge(scattered, 16 * y)
                    nc.gpsimd.indirect_dma_start(c.sum_rows[:, :],
                                                 bass.IndirectOffsetOnAxis(ap=c.sum_idx[:, y:y + 1], axis=0),
                                                 ys[:, y % 2, :], None, compute_op=ALU.add).then_inc(scattered, 16)
            pool.wait_ge(scattered, 16 * PAIRS)

        @block.tensor
        def _(pe):
            for s in (xt_psum, up_psum, ht_psum, y_psum):
                pe.sem_inc(s, 2)

            def step(i, r):
                x, up, ht, y = (Pair(i, r, lag) for lag in range(4))
                if x.live:
                    pe.wait_ge(gathered[x.n % XB], r * 16 + (16 * (x.n // XB) + 16))
                    pe.wait_ge(xt_ready, free(x.t))
                    nc.tensor.transpose(xt_bank[x.b][:, 0:P], rows[:, x.n % XB, 0:P], c.ident[:]).then_inc(xt_psum, 1)
                if up.live:
                    pe.wait_ge(xt_ready, done(up.t))
                    pe.wait_ge(h_ready, free(up.t))
                    nc.tensor.matmul(up_bank[up.b][:, 0:2 * P], xT[:, up.b, :],
                                     w["up"][:, bass.ds(up.items(2), 2), :].rearrange("d a f -> d (a f)"),
                                     start=True, stop=True).then_inc(up_psum, 1)
                if ht.live:
                    pe.wait_ge(h_ready, done(ht.t))
                    pe.wait_ge(ht_ready, free(ht.t))
                    nc.tensor.transpose(ht_bank[ht.b][:, 0:P], h[:, ht.b, :], c.ident[:]).then_inc(ht_psum, 1)
                if y.live:
                    pe.wait_ge(ht_ready, done(y.t))
                    pe.wait_ge(ys_ready, y.items(1, 3))
                    nc.tensor.matmul(y_bank[y.b][:, 0:P], hT[:, y.b, :],
                                     w["down"][:, bass.ds(y.t, 1), :].rearrange("d a f -> d (a f)"),
                                     start=True, stop=True).then_inc(y_psum, 1)

            run_steps(pe, step, FIRST, U, LOOPS, LAST)

        @block.scalar
        def _(act):
            for s in (xt_ready, silu_ready, ht_ready):
                act.sem_inc(s, 2)

            def step(i, r):
                x, up, ht = (Pair(i, r, lag) for lag in range(3))
                if x.live:
                    act.wait_ge(xt_psum, done(x.t))
                    act.wait_ge(up_psum, free(x.t))
                    nc.scalar.activation(xT[:, x.b, :], xt_bank[x.b][:, 0:P], ACT.Copy).then_inc(xt_ready, 1)
                if up.live:
                    act.wait_ge(up_psum, done(up.t))
                    act.wait_ge(h_ready, free(up.t))
                    nc.scalar.activation(silu[:, up.b], up_bank[up.b][:, 0:2 * P].rearrange("p (k f) -> p k f", k=2)[:, :, 0:I],
                                         ACT.Silu).then_inc(silu_ready, 1)
                if ht.live:
                    act.wait_ge(ht_psum, done(ht.t))
                    act.wait_ge(y_psum, free(ht.t))
                    nc.scalar.activation(hT[:, ht.b, :], ht_bank[ht.b][:, 0:P], ACT.Copy).then_inc(ht_ready, 1)

            run_steps(act, step, FIRST, U, LOOPS, LAST)

        @block.vector
        def _(dve):
            dve.sem_inc(h_ready, 2)
            dve.sem_inc(ys_ready, XB)

            def step(i, r):
                up, y = Pair(i, r, 1), Pair(i, r, 3)
                if up.live:
                    if up.n == 0 and isinstance(r, int):
                        dve.wait_ge(cleared, 1)
                    dve.wait_ge(silu_ready, done(up.t))
                    dve.wait_ge(ht_psum, free(up.t))
                    for k in range(2):
                        last = nc.vector.tensor_tensor(h[halves[k], up.b, k * I:(k + 1) * I], silu[halves[k], up.b, k, :],
                                                       up_bank[up.b][halves[k], k * P + I:(k + 1) * P], ALU.mult)
                    last.then_inc(h_ready, 1)
                if y.live:
                    dve.wait_ge(y_psum, done(y.t))
                    if y.n >= 2:
                        dve.wait_ge(scattered, y.items(16) - 16)
                    for k in range(2):
                        gate = rows[halves[k], y.n % XB, bass.ds(y.items(2, P + k), 1)]
                        last = nc.vector.tensor_scalar(ys[halves[k], y.b, :], y_bank[y.b][halves[k], 0:P], gate, None,
                                                       ALU.mult)
                    last.then_inc(ys_ready, 1)

            run_steps(dve, step, FIRST, U, LOOPS, LAST)


def ffn3(nc, c, d):
    with ExitStack() as own:
        gate, sgu, wd, chosen = scratch(nc, own, "w3", dict(
            gate=([P, 65], F32), sgu=([P, 512], F32), wd=([P, 2, P], F32), chosen=([P, NT // 2, 2, 64], F32)))
        c.chosen = chosen
        c.idx, c.sum_idx = scratch(nc, own, "w3", dict(idx=([P, 32], I32), sumidx=([P, 32], I32)))
        route(nc, c, 3, 64, 8, [(gate[:], d["f3_gate"]), (sgu[:], d["f3_sgu"]), (wd[:], d["f3_sdown"])])
        with ExitStack() as inner:
            up, down = scratch(nc, inner, "w3", dict(up=([P, 64, P], F32), down=([P, 32, P], F32)))
            dispatch(nc, c, d, [(up[:], d["f3_up"]), (down[:], d["f3_down"])])
            experts(nc, c, dict(up=up, down=down))
        gated_mlp(nc, c, 3, dict(sgu=sgu, wd=wd))


def finish(nc, c, out):
    PARTS = 4
    loaded, added, stored = (semaphores(nc, c, "end", " ".join(f"{k}{n}" for n in range(PARTS)))
                             for k in ("load", "add", "store"))
    with ExitStack() as own, nc.Block() as block:
        sums, = scratch(nc, own, "end", dict(sums=([P, 2, NT, P], F32)))

        def part(n):
            return slice(n * NT // PARTS, (n + 1) * NT // PARTS)

        @block.sync
        def _(sp):
            for n in range(PARTS):
                for k in range(2):
                    sp.dma_start(sums[:, k, part(n), :],
                                 c.sums[k][0:T, :].rearrange("(j t) f -> t j f", t=P)[:, part(n), :]).then_inc(loaded[n], 16)
            for n in range(PARTS):
                sp.wait_ge(added[n], 2)
                sp.dma_start(out.rearrange("b t f -> t b f")[:, part(n), :], c.x[:, part(n), :]).then_inc(stored[n], 16)
            for n in range(PARTS):
                sp.wait_ge(stored[n], 16)

        @block.vector
        def _(dve):
            for n in range(PARTS):
                dve.wait_ge(loaded[n], 32)
                for k in range(2):
                    if k:
                        dve.wait_ge(added[n], 1)
                    nc.vector.tensor_tensor(c.x[:, part(n), :], c.x[:, part(n), :], sums[:, k, part(n), :],
                                            ALU.add).then_inc(added[n], 1)


def setup(nc, c, d):
    loaded, made, cleared, stats, masks, zeroed, rows_out = semaphores(
        nc, c, "su", "load made clear stats mask zero rows")
    loads = [(c.ident[:], d["ident"]), (c.wa[:], d["wa"]), (c.wrot[:], d["wrot"]), (c.bcol[:], d["bcol"]),
             (c.rope[:], d["rope"]), (c.ctxT[:], d["ctxT"]),
             (c.before[:], d["before"].partition_broadcast(P)),
             (c.brow[:], d["brow"].partition_broadcast(P)), (c.causal[:], d["causal"]), (c.umask[:], d["umask"])]
    xs = [semaphores(nc, c, "su", f"x{g}")[0] for g in range(4)]
    with nc.Block() as block:
        @block.sync
        def _(sp):
            for g in range(4):
                part = slice(g * NT // 4, (g + 1) * NT // 4)
                sp.dma_start(c.x[:, part, :], d["x"].rearrange("b t f -> t b f")[:, part, :]).then_inc(xs[g], 16)
            for dst, src in loads:
                sp.dma_start(dst, src).then_inc(loaded, 16)
            sp.wait_ge(zeroed, 2)
            sp.dma_start(c.q_stack_dram[SR:SR + 2].rearrange("r h (j t) -> r (h j) t", t=P),
                         c.zeros[:].to_broadcast([2, H * NT, P])).then_inc(rows_out, 16)
            for table in c.slots_x:
                sp.dma_start(table.rearrange("(p n) f -> p n f", p=P), c.zero_row[:].to_broadcast([P, BLOCKS, P])
                             ).then_inc(rows_out, 16)
            sp.wait_ge(rows_out, 16 * (1 + HALVES))

        @block.vector
        def _(dve):
            nc.vector.memset(c.zero_row[:], 0.0).then_inc(zeroed, 1)
            dve.wait_ge(loaded, 16 * len(loads))
            nc.vector.tensor_copy(c.identb[:], c.ident[:]).then_inc(made, 1)
            for kind, src in enumerate((c.causal, c.umask)):
                for side in range(2):
                    nc.vector.tensor_scalar(c.mask[:, kind, side], src[:, side:side + 1, :].to_broadcast([P, 4, P]),
                                            NEG, None, ALU.mult).then_inc(masks, 1)
            for t in range(NT):
                if t % (NT // 4) == 0:
                    dve.wait_ge(xs[t // (NT // 4)], 16)
                nc.vector.bn_stats(c.stats0[:, t, :], c.x[:, t, :]).then_inc(stats, 1)
            for t in range(NT):
                dve.wait_ge(stats, t + 1)
                nc.vector.bn_aggr(c.mv[:, t, :], c.stats0[:, t, :])

        @block.gpsimd
        def _(pool):
            nc.gpsimd.memset(c.qs[:], 0.0)
            nc.gpsimd.memset(c.ks[:], 0.0).then_inc(cleared, 1)
            nc.gpsimd.memset(c.vx[:], 0.0).then_inc(cleared, 1)
            nc.gpsimd.memset(c.zeros[:], 0.0).then_inc(zeroed, 1)
            pool.wait_ge(cleared, 2)
            nc.gpsimd.memset(c.ks[32:64], 1.0).then_inc(cleared, 1)
            pool.wait_ge(cleared, 3)
            for odd in range(2):
                nc.gpsimd.memset(c.vx.rearrange("p b (g o) e -> p b g o e", o=2)[
                    :, :, :, odd, 16 * odd + HD:16 * odd + 2 * HD], 1.0)


def build(nc, d, out, stages=range(8)):
    with ExitStack() as ctx:
        c = Core()
        c.program = ctx
        c.next_gpsimd_semaphore = FIRST_GPSIMD_SEMAPHORE

        def sb(name, shape, dt=F32):
            return ctx.enter_context(nc.sbuf_tensor(name, shape, dt))

        c.psum = ctx.enter_context(nc.psum_tensor("psum", [P, 8, 512], F32))
        c.bank = [c.psum[:, n, :] for n in range(8)]
        c.x = sb("x_sb", [P, NT, P])
        c.ctxT = sb("ctx_T", [P, T])
        c.v = sb("v_sb", [P, NT, P])
        c.wa = sb("w_attn", [P, 4, 4, P])
        c.wrot = sb("w_rot", [P, 2, P])
        c.bcol = sb("b_cols", [P, 10])
        c.brow = sb("b_rows", [P, 8, P])
        c.rope = sb("rope_sb", [P, 2, P])
        c.ident = sb("ident_sb", [P, P])
        c.identb = sb("ident_bf", [P, P], BF16)
        c.causal = sb("causal_sb", [P, 2, P])
        c.umask = sb("umask_sb", [P, 2, P], U8)
        c.mask = sb("mask_sb", [P, 2, 2, 4, P], BF16)
        c.mv = sb("mean_var", [P, NT, 2])
        c.stats0 = sb("stats0", [P, NT, 6])
        c.stats = sb("stats", [P, 2, 6])
        c.mvs = sb("mean_var_new", [P, 2, 2])
        c.xs = sb("x_new", [P, 2, P])
        c.veps, c.root, c.rstd0, c.newt, c.rstd = (sb("ln_" + n, [P, NT]) for n in
                                                   ("veps", "root", "rstd0", "newt", "rstd"))
        c.gates = sb("gates", [P, NT, 64])
        c.before = sb("before_sb", [P, 1, 64])
        c.shared_gate = sb("shared_gate", [P, NT])
        c.xT = c.v.rearrange("p t f -> p (t f)")
        c.q_stack_dram = nc.dram_tensor("q_parts", [SR + 2, H, T], BF16, kind="Internal").ap()
        c.k_stack_dram = nc.dram_tensor("k_parts", [3 * HD, H, T], BF16, kind="Internal").ap()
        c.q_dram = c.q_stack_dram[0:SR].rearrange("(c d) h t -> (d h) c t", d=HD)
        c.k_dram = c.k_stack_dram.rearrange("(c d) h t -> (d h) c t", d=HD)
        c.STACK_INCS = 16 * (1 + len(K_RUNS))

        c.qs = sb("q_stack", [P, STACKS, H, 2 * P], BF16)
        c.ks = sb("k_stack", [P, STACKS, H, 2 * P], BF16)
        c.zeros = sb("zeros", [2, 1, P], BF16)
        c.zero_row = sb("zero_row", [P, 1, P])
        c.vx = sb("v_x", [P, 2, H, 32])
        c.table = nc.dram_tensor("table", [T + CAPACITY, P + 64], F32, kind="Internal").ap()
        c.slots_x, c.slots_y = ([nc.dram_tensor(f"{name}{half}", [BLOCKS * P, P], F32, kind="Internal").ap()
                                 for half in range(HALVES)] for name in ("slots_x", "slots_y"))
        c.sum_rows = nc.dram_tensor("sum_rows", [2 * (T + CAPACITY), P], F32, kind="Internal").ap()
        c.sums = [c.sum_rows[k * (T + CAPACITY):(k + 1) * (T + CAPACITY), :] for k in range(2)]
        for layer in range(4):
            with ExitStack() as sems:
                c.ctx = sems
                c.next_semaphore = FIRST_SEMAPHORE
                if layer == 0:
                    setup(nc, c, d)
                if 2 * layer in stages:
                    project(nc, c, layer)
                    attend(nc, c, layer)
                if 2 * layer + 1 in stages:
                    (ffn0, ffn1, ffn2, ffn3)[layer](nc, c, d)
                if layer == 3:
                    finish(nc, c, out)
                else:
                    zero_semaphores(nc, c)


def host_arrays(i):
    f = {}
    at = lambda n, k: np.asarray(i[f"L{n}_xattn_{k if n != 2 else k.lower()}"])
    f["x"] = np.asarray(i["x"])
    f["ctxT"] = np.ascontiguousarray(np.asarray(i["ctx_1024"]).reshape(T, P).T)
    order = np.arange(P).reshape(H, HD).T.reshape(P)
    f["wa"] = np.ascontiguousarray(np.stack([np.stack([at(n, k).T[:, order] for k in ("Wq", "Wk")]
                                                      + [at(n, k).T for k in ("Wv", "Wo")])
                                             for n in range(4)]).transpose(2, 0, 1, 3))
    swap = np.arange(P).reshape(H, 2, HD // 2)[:, ::-1].reshape(P)[order]
    f["wrot"] = np.ascontiguousarray(np.stack([at(3, k).T[:, swap] for k in ("Wq", "Wk")], 1))
    f["bcol"] = np.ascontiguousarray(np.stack([at(n, k)[order] for n in range(4) for k in ("bq", "bk")]
                                              + [at(3, k)[swap] for k in ("bq", "bk")], 1))
    f["brow"] = np.ascontiguousarray(np.stack([at(n, k) for n in range(4) for k in ("bv", "bo")]))
    angle = np.arange(P)[:, None] * (1.0 / 10000.0 ** (np.arange(0, HD, 2) / HD))[None, :]
    cos, sin = (np.tile(fn(angle), (1, 2 * H)).T for fn in (np.cos, np.sin))
    sign = np.where(np.arange(P) % HD < HD // 2, -1.0, 1.0)[:, None]
    f["rope"] = np.ascontiguousarray(np.stack([cos, sin * sign], 1)[order].astype(np.float32))
    f["ident"] = np.eye(P, dtype=np.float32)
    later = (np.arange(P)[None, :] > np.arange(P)[:, None]).astype(np.float32)
    f["causal"] = np.ascontiguousarray(np.stack([later, later.T], 1))
    f["before"] = np.ascontiguousarray((np.arange(8)[None, :] < np.arange(8)[:, None]).astype(np.float32).reshape(1, 64))
    up = {k: np.asarray(i[f"L0_ffn_{k}"]) for k in ("gate_w", "wg", "wu", "wd", "sg", "su", "sd")}
    f["f0_gate"] = np.ascontiguousarray(up["gate_w"].T)
    f["f0_wg"], f["f0_wu"] = (np.ascontiguousarray(up[k].reshape(512, P).T) for k in ("wg", "wu"))
    f["f0_ws"] = np.ascontiguousarray(np.concatenate([up["sg"], up["su"]]).T)
    f["f0_wd"] = np.ascontiguousarray(up["wd"].transpose(0, 2, 1).reshape(4, P, P).transpose(1, 0, 2))
    f["f0_sd"] = np.ascontiguousarray(up["sd"].T)
    up = {k: np.asarray(i[f"L1_ffn_{k}"]) for k in ("gate_w", "w1", "b1", "w2", "b2")}
    f["f1_gate"] = up["gate_w"]
    f["f1_w1"] = np.ascontiguousarray(up["w1"].transpose(1, 0, 2))
    f["f1_b1"] = up["b1"]
    f["f1_w2"] = np.ascontiguousarray(up["w2"].reshape(8, 4, P, P).transpose(2, 0, 1, 3).reshape(P, 8, 512))
    f["f1_b2"] = up["b2"]
    up = {k: np.asarray(i[f"L2_ffn_{k}"]) for k in ("router_indices", "routing_weights", "gate_up_proj",
                                                    "gate_up_proj_bias", "down_proj", "down_proj_bias")}
    f["f2_idx"], f["f2_weights"] = (np.ascontiguousarray(up[k].reshape(2, P, -1).transpose(1, 0, 2))
                                    for k in ("router_indices", "routing_weights"))
    f["numbers"] = np.arange(BLOCKS, dtype=np.float32).reshape(1, BLOCKS)
    f["f2_wgu"] = np.ascontiguousarray(up["gate_up_proj"].reshape(8, P, P, 2).transpose(1, 0, 3, 2))
    f["f2_bgu"] = np.ascontiguousarray(up["gate_up_proj_bias"].reshape(8, P, 2).transpose(1, 0, 2))
    f["f2_down"] = np.ascontiguousarray(up["down_proj"].transpose(1, 0, 2))
    f["f2_bdown"] = up["down_proj_bias"]
    up = {k: np.asarray(i[f"L3_ffn_{k}"]) for k in ("gate_w", "shared_gate_w", "shared_gate_up_w", "shared_down_w",
                                                    "expert_gate_up_w", "expert_down_w")}
    f["f3_gate"] = np.ascontiguousarray(np.concatenate([up["gate_w"], up["shared_gate_w"]], 1))
    f["f3_up"] = np.ascontiguousarray(up["expert_gate_up_w"].transpose(1, 0, 2))
    f["f3_down"] = np.ascontiguousarray(up["expert_down_w"].reshape(32, P, P).transpose(1, 0, 2))
    f["f3_sgu"] = up["shared_gate_up_w"]
    f["f3_sdown"] = np.ascontiguousarray(up["shared_down_w"].reshape(2, P, P).transpose(1, 0, 2))
    f["order"] = (T // 2 - np.arange(T // 2, dtype=np.float32)).reshape(1, -1)
    f["slots"] = np.arange(CAPACITY, dtype=np.float32).reshape(1, -1)
    f["region"] = np.repeat(np.array([0, T + CAPACITY], np.float32), 64).reshape(P, 1)
    mask = np.asarray(i["mask_SxS2_bk1"]).view(np.uint8)
    f["umask"] = np.ascontiguousarray(np.stack([mask, mask.T], 1))
    return f


def kernel(**inputs):
    import numpy as _np
    import concourse.bacc as _bacc
    from concourse import mybir as _mybir
    from concourse.bass_utils import run_bass_kernel_spmd as _run

    nc = _bacc.Bacc("TRN2", target_bir_lowering=False, num_devices=1)
    arrays = {f"in_{k}": _np.ascontiguousarray(a) for k, a in host_arrays(inputs).items()}
    dram = {k[3:]: nc.dram_tensor(k, a.shape, _mybir.dt.from_np(a.dtype), kind="ExternalInput").ap()
            for k, a in arrays.items()}
    out = nc.dram_tensor("out_0_dram", (NT, P, P), F32, kind="ExternalOutput").ap()
    build(nc, dram, out)
    r = _run(nc, [arrays], core_ids=[0])
    return r.results[0]["out_0_dram"]
```

```python
from contextlib import ExitStack

import numpy as np

import concourse.bass as bass
from concourse import mybir

F32 = mybir.dt.float32
BF16 = mybir.dt.bfloat16
I32 = mybir.dt.int32
U8 = mybir.dt.uint8
ALU = mybir.AluOpType
ACT = mybir.ActivationFunctionType
AX = mybir.AxisListType.X

P = 128
NT = 32
T = NT * P
GT = 4
GN = GT * P
NG = NT // GT
H, HD = 16, 8
TERMS = 6
SR = TERMS * HD
EPS = 1e-5
NEG = -float(2 ** 60)
STACKS = 3
FIRST_SEMAPHORE = 100
FIRST_GPSIMD_SEMAPHORE = 230
HALVES = 2
BLOCKS = NT // HALVES + 8
PAIR_LAG = 3
CAPACITY = 64
Q_PARTS = (0, 0, 0, 1, 1, 2)
K_RUNS = (3, 2, 1)


class Core:
    pass


def semaphores(nc, c, prefix, names):
    taken = [c.ctx.enter_context(nc.semaphore(f"{prefix}_{n}", num=c.next_semaphore + k))
             for k, n in enumerate(names.split())]
    c.next_semaphore += len(taken)
    return taken


def gpsimd_dma_semaphores(nc, c, prefix, names):
    taken = [c.program.enter_context(nc.semaphore(f"{prefix}_{n}", num=c.next_gpsimd_semaphore + k))
             for k, n in enumerate(names.split())]
    c.next_gpsimd_semaphore += len(taken)
    return taken


def zero_semaphores(nc, c):
    with nc.Block() as block:
        @block.gpsimd
        def _(pool):
            pool.sem_clear(range(FIRST_SEMAPHORE, c.next_semaphore))


def done(n, credit=2):
    return n + (1 + credit)


def free(n):
    return n + 1


def ln_vector(nc, c, dve, sems):
    var_ready, root_ready, chain = sems
    nc.vector.tensor_scalar(c.veps[:], c.mv[:, :, 1], EPS, None, ALU.add).then_inc(var_ready, 1)
    dve.wait_ge(root_ready, 1)
    nc.vector.reciprocal(c.rstd0[:], c.root[:]).then_inc(chain, 1)
    dve.wait_ge(chain, 1)
    nc.vector.tensor_tensor(c.newt[:], c.rstd0[:], c.rstd0[:], ALU.mult).then_inc(chain, 1)
    dve.wait_ge(chain, 2)
    nc.vector.tensor_tensor(c.newt[:], c.newt[:], c.veps[:], ALU.mult).then_inc(chain, 1)
    dve.wait_ge(chain, 3)
    nc.vector.tensor_scalar(c.newt[:], c.newt[:], -0.5, 1.5, ALU.mult, ALU.add).then_inc(chain, 1)
    dve.wait_ge(chain, 4)
    nc.vector.tensor_tensor(c.rstd[:], c.newt[:], c.rstd0[:], ALU.mult).then_inc(chain, 1)
    dve.wait_ge(chain, 5)


def load_table(nc, c, function):
    k, c.tables_loaded = c.tables_loaded, c.tables_loaded + 1
    nc.scalar.activation(c.table_out[:, k:k + 1], c.zero_row[:, 0, 0:1], function)


def ln_scalar(nc, c, act, sems):
    var_ready, root_ready, _ = sems
    act.wait_ge(var_ready, 1)
    nc.scalar.activation(c.root[:], c.veps[:], ACT.Sqrt).then_inc(root_ready, 1)


def scratch(nc, ctx, prefix, shapes):
    for name, (shape, dt) in shapes.items():
        yield ctx.enter_context(nc.sbuf_tensor(f"{prefix}_{name}", shape, dt))


def run_steps(engine, step, first, unroll, loops, last):
    for i in range(first):
        step(i, 0)
    with engine.Fori(0, loops) as r:
        for j in range(unroll):
            step(first + j, r)
    for i in range(first + unroll * loops, last):
        step(i, 0)


class Item:

    def __init__(self, n, r, unroll, total=NT):
        self.n, self.r, self.unroll = n, r, unroll
        self.live = not isinstance(r, int) or 0 <= n < total
        self.b = n % 2
        self.stack = (n // 2) % STACKS
        self.half = slice((n % 2) * P, (n % 2) * P + P)

    def items(self, k, m=0):
        return self.r * (self.unroll * k) + (self.n * k + m)

    @property
    def t(self):
        return self.items(1)

    @property
    def turn(self):
        return self.r * (self.unroll // 2) + self.n // 2

    @property
    def fill(self):
        return self.r * (self.unroll // 2 // STACKS) + self.n // 2 // STACKS


def project(nc, c, layer, own):
    rope = layer == 3

    pre = f"p{layer}"
    ln = semaphores(nc, c, pre, "var root chain")
    (xn_ready, xt_psum, xt_ready, q_psum, k_psum, v_psum, ctx_ready, v_ready,
     hi_ready, res_ready, mid_ready, lo_ready, turned, roped) = semaphores(
        nc, c, pre, "xn xtp xt q k v ctx vdone hi res mid lo turned roped")
    hi_out, rest_out = semaphores(nc, c, pre, "hiout0 hiout1"), semaphores(nc, c, pre, "out0 out1")
    c.parts_out = [(s, 2 * 16) for s in hi_out] + [(s, 3 * 16) for s in rest_out]
    c.stacked = semaphores(nc, c, pre, "stack0 stack1 stack2")
    wq, wk, wv = (c.wa[:, layer, n, :] for n in range(3))
    bias = [c.bcol[:, 2 * layer + n:2 * layer + n + 1] for n in range(2)]
    xt_bank = [c.bank[n] for n in (0, 1)]
    qk_bank = [[c.bank[2], c.bank[3]], [c.bank[4], c.bank[5]]]
    v_bank = [c.bank[n] for n in (6, 7)]

    with nc.Block() as block:
        c.xn, c.xnT, c.ctxg, c.parts, c.resid = scratch(nc, own, pre, dict(
            xn=([P, 2, GT, P], F32), xnT=([P, 2, GN], F32), ctxg=([P, 2, GN], F32),
            parts=([P, 2, 2, 3, GN], BF16), resid=([P, 2, 2, GN], F32)))
        if rope:
            c.roped, c.rot = scratch(nc, own, pre, dict(roped=([P, 2, 2, GN], F32), rot=([P, 2, GT, P], F32)))

        FIRST, U, LOOPS, LAST = 2, 2, 3, NG + 2

        def Group(i, r, lag):
            return Item(i - lag, r, U, NG)

        def columns(a):
            return bass.ds(a.items(GN), GN), bass.ds(a.items(GT), GT)

        @block.gpsimd
        def _(pool):
            pool.sem_inc(lo_ready, 4)

            def step(i, r):
                x, m = Group(i, r, 0), Group(i, r, 2)
                if m.live:
                    for n in range(2):
                        pool.wait_ge(mid_ready, done(m.items(2, n), 4))
                        nc.gpsimd.tensor_tensor(c.parts[:, m.b, n, 2, :], c.resid[:, m.b, n, :],
                                                c.parts[:, m.b, n, 1, :], ALU.subtract).then_inc(lo_ready, 1)
                if x.live:
                    pool.wait_ge(xn_ready, done(x.t))
                    tiles = columns(x)[1]
                    nc.gpsimd.tensor_tensor(
                        c.x[:, tiles, :], c.x[:, tiles, :],
                        c.brow[:, 2 * layer + 1:2 * layer + 2, :].to_broadcast([P, GT, P]), ALU.add)

            run_steps(pool, step, FIRST, U, LOOPS, LAST)

        @block.vector
        def _(dve):
            dve.sem_inc(xn_ready, 2)
            dve.sem_inc(v_ready, 2)
            dve.sem_inc(res_ready, 4)
            if rope:
                dve.sem_inc(roped, 2)
            ln_vector(nc, c, dve, ln)

            def step(i, r):
                x, m = Group(i, r, 0), Group(i, r, 2)
                if x.live:
                    dve.wait_ge(xt_psum, free(x.t))
                    for j in range(GT):
                        t = x.items(GT, j)
                        last = nc.vector.tensor_scalar(c.xn[:, x.b, j, :], c.x[:, t, :], c.mv[:, t, 0:1],
                                                       c.rstd[:, bass.ds(t, 1)], ALU.subtract, ALU.mult)
                    last.then_inc(xn_ready, 1)
                if not m.live:
                    return
                for n, psum in enumerate((q_psum, k_psum)):
                    k = m.items(2, n)
                    dve.wait_ge(psum, done(m.t))
                    if rope:
                        main, rot = (qk_bank[n][part].rearrange("p (j t) -> p j t", j=GT) for part in range(2))
                        cos = c.rope[:, 0:1, :].to_broadcast([P, GT, P])
                        sin = c.rope[:, 1:2, :].to_broadcast([P, GT, P])
                        dve.wait_ge(roped, k + 2)
                        nc.vector.scalar_tensor_tensor(c.rot[:, 0], main, bias[n], cos, ALU.add, ALU.mult)
                        nc.vector.scalar_tensor_tensor(c.rot[:, 1], rot, c.bcol[:, 8 + n:9 + n], sin,
                                                       ALU.add, ALU.mult).then_inc(turned, 1)
                        dve.wait_ge(turned, k + 1)
                        dve.wait_ge(hi_ready, free(k))
                        nc.vector.tensor_tensor(c.roped[:, m.b, n, :], c.rot[:, 0].rearrange("p j t -> p (j t)"),
                                                c.rot[:, 1].rearrange("p j t -> p (j t)"),
                                                ALU.add).then_inc(roped, 1)
                for n in range(2):
                    k = m.items(2, n)
                    dve.wait_ge(hi_ready, done(k, 4))
                    dve.wait_ge(lo_ready, free(k))
                    if rope:
                        nc.vector.tensor_tensor(c.resid[:, m.b, n, :], c.roped[:, m.b, n, :],
                                                c.parts[:, m.b, n, 0, :], ALU.subtract).then_inc(res_ready, 1)
                    else:
                        nc.vector.scalar_tensor_tensor(c.resid[:, m.b, n, :], qk_bank[n][m.b], bias[n],
                                                       c.parts[:, m.b, n, 0, :], ALU.add,
                                                       ALU.subtract).then_inc(res_ready, 1)
                dve.wait_ge(v_psum, done(m.t))
                nc.vector.tensor_tensor(
                    c.v[:, columns(m)[1], :], v_bank[m.b].rearrange("p (j f) -> p j f", j=GT),
                    c.brow[:, 2 * layer:2 * layer + 1, :].to_broadcast([P, GT, P]), ALU.add
                ).then_inc(v_ready, 1)

            run_steps(dve, step, FIRST, U, LOOPS, LAST)

        @block.scalar
        def _(act):
            act.sem_inc(xt_ready, 2)
            act.sem_inc(hi_ready, 4)
            act.sem_inc(mid_ready, 4)
            act.sem_inc(ctx_ready, 2)
            ln_scalar(nc, c, act, ln)
            if layer == 0:
                act.wait_ge(c.context_in, 16)

            def step(i, r):
                a, m = Group(i, r, 1), Group(i, r, 2)
                if m.live:
                    act.wait_ge(hi_out[m.b], m.turn * 32 + 32)
                for n, psum in enumerate((q_psum, k_psum)):
                    if m.live and rope:
                        act.wait_ge(roped, done(m.items(2, n)))
                        nc.scalar.activation(c.parts[:, m.b, n, 0, :], c.roped[:, m.b, n, :],
                                             ACT.Identity).then_inc(hi_ready, 1)
                    elif m.live:
                        act.wait_ge(psum, done(m.t))
                        nc.scalar.activation(c.parts[:, m.b, n, 0, :], qk_bank[n][m.b], ACT.Identity,
                                             bias=bias[n]).then_inc(hi_ready, 1)
                    if a.live and n == (0 if rope else 1):
                        act.wait_ge(xt_psum, done(a.t))
                        act.wait_ge(q_psum, free(a.t))
                        nc.scalar.activation(c.xnT[:, a.b, :], xt_bank[a.b], ACT.Identity).then_inc(xt_ready, 1)
                        act.wait_ge(v_psum, free(a.t))
                        nc.scalar.activation(c.ctxg[:, a.b, :], c.ctxT[:, columns(a)[0]], ACT.Identity).then_inc(ctx_ready, 1)
                if m.live:
                    act.wait_ge(rest_out[m.b], m.turn * 48 + 48)
                    for n in range(2):
                        act.wait_ge(res_ready, done(m.items(2, n), 4))
                        nc.scalar.activation(c.parts[:, m.b, n, 1, :], c.resid[:, m.b, n, :],
                                             ACT.Identity).then_inc(mid_ready, 1)

            run_steps(act, step, FIRST, U, LOOPS, LAST)
            load_table(nc, c, ACT.Exp)

        @block.tensor
        def _(pe):
            for s in (xt_psum, q_psum, k_psum, v_psum):
                pe.sem_inc(s, 2)
            if layer == 0:
                pe.wait_ge(c.context_in, 16)

            def step(i, r):
                a, m = Group(i, r, 1), Group(i, r, 2)
                if m.live:
                    pe.wait_ge(xt_ready, done(m.t))
                    keys = c.ctxT[:, columns(m)[0]]
                    for n, (psum, w, src) in enumerate(((q_psum, wq, c.xnT[:, m.b, :]), (k_psum, wk, keys))):
                        k = m.items(2, n)
                        if rope:
                            pe.wait_ge(roped, k + 1)
                            nc.tensor.matmul(qk_bank[n][0], w, src, start=True, stop=True)
                            nc.tensor.matmul(qk_bank[n][1], c.wrot[:, n, :], src, start=True,
                                             stop=True).then_inc(psum, 1)
                        else:
                            pe.wait_ge(res_ready, free(k))
                            nc.tensor.matmul(qk_bank[n][m.b], w, src, start=True, stop=True).then_inc(psum, 1)
                if a.live:
                    pe.wait_ge(xn_ready, done(a.t))
                    pe.wait_ge(xt_ready, free(a.t))
                    for j in range(GT):
                        last = nc.tensor.transpose(xt_bank[a.b][:, j * P:(j + 1) * P], c.xn[:, a.b, j, :], c.ident[:])
                    last.then_inc(xt_psum, 1)
                if m.live:
                    pe.wait_ge(ctx_ready, done(m.t))
                    pe.wait_ge(v_ready, free(m.t))
                    for j in range(GT):
                        last = nc.tensor.matmul(v_bank[m.b][:, j * P:(j + 1) * P], c.ctxg[:, m.b, j * P:(j + 1) * P],
                                                wv, start=True, stop=True)
                    last.then_inc(v_psum, 1)

            run_steps(pe, step, FIRST, U, LOOPS, LAST)

        @block.sync
        def _(sp):
            for out, group in c.parts_out:
                sp.sem_inc(out, group)

            def store(it, first):
                for b in range(2):
                    g = it * 2 + (first + b)
                    tokens = bass.ds(g * GN, GN)
                    for parts, outs, k_parts in (((0,), hi_out, slice(0, 1)), ((1, 2), rest_out, slice(1, 3))):
                        sp.wait_ge(hi_ready if outs is hi_out else lo_ready, done(g * 2 + 1, 4))
                        for part in parts:
                            copies = [n for n, p in enumerate(Q_PARTS) if p == part]
                            sp.dma_start(c.q_dram[:, copies[0]:copies[-1] + 1, tokens],
                                         c.parts[:, b, 0, part:part + 1, :].to_broadcast([P, len(copies), GN])
                                         ).then_inc(outs[b], 16)
                        sp.dma_start(c.k_dram[:, k_parts, tokens], c.parts[:, b, 1, k_parts, :]).then_inc(outs[b], 16)

            with sp.Fori(0, 2) as it:
                store(it, 0)
            for out, group in c.parts_out:
                sp.wait_ge(out, 2 * group)
            load_stacks(sp, c, 0, slice(0, 2 * P))
            with sp.Fori(0, NG // 2 - 2) as it:
                store(it, 4)


def load_stacks(sp, c, stack, tokens):
    sp.dma_start(c.qs[0:SR + 2, stack], c.q_stack_dram[:, :, tokens]).then_inc(c.stacked[stack], 16)
    start = 0
    for run in K_RUNS:
        sp.dma_start(c.ks[start:start + run * HD, stack],
                     c.k_stack_dram[0:run * HD, :, tokens]).then_inc(c.stacked[stack], 16)
        start += run * HD


def attend(nc, c, layer, own):
    scale = 1.0 if layer == 0 else float(1 / np.sqrt(np.float32(HD)))
    mask = {0: 0, 2: 1}.get(layer)

    (scores, maxed, m_ready, mt_psum, mt_ready, st_psum, exp_ready, vx_ready, pv_psum, pv_ready,
     n_psum, rd_ready, n_ready, at_psum, at_ready, y_psum, x_ready, stats_ready, hi_ready,
     mv_ready, x_stored) = semaphores(
        nc, c, f"a{layer}", "s max m mtp mt st exp vx pvp pv np rd n atp at y x bn hi mv xst")
    m_rows = semaphores(nc, c, f"a{layer}", "row0 row1")
    stacked = c.stacked
    wo = c.wa[:, layer, 3, :]
    s_bank = [c.bank[n].rearrange("p (h k) -> p h k", h=4) for n in (0, 1)]
    st_bank = [c.bank[n] for n in (2, 3)]
    pv = c.bank[4][:, 0:2 * P].rearrange("p (a q) -> p a q", a=2)
    back = c.bank[5][:, 0:2 * P]
    at = c.bank[6][:, 0:P]
    mt = c.bank[6][:, P:P + P // 2].bitcast(BF16)
    y = c.bank[7][:, 0:P]
    LAG = dict(S=0, M=1, ST=2, PV=3, BACK=4, NORM=5, AT=5, Y=6, X=7)
    FIRST, LOOPS, U = 8, 4, 6
    LAST = NT + LAG["X"]

    def steps(engine, step, loops=LOOPS):
        run_steps(engine, step, FIRST, U, loops, LAST)

    def Tile(i, r, lag):
        return Item(i - lag, r, U)

    with nc.Block() as block:
        c.pt, c.m, c.mneg, c.mt, c.pvs, c.rd, c.an, c.at = scratch(nc, own, f"a{layer}", dict(
            pt=([P, 2, H, P], F32), m=([P, 2, H], F32), mneg=([P, 2, 2 * H], BF16), mt=([2 * H, 2, P], BF16),
            pvs=([P, 2, 2, P], F32), rd=([P, 2, H], F32), an=([P, 2, P], F32), at=([P, 2, P], F32)))

        @block.tensor
        def _(pe):
            for s in (scores, st_psum, mt_psum, pv_psum, n_psum, at_psum, y_psum):
                pe.sem_inc(s, 2)

            def quarter(a, q):
                if not a.live:
                    return
                n = a.items(4, q)
                pe.wait_ge(maxed, free(n))
                if q == 0 and a.n % 2 == 0:
                    pe.wait_ge(stacked[a.stack], a.fill * c.STACK_INCS + c.STACK_INCS)
                for h in range(4):
                    last = nc.tensor.matmul(s_bank[q % 2][:, h, :], c.qs[:, a.stack, 4 * q + h, a.half],
                                            c.ks[:, a.stack, 4 * q + h, a.half], start=mask is None or h == 0,
                                            stop=mask is None)
                if mask is not None:
                    last = nc.tensor.matmul(s_bank[q % 2], c.identb[:], c.mask[:, mask, 0],
                                            start=False, stop=True)
                last.then_inc(scores, 1)

            def turned_quarter(a, q):
                if not a.live:
                    return
                n = a.items(4, q)
                if q == 0:
                    pe.wait_ge(m_rows[a.b], a.turn * 16 + 16)
                pe.wait_ge(exp_ready, free(n))
                for h in range(4):
                    last = nc.tensor.matmul(st_bank[q % 2][:, h * P:(h + 1) * P],
                                            c.ks[:, a.stack, 4 * q + h, a.half],
                                            c.qs[:, a.stack, 4 * q + h, a.half],
                                            start=mask is None or h == 0, stop=mask is None)
                if mask is not None:
                    last = nc.tensor.matmul(st_bank[q % 2], c.identb[:],
                                            c.mask[:, mask, 1].rearrange("p h k -> p (h k)"),
                                            start=False, stop=True)
                last.then_inc(st_psum, 1)

            def values(a, f):
                if not a.live:
                    return
                if f == 0:
                    pe.wait_ge(vx_ready, done(a.t))
                    pe.wait_ge(pv_ready, a.items(1, 2))
                pe.wait_ge(exp_ready, done(a.items(4, 2 * f + 1)))
                for odd in range(2):
                    for g in range(4):
                        h = 8 * f + 2 * g + odd
                        last = nc.tensor.matmul(pv[32 * g:32 * g + 32, f, :], c.vx[:, a.b, h, :],
                                                c.pt[:, a.b, h, :], start=odd == 0, stop=odd == 1)
                if f == 1:
                    last.then_inc(pv_psum, 1)

            def step(i, r):
                s, m, st, v, bk, a, yy = (Tile(i, r, LAG[k]) for k in ("S", "M", "ST", "PV", "BACK", "AT", "Y"))
                quarter(s, 0)
                turned_quarter(st, 0)
                turned_quarter(st, 1)
                if m.live:
                    pe.wait_ge(m_ready, done(m.t))
                    pe.wait_ge(mt_ready, m.items(1, 2))
                    if yy.live:
                        pe.wait_ge(at_ready, done(yy.t))
                    nc.tensor.transpose(mt[0:2 * H, :], c.mneg[:, m.b, :], c.identb[:]).then_inc(mt_psum, 1)
                quarter(s, 1)
                values(v, 0)
                quarter(s, 2)
                turned_quarter(st, 2)
                if bk.live:
                    pe.wait_ge(pv_ready, done(bk.t))
                    pe.wait_ge(n_ready, bk.items(1, 2))
                    for f in range(2):
                        last = nc.tensor.transpose(back[:, f * P:(f + 1) * P], c.pvs[:, bk.b, f, :], c.ident[:])
                    last.then_inc(n_psum, 1)
                turned_quarter(st, 3)
                quarter(s, 3)
                values(v, 1)
                if a.live:
                    pe.wait_ge(n_ready, done(a.t))
                    if m.live:
                        pe.wait_ge(mt_ready, done(m.t))
                    pe.wait_ge(at_ready, a.items(1, 2))
                    nc.tensor.transpose(at, c.an[:, a.b, :], c.ident[:]).then_inc(at_psum, 1)
                if yy.live:
                    pe.wait_ge(at_ready, done(yy.t))
                    pe.wait_ge(x_ready, yy.items(1, 2))
                    nc.tensor.matmul(y, c.at[:, yy.b, :], wo, start=True, stop=True).then_inc(y_psum, 1)

            steps(pe, step)

        @block.vector
        def _(dve):
            for s in (maxed, m_ready, n_ready, x_ready):
                dve.sem_inc(s, 2)

            def quarter_max(a, q):
                if not a.live:
                    return
                n = a.items(4, q)
                dve.wait_ge(scores, done(n))
                if q == 0:
                    dve.wait_ge(m_ready, free(a.t))
                nc.vector.reduce_max(c.m[:, a.b, 4 * q:4 * q + 4], s_bank[q % 2], AX).then_inc(maxed, 1)

            def step(i, r):
                s, nm, xx = (Tile(i, r, LAG[k]) for k in ("S", "NORM", "X"))
                quarter_max(s, 0)
                if xx.live:
                    dve.wait_ge(y_psum, done(xx.t))
                    dve.wait_ge(x_stored, free(xx.t))
                    nc.vector.tensor_tensor(c.xs[:, xx.b, :], c.x[:, xx.t, :], y, ALU.add).then_inc(x_ready, 1)
                heads = back.rearrange("p (h e) -> p h e", h=H)
                if nm.live:
                    dve.wait_ge(n_psum, done(nm.t))
                    nc.vector.reciprocal(c.rd[:, nm.b, :], heads[:, :, HD]).then_inc(rd_ready, 1)
                if xx.live:
                    dve.wait_ge(x_ready, done(xx.t))
                    nc.vector.bn_stats(c.stats[:, xx.b, :], c.xs[:, xx.b, :]).then_inc(stats_ready, 1)
                if nm.live:
                    dve.wait_ge(rd_ready, nm.t + 1)
                    dve.wait_ge(at_psum, free(nm.t))
                    nc.vector.tensor_tensor(c.an[:, nm.b, :].rearrange("p (h d) -> p h d", h=H), heads[:, :, 0:HD],
                                            c.rd[:, nm.b, :].rearrange("p (h a) -> p h a", a=1).to_broadcast([P, H, HD]),
                                            ALU.mult).then_inc(n_ready, 1)
                quarter_max(s, 1)
                quarter_max(s, 2)
                if xx.live:
                    dve.wait_ge(stats_ready, xx.t + 1)
                quarter_max(s, 3)
                if xx.live:
                    nc.vector.bn_aggr(c.mvs[:, xx.b, :], c.stats[:, xx.b, :]).then_inc(mv_ready, 1)
                if s.live:
                    dve.wait_ge(maxed, done(s.items(4, 3)))
                    dve.wait_ge(mt_psum, free(s.t))
                    nc.vector.tensor_scalar(c.mneg[:, s.b, 0:H], c.m[:, s.b, :], -1.0, None, ALU.mult).then_inc(hi_ready, 1)
                    dve.wait_ge(hi_ready, s.t + 1)
                    nc.vector.scalar_tensor_tensor(c.mneg[:, s.b, H:2 * H], c.m[:, s.b, :], -1.0,
                                                   c.mneg[:, s.b, 0:H], ALU.mult, ALU.subtract).then_inc(m_ready, 1)

            steps(dve, step)

        @block.scalar
        def _(act):
            for s in (mt_ready, exp_ready, pv_ready, at_ready):
                act.sem_inc(s, 2)

            def exponentials(a, q):
                if not a.live:
                    return
                act.wait_ge(st_psum, done(a.items(4, q)))
                if q == 0:
                    act.wait_ge(pv_psum, free(a.t))
                nc.scalar.activation(c.pt[:, a.b, 4 * q:4 * q + 4, :].rearrange("p h q -> p (h q)"),
                                     st_bank[q % 2], ACT.Exp, scale=scale).then_inc(exp_ready, 1)

            def step(i, r):
                m, st, v, yy = (Tile(i, r, LAG[k]) for k in ("M", "ST", "PV", "Y"))
                if yy.live:
                    act.wait_ge(at_psum, done(yy.t))
                    act.wait_ge(y_psum, free(yy.t))
                    nc.scalar.activation(c.at[:, yy.b, :], at, ACT.Identity).then_inc(at_ready, 1)
                exponentials(st, 0)
                if m.live:
                    act.wait_ge(mt_psum, done(m.t))
                    act.wait_ge(m_rows[m.b], m.turn * 16)
                    nc.scalar.activation(c.mt[:, m.b, :], mt[0:2 * H, :], ACT.Identity).then_inc(mt_ready, 1)
                for q in (1, 2, 3):
                    exponentials(st, q)
                if v.live:
                    act.wait_ge(pv_psum, done(v.t))
                    act.wait_ge(n_psum, free(v.t))
                    nc.scalar.activation(c.pvs[:, v.b], pv, ACT.Identity).then_inc(pv_ready, 1)

            steps(act, step)
            load_table(nc, c, ACT.Sqrt)

        @block.gpsimd
        def _(pool):
            pool.sem_inc(vx_ready, 2)
            pool.sem_inc(x_stored, 2)

            def step(i, r):
                spread_values(Tile(i, r, LAG["M"]))
                store(Tile(i, r, LAG["X"]))

            def store(a):
                if not a.live:
                    return
                pool.wait_ge(mv_ready, a.t + 1)
                nc.gpsimd.tensor_copy(c.x[:, a.t, :], c.xs[:, a.b, :])
                nc.gpsimd.tensor_copy(c.mv[:, a.t, :], c.mvs[:, a.b, :]).then_inc(x_stored, 1)

            def spread_values(a):
                if not a.live:
                    return
                pool.wait_ge(pv_psum, free(a.t))
                src = c.v[:, a.t, :].rearrange("p (g o d) -> p g o d", o=2, d=HD)
                dst = c.vx[:, a.b].rearrange("p (g o) e -> p g o e", o=2)
                for odd in range(2):
                    last = nc.gpsimd.tensor_copy(dst[:, :, odd, 16 * odd:16 * odd + HD], src[:, :, odd, :])
                last.then_inc(vx_ready, 1)

            steps(pool, step)

        @block.sync
        def _(sp):
            for stack in range(1, STACKS):
                load_stacks(sp, c, stack, slice(stack * 2 * P, (stack + 1) * 2 * P))
            for out, group in c.parts_out:
                sp.wait_ge(out, group * (NG // 2 + 1))

            def step(i, r):
                m = Tile(i, r, LAG["M"])
                if m.live:
                    sp.wait_ge(mt_ready, done(m.t))
                    sp.dma_start(c.qs[SR:SR + 2, m.stack, :, m.half], c.mt[:, m.b, :]).then_inc(m_rows[m.b], 16)
                nxt = Tile(i, r, -3)
                if i % 2 == 1 and nxt.live and i >= 3:
                    sp.wait_ge(st_psum, done(Tile(i, r, 2).items(4, 3)))
                    load_stacks(sp, c, nxt.stack, bass.ds(nxt.t * P, 2 * P))

            steps(sp, step, LOOPS - 1)
            for row in range(2):
                sp.wait_ge(m_rows[row], NT // 2 * 16)


class Shared:

    def __init__(self, nc, c, w, own, half):
        pre = f"s3{half}"
        self.w, self.base = w, half * NT // 2
        (self.xt_ready, self.up_psum, self.gu_ready, self.h_ready, self.ht_psum, self.ht_ready, self.y_psum,
         self.yg_ready, self.x_ready) = semaphores(nc, c, pre, "xt up gu h htp ht y yg x")
        self.xt, self.g, self.u, self.h, self.hT, self.yg = scratch(nc, own, pre, dict(
            xt=([P, 2, P], F32), g=([P, 2, 2 * P], F32), u=([P, 2, 2 * P], F32), h=([P, 2, 2 * P], F32),
            hT=([P, 2, 2, P], F32), yg=([P, 2, P], F32)))
        self.up_bank, self.ht_bank, self.y_bank = [c.bank[5], c.bank[6]], c.bank[7], c.bank[4]

    def tile(self, i, r, lag=0):
        return Item(i - lag, r, 2, NT // 2)

    def run(self, engine, step, ahead=0):
        run_steps(engine, step, 4, 2, NT // 4 - 2 - ahead, NT // 2 + 3)


def shared_gpsimd(nc, c, s, pool):
    for sem in (s.xt_ready, s.h_ready, s.x_ready):
        pool.sem_inc(sem, 2)

    def stage(a):
        if a.live:
            pool.wait_ge(s.up_psum, free(a.t))
            nc.gpsimd.tensor_copy(s.xt[:, a.b, :], c.xT[:, bass.ds(a.items(P, s.base * P), P)]).then_inc(s.xt_ready, 1)

    def step(i, r):
        up, y = s.tile(i, r), s.tile(i, r, 3)
        if i == 0 and isinstance(r, int):
            stage(up)
        stage(s.tile(i, r, -1))
        if up.live:
            pool.wait_ge(s.gu_ready, done(up.t))
            pool.wait_ge(s.ht_psum, free(up.t))
            nc.gpsimd.tensor_tensor(s.h[:, up.b, :], s.g[:, up.b, :], s.u[:, up.b, :], ALU.mult).then_inc(s.h_ready, 1)
        if y.live:
            pool.wait_ge(s.yg_ready, done(y.t))
            t = y.items(1, s.base)
            nc.gpsimd.tensor_tensor(c.x[:, t, :], c.x[:, t, :], s.yg[:, y.b, :], ALU.add).then_inc(s.x_ready, 1)

    s.run(pool, step, ahead=1)


def shared_scalar(nc, c, s, act):
    for sem in (s.gu_ready, s.ht_ready, s.yg_ready):
        act.sem_inc(sem, 2)

    def step(i, r):
        up, ht, y = s.tile(i, r), s.tile(i, r, 2), s.tile(i, r, 3)
        if up.live:
            act.wait_ge(s.up_psum, done(up.t))
            act.wait_ge(s.h_ready, free(up.t))
            nc.scalar.activation(s.g[:, up.b, :], s.up_bank[up.b][:, 0:2 * P], ACT.Silu)
            nc.scalar.activation(s.u[:, up.b, :], s.up_bank[up.b][:, 2 * P:4 * P], ACT.Identity).then_inc(s.gu_ready, 1)
        if ht.live:
            act.wait_ge(s.ht_psum, done(ht.t))
            act.wait_ge(s.y_psum, free(ht.t))
            nc.scalar.activation(s.hT[:, ht.b].rearrange("p k t -> p (k t)"), s.ht_bank[:, 0:2 * P],
                                 ACT.Identity).then_inc(s.ht_ready, 1)
        if y.live:
            act.wait_ge(s.y_psum, done(y.t))
            act.wait_ge(s.x_ready, free(y.t))
            nc.scalar.activation(s.yg[:, y.b, :], s.y_bank[:, 0:P], ACT.Identity,
                                 scale=c.shared_gate[:, bass.ds(y.items(1, s.base), 1)]).then_inc(s.yg_ready, 1)

    s.run(act, step)


def shared_tensor(nc, c, s, pe):
    for sem in (s.up_psum, s.ht_psum, s.y_psum):
        pe.sem_inc(sem, 2)

    def step(i, r):
        up, ht, y = s.tile(i, r), s.tile(i, r, 2), s.tile(i, r, 3)
        if up.live:
            pe.wait_ge(s.xt_ready, done(up.t))
            pe.wait_ge(s.gu_ready, free(up.t))
            nc.tensor.matmul(s.up_bank[up.b], s.xt[:, up.b, :], s.w["up"][:], start=True, stop=True).then_inc(s.up_psum, 1)
        if ht.live:
            pe.wait_ge(s.h_ready, done(ht.t))
            pe.wait_ge(s.ht_ready, ht.items(1, 2))
            for k in range(2):
                last = nc.tensor.transpose(s.ht_bank[:, k * P:(k + 1) * P], s.h[:, ht.b, k * P:(k + 1) * P], c.ident[:])
            last.then_inc(s.ht_psum, 1)
        if y.live:
            pe.wait_ge(s.ht_ready, done(y.t))
            pe.wait_ge(s.yg_ready, y.items(1, 2))
            for k in range(2):
                last = nc.tensor.matmul(s.y_bank[:, 0:P], s.hT[:, y.b, k, :], s.w["down"][:, k, :],
                                        start=k == 0, stop=k == 1)
            last.then_inc(s.y_psum, 1)

    s.run(pe, step)


def route(nc, c, layer, experts, top, loads, shared_weights=None):
    pre = f"r{layer}"
    ln = semaphores(nc, c, pre, "var root chain")
    (xn_ready, xt_psum, xt_ready, xt_kept, log_psum, log_ready, soft, exp_ready, gate_ready, gate_in) = semaphores(
        nc, c, pre, "xn xtp xt keep lp log soft exp shared gate")
    loaded, = semaphores(nc, c, pre, "loaded")
    table_out = semaphores(nc, c, pre, "out0 out1")
    E = loads[0][0].shape[-1]
    gate = loads[0][0]
    big, rows = layer == 3, layer == 1
    xt_bank, log_bank = [c.bank[n] for n in (0, 1)], [c.bank[n] for n in (2, 3)]
    with ExitStack() as own, nc.Block() as block:
        xn, xnT, logits, mx, tot = scratch(nc, own, pre, dict(
            xn=([P, 2, GT, P], F32), xnT=([P, 2, GN], F32), logits=([P, NT, E], F32), mx=([P, NT], F32),
            tot=([P, NT], F32)))
        if not big:
            above, rank = scratch(nc, own, pre, dict(
                above=([P, NT, experts, experts], F32), rank=([P, NT, experts], F32)))
        else:
            top8, rest = scratch(nc, own, pre, dict(top8=([P, NT, 8], F32), rest=([P, NT, experts], F32)))
            shared = Shared(nc, c, shared_weights, own, 0)
        scores = logits[:, :, 0:experts]

        def Group(i, r, lag):
            return Item(i - lag, r, 2, NG)

        @block.sync
        def _(sp):
            sp.dma_start(gate, loads[0][1]).then_inc(gate_in, 16)
            for dst, src in loads[1:]:
                sp.dma_start(dst, src).then_inc(loaded, 16)
            if big:
                for s in table_out:
                    sp.sem_inc(s, 16)
                with sp.Fori(0, NG // 2) as it:
                    for b in range(2):
                        g = it * 2 + b
                        sp.wait_ge(xn_ready, done(g))
                        sp.dma_start(c.table[bass.ds(g * GN, GN), 0:P].rearrange("(j t) f -> t j f", t=P), xn[:, b]).then_inc(table_out[b], 16)
                for s in table_out:
                    sp.wait_ge(s, 16 * (NG // 2 + 1))
            sp.wait_ge(loaded, 16 * (len(loads) - 1))

        @block.gpsimd
        def _(pool):
            pool.sem_inc(xt_kept, 2)
            with pool.Fori(0, NG // 2) as it:
                for b in range(2):
                    g = it * 2 + b
                    if rows:
                        pool.wait_ge(xn_ready, done(g))
                        nc.gpsimd.tensor_copy(c.v[:, bass.ds(g * GT, GT), :], xn[:, b]).then_inc(xt_kept, 1)
                    else:
                        pool.wait_ge(xt_ready, done(g))
                        nc.gpsimd.tensor_copy(c.xT[:, bass.ds(g * GN, GN)], xnT[:, b, :]).then_inc(xt_kept, 1)
            if big:
                pool.wait_ge(xt_kept, done(NG - 1))
                shared_gpsimd(nc, c, shared, pool)

        @block.vector
        def _(dve):
            dve.sem_inc(xn_ready, 2)
            ln_vector(nc, c, dve, ln)
            with dve.Fori(0, NG // 2) as it:
                for b in range(2):
                    g = it * 2 + b
                    dve.wait_ge(xt_psum, free(g))
                    if rows:
                        dve.wait_ge(xt_kept, free(g))
                    if big:
                        dve.wait_ge(table_out[b], it * 16 + 16)
                    for j in range(GT):
                        t = g * GT + j
                        last = nc.vector.tensor_scalar(xn[:, b, j, :], c.x[:, t, :], c.mv[:, t, 0:1],
                                                       c.rstd[:, bass.ds(t, 1)], ALU.subtract, ALU.mult)
                    last.then_inc(xn_ready, 1)
            dve.wait_ge(log_ready, done(NG - 1))
            links = [0]

            def link(instruction):
                instruction.then_inc(soft, 1)
                links[0] += 1
                dve.wait_ge(soft, links[0])

            wide = [P, NT, experts]
            link(nc.vector.reduce_max(mx[:], scores, AX))
            link(nc.vector.tensor_tensor(scores, scores, mx.rearrange("p (t a) -> p t a", a=1).to_broadcast(wide),
                                         ALU.subtract))
            dve.wait_ge(exp_ready, 1)
            link(nc.vector.reduce_sum(tot[:], scores, AX))
            link(nc.vector.reciprocal(tot[:], tot[:]))
            link(nc.vector.tensor_tensor(scores, scores, tot.rearrange("p (t a) -> p t a", a=1).to_broadcast(wide),
                                         ALU.mult))
            if not big:
                for e in range(experts):
                    mine = scores[:, :, e:e + 1]
                    if e:
                        nc.vector.tensor_tensor(above[:, :, e, 0:e], scores[:, :, 0:e],
                                                mine.to_broadcast([P, NT, e]), ALU.is_ge)
                    last = nc.vector.tensor_tensor(above[:, :, e, e:experts], scores[:, :, e:experts],
                                                   mine.to_broadcast([P, NT, experts - e]), ALU.is_gt)
                link(last)
                link(nc.vector.reduce_sum(rank[:], above[:], AX))
                nc.vector.scalar_tensor_tensor(c.gates[:, :, 0:experts], rank[:], float(top), scores, ALU.is_lt, ALU.mult)
            else:
                for t in range(NT):
                    last = nc.vector.max(top8[:, t, :], scores[:, t, :])
                link(last)
                for t in range(NT):
                    last = nc.vector.match_replace(rest[:, t, :], top8[:, t, :], scores[:, t, :], -1.0)
                link(last)
                link(nc.vector.reduce_sum(tot[:], top8[:], AX))
                link(nc.vector.reciprocal(tot[:], tot[:]))
                link(nc.vector.tensor_scalar(rest[:], rest[:], 0.0, None, ALU.is_lt))
                nc.vector.tensor_copy(c.chosen.rearrange("p t h e -> p h t e"), rest.rearrange("p (h t) e -> p h t e", h=2))
                link(nc.vector.tensor_tensor(scores, scores, rest[:], ALU.mult))
                nc.vector.tensor_tensor(c.gates[:], scores, tot.rearrange("p (t a) -> p t a", a=1).to_broadcast(wide),
                                        ALU.mult)

        @block.scalar
        def _(act):
            act.sem_inc(xt_ready, 2)
            act.sem_inc(log_ready, 2)
            ln_scalar(nc, c, act, ln)

            def step(i, r):
                a, m = Group(i, r, 0), Group(i, r, 1)
                if a.live:
                    act.wait_ge(xt_psum, done(a.t))
                    act.wait_ge(log_psum, free(a.t))
                    if not rows:
                        act.wait_ge(xt_kept, free(a.t))
                    nc.scalar.activation(xnT[:, a.b, :], xt_bank[a.b], ACT.Identity).then_inc(xt_ready, 1)
                if m.live:
                    act.wait_ge(log_psum, done(m.t))
                    nc.scalar.activation(logits[:, bass.ds(m.items(GT), GT), :],
                                         log_bank[m.b][:, 0:GT * E].rearrange("p (j e) -> p j e", j=GT),
                                         ACT.Identity).then_inc(log_ready, 1)

            run_steps(act, step, 2, 2, NG // 2 - 1, NG + 1)
            if big:
                act.wait_ge(log_ready, done(NG - 1))
                nc.scalar.activation(c.shared_gate[:], logits[:, :, experts], ACT.Sigmoid).then_inc(gate_ready, 1)
            load_table(nc, c, ACT.Exp)
            act.wait_ge(soft, 2)
            nc.scalar.activation(scores, scores, ACT.Exp).then_inc(exp_ready, 1)
            load_table(nc, c, ACT.Gelu if layer == 1 else ACT.Silu)
            if big:
                act.wait_ge(gate_ready, 1)
                shared_scalar(nc, c, shared, act)

        @block.tensor
        def _(pe):
            pe.sem_inc(xt_psum, 2)
            pe.sem_inc(log_psum, 2)
            pe.wait_ge(gate_in, 16)

            def step(i, r):
                a, m = Group(i, r, 0), Group(i, r, 1)
                if a.live:
                    pe.wait_ge(xn_ready, done(a.t))
                    pe.wait_ge(xt_ready, free(a.t))
                    for j in range(GT):
                        last = nc.tensor.transpose(xt_bank[a.b][:, j * P:(j + 1) * P], xn[:, a.b, j, :], c.ident[:])
                    last.then_inc(xt_psum, 1)
                if m.live:
                    pe.wait_ge(xt_ready, done(m.t))
                    pe.wait_ge(log_ready, free(m.t))
                    for j in range(GT):
                        last = nc.tensor.matmul(log_bank[m.b][:, j * E:(j + 1) * E], xnT[:, m.b, j * P:(j + 1) * P],
                                                gate, start=True, stop=True)
                    last.then_inc(log_psum, 1)

            run_steps(pe, step, 2, 2, NG // 2 - 1, NG + 1)
            if big:
                pe.wait_ge(loaded, 16 * (len(loads) - 1))
                shared_tensor(nc, c, shared, pe)


def gated_mlp(nc, c, w):
    pre = "g0"
    (xt_ready, up_psum, silu_ready, h_ready, hw_ready, ht_psum, ht_ready, y_psum, x_ready, stats_ready, mv_ready,
     x_stored, zero_fill) = semaphores(nc, c, pre, "xt up silu h hw htp ht y x bn mv xst fill")
    chunks = 5
    LAG = dict(UP=0, HW=1, HT=2, Y=3, X=4)
    FIRST, U, LOOPS, LAST = 4, 2, 14, NT + LAG["X"]
    up_bank = [[c.bank[0], c.bank[1]], [c.bank[2], c.bank[3]]]
    shared_bank, ht_bank, hs_bank, y_bank = (c.bank[n] for n in (4, 5, 6, 7))
    routed = slice(0, 512)
    with ExitStack() as own, nc.Block() as block:
        xt, act_g, h, hT, xs, stats, mvs = scratch(nc, own, pre, dict(
            xt=([P, 2, P], F32), g=([P, 2, 640], F32), h=([P, 2, 640], F32), hT=([P, 2, 5, P], F32),
            xs=([P, 2, P], F32), stats=([P, 2, 6], F32), mvs=([P, 2, 2], F32)))

        def Tile(i, r, lag):
            return Item(i - lag, r, U)

        @block.sync
        def _(sp):
            tables = (*c.slots_x, c.sum_rows)
            for table in tables:
                sp.dma_start(table.rearrange("(p n) f -> p n f", p=P),
                             c.zero_row[:, :, 0:P].to_broadcast([P, table.shape[0] // P, P])).then_inc(zero_fill, 16)
            sp.dma_start(c.table[T:T + CAPACITY, :], c.zero_row[0:CAPACITY, 0, :]).then_inc(zero_fill, 16)
            sp.wait_ge(zero_fill, 16 * (len(tables) + 1))

        @block.tensor
        def _(pe):
            for s in (up_psum, ht_psum, y_psum):
                pe.sem_inc(s, 2)

            def step(i, r):
                up, ht, y = (Tile(i, r, LAG[k]) for k in ("UP", "HT", "Y"))
                if up.live:
                    pe.wait_ge(xt_ready, done(up.t))
                    pe.wait_ge(h_ready, free(up.t))
                    nc.tensor.matmul(up_bank[up.b][0], xt[:, up.b, :], w["wg"][:], start=True, stop=True)
                    nc.tensor.matmul(up_bank[up.b][1], xt[:, up.b, :], w["wu"][:], start=True, stop=True)
                if ht.live:
                    pe.wait_ge(hw_ready, done(ht.t))
                    pe.wait_ge(ht_ready, ht.items(1, 2))
                    for k in range(4):
                        nc.tensor.transpose(ht_bank[:, k * P:(k + 1) * P], h[:, ht.b, k * P:(k + 1) * P], c.ident[:])
                    nc.tensor.transpose(hs_bank[0:64, 0:P], h[:, ht.b, 512:576], c.ident[:]).then_inc(ht_psum, 1)
                if y.live:
                    pe.wait_ge(ht_ready, done(y.t))
                    pe.wait_ge(x_ready, y.items(1, 2))
                    for k in range(chunks):
                        rows = slice(0, 64 if k == 4 else P)
                        last = nc.tensor.matmul(y_bank[:, 0:P], hT[rows, y.b, k, :], w["wd"][rows, k, :],
                                                start=k == 0, stop=k == chunks - 1)
                    last.then_inc(y_psum, 1)
                if up.live:
                    pe.wait_ge(h_ready, up.items(1, 2))
                    nc.tensor.matmul(shared_bank[:, 0:P], xt[:, up.b, :], w["ws"][:], start=True,
                                     stop=True).then_inc(up_psum, 1)

            run_steps(pe, step, FIRST, U, LOOPS, LAST)

        @block.scalar
        def _(act):
            for s in (xt_ready, silu_ready, ht_ready):
                act.sem_inc(s, 2)

            def stage(a):
                if a.live:
                    act.wait_ge(up_psum, free(a.t))
                    nc.scalar.activation(xt[:, a.b, :], c.xT[:, bass.ds(a.t * P, P)], ACT.Identity).then_inc(xt_ready, 1)

            def step(i, r):
                up, ht = (Tile(i, r, LAG[k]) for k in ("UP", "HT"))
                if i == 0 and isinstance(r, int):
                    stage(up)
                if ht.live:
                    act.wait_ge(ht_psum, done(ht.t))
                    act.wait_ge(y_psum, free(ht.t))
                    nc.scalar.activation(hT[:, ht.b, 0:4, :].rearrange("p k t -> p (k t)"), ht_bank[:, 0:4 * P],
                                         ACT.Identity)
                    nc.scalar.activation(hT[0:64, ht.b, 4, :], hs_bank[0:64, 0:P], ACT.Identity).then_inc(ht_ready, 1)
                stage(Tile(i, r, -1))
                if up.live:
                    act.wait_ge(up_psum, done(up.t))
                    act.wait_ge(h_ready, free(up.t))
                    nc.scalar.activation(act_g[:, up.b, 0:512], up_bank[up.b][0], ACT.Silu)
                    nc.scalar.activation(act_g[:, up.b, 512:576], shared_bank[:, 0:64], ACT.Silu).then_inc(silu_ready, 1)

            run_steps(act, step, FIRST, U, LOOPS - 1, LAST)
            load_table(nc, c, ACT.Sqrt)

        @block.vector
        def _(dve):
            for s in (h_ready, x_ready):
                dve.sem_inc(s, 2)

            def step(i, r):
                up, xx = (Tile(i, r, LAG[k]) for k in ("UP", "X"))
                if xx.live:
                    dve.wait_ge(y_psum, done(xx.t))
                    dve.wait_ge(x_stored, free(xx.t))
                    nc.vector.tensor_tensor(xs[:, xx.b, :], c.x[:, xx.t, :], y_bank[:, 0:P], ALU.add).then_inc(x_ready, 1)
                    dve.wait_ge(x_ready, done(xx.t))
                    nc.vector.bn_stats(stats[:, xx.b, :], xs[:, xx.b, :]).then_inc(stats_ready, 1)
                    dve.wait_ge(stats_ready, xx.t + 1)
                if up.live:
                    dve.wait_ge(silu_ready, done(up.t))
                    dve.wait_ge(ht_psum, free(up.t))
                    dve.wait_ge(hw_ready, free(up.t))
                    nc.vector.tensor_tensor(h[:, up.b, routed], act_g[:, up.b, routed], up_bank[up.b][1], ALU.mult)
                    nc.vector.tensor_tensor(h[:, up.b, 512:576], act_g[:, up.b, 512:576], shared_bank[:, 64:128],
                                            ALU.mult).then_inc(h_ready, 1)
                if xx.live:
                    nc.vector.bn_aggr(mvs[:, xx.b, :], stats[:, xx.b, :]).then_inc(mv_ready, 1)

            run_steps(dve, step, FIRST, U, LOOPS, LAST)

        @block.gpsimd
        def _(pool):
            for s in (hw_ready, x_stored):
                pool.sem_inc(s, 2)

            def step(i, r):
                up, xx = (Tile(i, r, LAG[k]) for k in ("UP", "X"))
                if up.live:
                    pool.wait_ge(h_ready, done(up.t))
                    gates = c.gates[:, up.t, 0:8].rearrange("p (e a) -> p e a", a=1).to_broadcast([P, 8, 64])
                    cols = h[:, up.b, routed].rearrange("p (e f) -> p e f", e=8)
                    nc.gpsimd.tensor_tensor(cols, cols, gates, ALU.mult).then_inc(hw_ready, 1)
                if xx.live:
                    pool.wait_ge(mv_ready, xx.t + 1)
                    nc.gpsimd.tensor_copy(c.mv[:, xx.t, :], mvs[:, xx.b, :])
                    nc.gpsimd.tensor_copy(c.x[:, xx.t, :], xs[:, xx.b, :]).then_inc(x_stored, 1)

            run_steps(pool, step, FIRST, U, LOOPS, LAST)


def places(nc, c, d):
    EX, HT = 8, NT // HALVES
    loaded, made, counts_psum, links = semaphores(nc, c, "l1", "load made counts link")
    within, total = (c.bank[n][:, 0:NT * EX].rearrange("p (g j e) -> p g j e", g=HALVES, j=HT) for n in (0, 1))
    with ExitStack() as own, nc.Block() as block:
        numbers, ones, sel, ping, pong, share, over, blocks, ends, ends_b, start, slot, late, ids, pair = scratch(
            nc, own, "l1", dict(
                numbers=([P, BLOCKS], F32), ones=([P, P], F32), sel=([P, HALVES, HT, EX], F32),
                ping=([P, HALVES, HT, EX], F32), pong=([P, HALVES, HT, EX], F32), share=([P, HALVES, EX], F32),
                over=([P, HALVES, EX, HT], F32), blocks=([P, HALVES, EX], F32), ends=([P, HALVES, EX], F32),
                endsb=([P, HALVES, EX], F32), start=([P, HALVES, EX], F32), slot=([P, NT], F32),
                late=([1, HALVES, BLOCKS, EX], F32), ids=([1, HALVES, BLOCKS], F32),
                pair=([1, HALVES * BLOCKS + PAIR_LAG], F32)))

        @block.sync
        def _(sp):
            sp.dma_start(numbers[:], d["numbers"].partition_broadcast(P)).then_inc(loaded, 16)

        @block.tensor
        def _(pe):
            pe.wait_ge(made, 2)
            flat = sel.rearrange("p g j e -> p (g j e)")
            nc.tensor.matmul(c.bank[0][:, 0:NT * EX], c.causal[:, 0, :], flat, start=True, stop=True)
            nc.tensor.matmul(c.bank[1][:, 0:NT * EX], ones[:], flat, start=True, stop=True).then_inc(counts_psum, 1)

        @block.gpsimd
        def _(pool):
            nc.gpsimd.memset(ones[:], 1.0).then_inc(made, 1)

        @block.vector
        def _(dve):
            count = [0]

            def link(instruction):
                instruction.then_inc(links, 1)
                count[0] += 1
                dve.wait_ge(links, count[0])

            def scan(old, new, length):
                step = 1
                while step < length:
                    nc.vector.tensor_copy(new[:, :, 0:step], old[:, :, 0:step])
                    link(nc.vector.tensor_tensor(new[:, :, step:], old[:, :, step:], old[:, :, :length - step], ALU.add))
                    old, new = new, old
                    step *= 2
                return old

            gates = c.gates[:, :, 0:EX]
            nc.vector.memset(pair[:], 0.0)
            nc.vector.tensor_scalar(sel.rearrange("p g j e -> p (g j) e"), gates, 0.0, None, ALU.is_gt).then_inc(made, 1)
            nc.vector.reduce_sum(c.token_gate[:], gates, AX)
            dve.wait_ge(counts_psum, 1)
            link(nc.vector.tensor_copy(ping[:], total))
            sums = scan(ping, pong, HT)
            tiles_before = pong if sums is ping else ping
            nc.vector.tensor_scalar(share[:], sums[:, :, HT - 1, :], 1.0 / P, None, ALU.mult)
            link(nc.vector.tensor_tensor(tiles_before[:], sums[:], total, ALU.subtract))
            dve.wait_ge(loaded, 16)
            for g in range(HALVES):
                last = nc.vector.tensor_tensor(
                    over[:, g], share[:, g, :].rearrange("p (e a) -> p e a", a=1).to_broadcast([P, EX, HT]),
                    numbers[:, 0:HT].rearrange("p (a k) -> p a k", a=1).to_broadcast([P, EX, HT]), ALU.is_gt)
            link(last)
            link(nc.vector.reduce_sum(blocks[:], over[:], AX))
            link(nc.vector.tensor_copy(ends[:], blocks[:]))
            done_ends = scan(ends, ends_b, EX)
            nc.vector.tensor_tensor(tiles_before[:], tiles_before[:], within, ALU.add)
            link(nc.vector.tensor_tensor(start[:], done_ends[:], blocks[:], ALU.subtract))
            link(nc.vector.tensor_scalar(start[:], start[:], float(P), None, ALU.mult))
            other = sums
            for g in range(HALVES):
                last = nc.vector.tensor_tensor(
                    other[:, g], tiles_before[:, g],
                    start[:, g:g + 1, :].to_broadcast([P, HT, EX]), ALU.add)
            link(last)
            link(nc.vector.tensor_tensor(other[:], other[:], sel[:], ALU.mult))
            link(nc.vector.reduce_sum(slot[:], other.rearrange("p g j e -> p (g j) e"), AX))
            nc.vector.tensor_copy(c.slot[:], slot[:])
            for g in range(HALVES):
                last = nc.vector.tensor_tensor(
                    late[:, g], numbers[0:1, :].rearrange("p (b a) -> p b a", a=1).to_broadcast([1, BLOCKS, EX]),
                    done_ends[0:1, g:g + 1, :].to_broadcast([1, BLOCKS, EX]), ALU.is_ge)
            link(last)
            link(nc.vector.reduce_sum(ids[:], late[:], AX))
            flat_ids = ids.rearrange("p g b -> p (g b)")
            link(nc.vector.tensor_scalar(flat_ids, flat_ids, float(EX - 1), None, ALU.min))
            nc.vector.tensor_copy(c.block_expert[:], flat_ids)
            NB = HALVES * BLOCKS
            link(nc.vector.tensor_scalar(pair[:, PAIR_LAG:PAIR_LAG + NB], flat_ids, 8.0, None, ALU.mult))
            link(nc.vector.tensor_tensor(pair[:, 0:NB], pair[:, 0:NB], flat_ids, ALU.add))
            nc.vector.tensor_copy(c.expert_pair[:], pair[:])


def routed_gelu(nc, c, w):
    CH, XB = 4, 4
    HT, NB, FF = NT // HALVES, HALVES * BLOCKS, 512
    (xt_psum, xt_ready, h_psum, hb_ready, gelu_ready, ht_psum, ht_ready, y_psum, y_ready, added, stats_ready) = semaphores(
        nc, c, "e1", "xtp xt h hb gelu htp ht yp y add bn")
    placed = gpsimd_dma_semaphores(nc, c, "e1", "place0 place1")
    back = gpsimd_dma_semaphores(nc, c, "e1", " ".join(f"back{n}" for n in range(8)))
    block_in = semaphores(nc, c, "e1", "in0 in1 in2 in3")
    y_out = semaphores(nc, c, "e1", "out0 out1")
    xt_bank, h_bank, ht_bank, y_bank = ([c.bank[n], c.bank[n + 1]] for n in (0, 2, 4, 6))
    FIRST, U, LOOPS, LAST = 4, 4, NB // 4 - 1, NB + 6
    LAG = dict(X=0, UP=1, HT=3, Y=1 + PAIR_LAG, STORE=6)
    TB = HT // 4

    def Block(i, r, lag=0):
        return Item(i - lag, r, U, NB)

    with ExitStack() as own, nc.Block() as block:
        xb, xT, hb, h, hT, y, stats = scratch(nc, own, "e1", dict(
            xb=([P, XB, P], F32), xT=([P, 2, P], F32), hb=([P, 2, FF], F32), h=([P, 2, FF], F32),
            hT=([P, 2, CH, P], F32), y=([P, 2, P], F32), stats=([P, NT, 6], F32)))

        def rows(halves, a):
            half = a.n // BLOCKS
            return halves[half][bass.ds(a.items(P, -half * BLOCKS * P), P), :]

        @block.gpsimd
        def _(pool):
            for j in range(NT):
                nc.gpsimd.indirect_dma_start(c.slots_x[j // HT][:, :], bass.IndirectOffsetOnAxis(ap=c.slot[:, j:j + 1], axis=0),
                                             c.v[:, j, :], None).then_inc(placed[j // HT], 16)
            for half in range(HALVES):
                pool.wait_ge(placed[half], 16 * HT)
                for k in range(2):
                    pool.wait_ge(y_out[k], 16 * (half + 1) * BLOCKS // 2 + 16)
                for j in range(half * HT, (half + 1) * HT):
                    nc.gpsimd.indirect_dma_start(c.v[:, j, :], None, c.slots_y[half][:, :],
                                                 bass.IndirectOffsetOnAxis(ap=c.slot[:, j:j + 1], axis=0)
                                                 ).then_inc(back[j // TB], 16)

        @block.sync
        def _(sp):
            for s in y_out:
                sp.sem_inc(s, 16)

            def step(i, r):
                x, yy = Block(i, r), Block(i, r, LAG["STORE"])
                if x.live:
                    if x.n >= XB:
                        sp.wait_ge(xt_psum, x.items(1, -1))
                    sp.dma_start(xb[:, x.n % XB, :], rows(c.slots_x, x)).then_inc(block_in[x.n % XB], 16)
                if yy.live:
                    sp.wait_ge(y_ready, done(yy.t))
                    sp.dma_start(rows(c.slots_y, yy), y[:, yy.b, :]).then_inc(y_out[yy.b], 16)

            sp.wait_ge(placed[0], 16 * HT)
            run_steps(sp, step, 2 * U, U, BLOCKS // U - 2, BLOCKS)
            sp.wait_ge(placed[1], 16 * HT)
            for i in range(BLOCKS, BLOCKS + 2 * U):
                step(i, 0)
            with sp.Fori(0, BLOCKS // U - 2) as r:
                for n in range(U):
                    step(BLOCKS + 2 * U + n, r)
            for i in range(NB, LAST):
                step(i, 0)
            for s in y_out:
                sp.wait_ge(s, 16 * NB // 2 + 16)

        @block.tensor
        def _(pe):
            for s in (xt_psum, h_psum, ht_psum, y_psum):
                pe.sem_inc(s, 2)

            def step(i, r):
                x, up, ht, yy = (Block(i, r, LAG[k]) for k in ("X", "UP", "HT", "Y"))
                if up.live or yy.live:
                    both = pe.value_load(c.expert_pair[0:1, bass.ds(up.t, 1)], min_val=0, max_val=63)
                    y_expert = (both >> 3) & 7
                    up_expert = both & 7
                if x.live:
                    pe.wait_ge(block_in[x.n % XB], r * 16 + (16 * (x.n // XB) + 16))
                    pe.wait_ge(xt_ready, free(x.t))
                    nc.tensor.transpose(xt_bank[x.b][:, 0:P], xb[:, x.n % XB, :], c.ident[:]).then_inc(xt_psum, 1)
                if up.live:
                    pe.wait_ge(xt_ready, done(up.t))
                    pe.wait_ge(hb_ready, free(up.t))
                    nc.tensor.matmul(h_bank[up.b], xT[:, up.b, :],
                                     w["w1"][:, bass.ds(up_expert, 1), :].rearrange("d a f -> d (a f)"),
                                     start=True, stop=True).then_inc(h_psum, 1)
                if ht.live:
                    pe.wait_ge(gelu_ready, done(ht.t))
                    pe.wait_ge(ht_ready, free(ht.t))
                    for k in range(CH):
                        last = nc.tensor.transpose(ht_bank[ht.b][:, k * P:(k + 1) * P], h[:, ht.b, k * P:(k + 1) * P], c.ident[:])
                    last.then_inc(ht_psum, 1)
                if yy.live:
                    pe.wait_ge(ht_ready, done(yy.t))
                    pe.wait_ge(y_ready, free(yy.t))
                    for k in range(CH):
                        last = nc.tensor.matmul(y_bank[yy.b][:, 0:P], hT[:, yy.b, k, :],
                                                w["w2"][:, bass.ds(y_expert, 1), k * P:(k + 1) * P].rearrange("d a f -> d (a f)"),
                                                start=k == 0, stop=k == CH - 1)
                    last.then_inc(y_psum, 1)

            run_steps(pe, step, FIRST, U, LOOPS, LAST)

        @block.scalar
        def _(act):
            for s in (xt_ready, gelu_ready, ht_ready):
                act.sem_inc(s, 2)

            def step(i, r):
                x, up, ht = (Block(i, r, LAG[k]) for k in ("X", "UP", "HT"))
                if x.live:
                    act.wait_ge(xt_psum, done(x.t))
                    act.wait_ge(h_psum, free(x.t))
                    nc.scalar.activation(xT[:, x.b, :], xt_bank[x.b][:, 0:P], ACT.Identity).then_inc(xt_ready, 1)
                if ht.live:
                    act.wait_ge(ht_psum, done(ht.t))
                    act.wait_ge(y_psum, free(ht.t))
                    nc.scalar.activation(hT[:, ht.b].rearrange("p k t -> p (k t)"), ht_bank[ht.b],
                                         ACT.Identity).then_inc(ht_ready, 1)
                if up.live:
                    act.wait_ge(hb_ready, done(up.t))
                    act.wait_ge(ht_psum, free(up.t))
                    nc.scalar.activation(h[:, up.b, :], hb[:, up.b, :], ACT.Gelu).then_inc(gelu_ready, 1)

            run_steps(act, step, FIRST, U, LOOPS, LAST)
            load_table(nc, c, ACT.Sqrt)

        @block.vector
        def _(dve):
            for s in (hb_ready, y_ready):
                dve.sem_inc(s, 2)

            def step(i, r):
                up, yy = (Block(i, r, LAG[k]) for k in ("UP", "Y"))
                if up.live:
                    e = dve.value_load(c.block_expert[0:1, bass.ds(up.t, 1)], min_val=0, max_val=7)
                    dve.wait_ge(h_psum, done(up.t))
                    dve.wait_ge(gelu_ready, free(up.t))
                    nc.vector.tensor_tensor(hb[:, up.b, :], h_bank[up.b],
                                            w["b1"][:, bass.ds(e, 1), :].rearrange("p a f -> p (a f)"),
                                            ALU.add).then_inc(hb_ready, 1)
                if yy.live:
                    e = dve.value_load(c.block_expert[0:1, bass.ds(yy.t, 1)], min_val=0, max_val=7)
                    dve.wait_ge(y_psum, done(yy.t))
                    dve.wait_ge(y_out[yy.b], r * 32 + (yy.n // 2) * 16 + 16)
                    nc.vector.tensor_tensor(y[:, yy.b, :], y_bank[yy.b][:, 0:P],
                                            w["b2"][:, bass.ds(e, 1), :].rearrange("p a f -> p (a f)"),
                                            ALU.add).then_inc(y_ready, 1)

            run_steps(dve, step, FIRST, U, LOOPS, LAST)
            for j in range(NT):
                if j % TB == 0:
                    dve.wait_ge(back[j // TB], 16 * TB)
                nc.vector.scalar_tensor_tensor(c.x[:, j, :], c.v[:, j, :], c.token_gate[:, j:j + 1], c.x[:, j, :],
                                               ALU.mult, ALU.add).then_inc(added, 1)
                if j:
                    dve.wait_ge(added, j)
                    nc.vector.bn_stats(stats[:, j - 1, :], c.x[:, j - 1, :]).then_inc(stats_ready, 1)
            dve.wait_ge(added, NT)
            nc.vector.bn_stats(stats[:, NT - 1, :], c.x[:, NT - 1, :]).then_inc(stats_ready, 1)
            dve.wait_ge(stats_ready, NT)
            for j in range(NT):
                nc.vector.bn_aggr(c.mv[:, j, :], stats[:, j, :])


def ffn0(nc, c, d):
    with ExitStack() as own:
        gate, wg, wu, ws, wd = scratch(nc, own, "w0", dict(
            gate=([P, 8], F32), wg=([P, 512], F32), wu=([P, 512], F32), ws=([P, P], F32), wd=([P, 5, P], F32)))
        w = dict(wg=wg, wu=wu, ws=ws, wd=wd)
        route(nc, c, 0, 8, 2, [(gate[:], d["f0_gate"]), (wg[:], d["f0_wg"]), (wu[:], d["f0_wu"]), (ws[:], d["f0_ws"]),
                               (wd[:, 0:4, :], d["f0_wd"]), (wd[0:64, 4, :], d["f0_sd"])])
        gated_mlp(nc, c, w)


def ffn1(nc, c, d):
    with ExitStack() as own:
        gate, w1, b1, w2, b2, c.slot, c.block_expert, c.expert_pair, c.token_gate = scratch(nc, own, "w1", dict(
            gate=([P, 8], F32), w1=([P, 8, 512], F32), b1=([P, 8, 512], F32), w2=([P, 8, 512], F32),
            b2=([P, 8, P], F32), slot=([P, NT], I32), blockexpert=([1, HALVES * BLOCKS], I32),
            pair=([1, HALVES * BLOCKS + PAIR_LAG], I32), tokengate=([P, NT], F32)))
        route(nc, c, 1, 8, 1, [(gate[:], d["f1_gate"]), (w1[:], d["f1_w1"]), (w2[:], d["f1_w2"]),
                               (b1[:], d["f1_b1"].partition_broadcast(P)), (b2[:], d["f1_b2"].partition_broadcast(P))])
        places(nc, c, d)
        routed_gelu(nc, c, dict(w1=w1, b1=b1, w2=w2, b2=b2))


def ffn2(nc, c, d):
    EX, TILES, LIMIT, ALPHA = 8, 2, 7.0, 1.702
    NTOK = TILES * P
    ln = semaphores(nc, c, "e2", "var root chain")
    (loaded, xn_ready, xt_psum, xt_ready, h_psum, gate_ready, up_clipped, up_ready, sig_ready, glu_ready,
     inter_ready, y_psum, yb_ready, acc_ready, cw_links, stats_ready) = semaphores(
        nc, c, "e2", "load xn xtp xt h gate upc up sig glu inter y yb acc cw bn")
    h_bank, y_bank, xt_bank = [c.bank[0], c.bank[1]], [c.bank[2], c.bank[3]], c.bank[4]
    with ExitStack() as own, nc.Block() as block:
        w_gu, w_down, b_gu, b_down, numbers, idx, weights = scratch(nc, own, "e2", dict(
            wgu=([P, EX, 2, P], F32), wdown=([P, EX, P], F32), bgu=([P, EX, 2], F32), bdown=([P, EX, P], F32),
            numbers=([P, EX], F32), idx=([P, TILES, 2], I32), weights=([P, TILES, EX], F32)))
        xn, xT, idx_f, picked, cw, gate, up, sig, glu, inter, yb, stats = scratch(nc, own, "e2", dict(
            xn=([P, TILES, P], F32), xT=([P, NTOK], F32), idxf=([P, TILES, 2], F32), picked=([P, TILES, 2, EX], F32),
            cw=([P, TILES, EX], F32), gate=([P, 2, NTOK], F32), up=([P, 2, NTOK], F32), sig=([P, 2, NTOK], F32),
            glu=([P, 2, NTOK], F32), inter=([P, 2, NTOK], F32), yb=([P, 2, TILES, P], F32), stats=([P, TILES, 6], F32)))
        loads = [(idx[:], d["f2_idx"]), (weights[:], d["f2_weights"]), (numbers[:], d["numbers"][:, 0:EX].partition_broadcast(P)),
                 (b_gu[:], d["f2_bgu"]), (w_gu[:], d["f2_wgu"]), (w_down[:], d["f2_down"]),
                 (b_down[:], d["f2_bdown"].partition_broadcast(P))]

        @block.sync
        def _(sp):
            for dst, src in loads:
                sp.dma_start(dst, src).then_inc(loaded, 16)

        @block.tensor
        def _(pe):
            pe.wait_ge(xn_ready, 1)
            for t in range(TILES):
                last = nc.tensor.transpose(xt_bank[:, t * P:(t + 1) * P], xn[:, t, :], c.ident[:])
            last.then_inc(xt_psum, 1)
            pe.wait_ge(xt_ready, 1)
            pe.wait_ge(loaded, 16 * len(loads))
            for i in range(EX + 2):
                if i < EX:
                    if i >= 2:
                        pe.wait_ge(gate_ready, i - 1)
                        pe.wait_ge(up_clipped, i - 1)
                    for k in range(2):
                        last = nc.tensor.matmul(h_bank[i % 2][:, k * NTOK:(k + 1) * NTOK], w_gu[:, i, k, :], xT[:],
                                                start=True, stop=True)
                    last.then_inc(h_psum, 1)
                if i >= 2:
                    e = i - 2
                    pe.wait_ge(inter_ready, e + 1)
                    if e >= 2:
                        pe.wait_ge(yb_ready, e - 1)
                    for t in range(TILES):
                        last = nc.tensor.matmul(y_bank[e % 2][:, t * P:(t + 1) * P],
                                                inter[:, e % 2, t * P:(t + 1) * P], w_down[:, e, :],
                                                start=True, stop=True)
                    last.then_inc(y_psum, 1)

        @block.scalar
        def _(act):
            ln_scalar(nc, c, act, ln)
            load_table(nc, c, ACT.Sigmoid)
            act.wait_ge(xt_psum, 1)
            nc.scalar.activation(xT[:], xt_bank[:, 0:NTOK], ACT.Identity).then_inc(xt_ready, 1)
            for e in range(EX):
                act.wait_ge(gate_ready, e + 1)
                if e >= 2:
                    act.wait_ge(glu_ready, e - 1)
                nc.scalar.activation(sig[:, e % 2, :], gate[:, e % 2, :], ACT.Sigmoid, scale=ALPHA).then_inc(sig_ready, 1)
            load_table(nc, c, ACT.Sqrt)

        @block.vector
        def _(dve):
            ln_vector(nc, c, dve, ln)
            for t in range(TILES):
                last = nc.vector.tensor_scalar(xn[:, t, :], c.x[:, t, :], c.mv[:, t, 0:1], c.rstd[:, t:t + 1],
                                               ALU.subtract, ALU.mult)
            last.then_inc(xn_ready, 1)
            dve.wait_ge(loaded, 16 * len(loads))
            nc.vector.tensor_copy(idx_f[:], idx[:]).then_inc(cw_links, 1)
            dve.wait_ge(cw_links, 1)
            for k in range(2):
                last = nc.vector.tensor_tensor(picked[:, :, k, :], idx_f[:, :, k:k + 1].to_broadcast([P, TILES, EX]),
                                               numbers.rearrange("p (t e) -> p t e", t=1).to_broadcast([P, TILES, EX]),
                                               ALU.is_equal)
            last.then_inc(cw_links, 1)
            dve.wait_ge(cw_links, 2)
            nc.vector.tensor_tensor(cw[:], picked[:, :, 0, :], picked[:, :, 1, :], ALU.add).then_inc(cw_links, 1)
            dve.wait_ge(cw_links, 3)
            nc.vector.tensor_tensor(cw[:], cw[:], weights[:], ALU.mult).then_inc(cw_links, 1)
            dve.wait_ge(cw_links, 4)
            for i in range(EX + 3):
                b = i % 2
                if i < EX:
                    dve.wait_ge(h_psum, i + 1)
                    if i >= 2:
                        dve.wait_ge(inter_ready, i - 1)
                    nc.vector.tensor_scalar(gate[:, b, :], h_bank[b][:, 0:NTOK], b_gu[:, i, 0:1], LIMIT,
                                            ALU.add, ALU.min).then_inc(gate_ready, 1)
                    nc.vector.tensor_scalar(up[:, b, :], h_bank[b][:, NTOK:2 * NTOK], b_gu[:, i, 1:2], LIMIT,
                                            ALU.add, ALU.min).then_inc(up_clipped, 1)
                e = i - 1
                if 0 <= e < EX:
                    dve.wait_ge(sig_ready, e + 1)
                    nc.vector.tensor_tensor(glu[:, e % 2, :], gate[:, e % 2, :], sig[:, e % 2, :],
                                            ALU.mult).then_inc(glu_ready, 1)
                if i < EX:
                    dve.wait_ge(up_clipped, i + 1)
                    nc.vector.tensor_scalar(up[:, b, :], up[:, b, :], -LIMIT, 1.0, ALU.max, ALU.add).then_inc(up_ready, 1)
                if 0 <= e < EX:
                    dve.wait_ge(glu_ready, e + 1)
                    dve.wait_ge(up_ready, e + 1)
                    if e >= 2:
                        dve.wait_ge(y_psum, e - 1)
                    nc.vector.tensor_tensor(inter[:, e % 2, :], glu[:, e % 2, :], up[:, e % 2, :],
                                            ALU.mult).then_inc(inter_ready, 1)
                e = i - 3
                if e >= 0:
                    dve.wait_ge(y_psum, e + 1)
                    nc.vector.tensor_tensor(yb[:, e % 2], y_bank[e % 2][:, 0:NTOK].rearrange("p (t f) -> p t f", t=TILES),
                                            b_down[:, e:e + 1, :].to_broadcast([P, TILES, P]), ALU.add).then_inc(yb_ready, 1)
                    dve.wait_ge(yb_ready, e + 1)
                    if e >= 1:
                        dve.wait_ge(acc_ready, e)
                    for t in range(TILES):
                        last = nc.vector.scalar_tensor_tensor(c.x[:, t, :], yb[:, e % 2, t, :], cw[:, t, e:e + 1],
                                                              c.x[:, t, :], ALU.mult, ALU.add)
                    last.then_inc(acc_ready, 1)
            dve.wait_ge(acc_ready, EX)
            for t in range(TILES):
                last = nc.vector.bn_stats(stats[:, t, :], c.x[:, t, :])
            last.then_inc(stats_ready, 1)
            dve.wait_ge(stats_ready, 1)
            for t in range(TILES):
                nc.vector.bn_aggr(c.mv[:, t, :], stats[:, t, :])


def dispatch(nc, c, d, weights, w):
    HALF = T // 2
    ROUNDS = CAPACITY // 8
    (loaded, sel_psum, sel_read, searched, links, moved, twice, tok_psum, stored, weights_in) = semaphores(
        nc, c, "d3", "load sp sr search link moved twice tp stored win")
    tok_bank = c.bank[3]
    with ExitStack() as own, nc.Block() as block:
        order, value = c.ctxT[:, 0:HALF], c.ctxT[:, HALF:T]
        slots, region, top, some, merged, best, empty, tok = scratch(nc, own, "d3", dict(
            slots=([64, CAPACITY], F32), region=([P, 1], F32),
            top=([P, CAPACITY], F32), some=([64, CAPACITY], F32),
            merged=([64, 2, CAPACITY], F32), best=([64, CAPACITY], F32), empty=([64, CAPACITY], F32),
            tok=([64, 2, CAPACITY], F32)))
        loads = [(order, d["order"].partition_broadcast(P)), (slots[:], d["slots"].partition_broadcast(64)),
                 (region[:], d["region"])]
        shared = Shared(nc, c, w, own, 1)

        @block.sync
        def _(sp):
            for dst, src in loads:
                sp.dma_start(dst, src).then_inc(loaded, 16)
            sp.dma_start(c.table[0:T, P:P + 64].rearrange("(j t) e -> t j e", t=P), c.gates[:]).then_inc(stored, 16)
            for dst, src in weights:
                sp.dma_start(dst, src).then_inc(weights_in, 16)
            sp.wait_ge(searched, 2 * ROUNDS - 1)
            sp.dma_start(merged[:, 1, :], top[64:P, :]).then_inc(moved, 16)
            sp.wait_ge(stored, 16)
            sp.wait_ge(weights_in, 16 * len(weights))

        @block.gpsimd
        def _(pool):
            shared_gpsimd(nc, c, shared, pool)

        @block.scalar
        def _(act):
            shared_scalar(nc, c, shared, act)

        @block.tensor
        def _(pe):
            for k in range(4):
                for j in range(4):
                    last = nc.tensor.transpose(c.bank[k][:, j * P:(j + 1) * P],
                                               c.chosen[:, 4 * k + j].rearrange("p h e -> p (h e)"), c.ident[:])
                last.then_inc(sel_psum, 1)

            shared_tensor(nc, c, shared, pe)
            pe.wait_ge(sel_read, 1)
            pe.wait_ge(twice, 1)
            nc.tensor.transpose(tok_bank[:, 0:64], tok.rearrange("e k s -> e (k s)"), c.ident[0:64, 0:64]).then_inc(tok_psum, 1)

        @block.vector
        def _(dve):
            count = [0]

            def link(instruction):
                instruction.then_inc(links, 1)
                count[0] += 1
                dve.wait_ge(links, count[0])

            dve.wait_ge(loaded, 16 * len(loads))
            for k in range(4):
                dve.wait_ge(sel_psum, k + 1)
                part = slice(k * GN, (k + 1) * GN)
                last = nc.vector.tensor_tensor(value[:, part], c.bank[k], order[:, part], ALU.mult)
            link(last)
            dve.sem_inc(sel_read, 1)
            for k in range(ROUNDS):
                found = top[:, 8 * k:8 * k + 8]
                nc.vector.max(found, value).then_inc(searched, 1)
                dve.wait_ge(searched, 2 * k + 1)
                if k < ROUNDS - 1:
                    nc.vector.match_replace(value, found, value, 0.0).then_inc(searched, 1)
                    dve.wait_ge(searched, 2 * k + 2)
            link(nc.vector.tensor_scalar(some[:], top[0:64, :], 0.0, float(HALF), ALU.is_gt, ALU.mult))
            link(nc.vector.tensor_tensor(merged[:, 0, :], some[:], top[0:64, :], ALU.add))
            dve.wait_ge(moved, 16)
            both = merged.rearrange("e h s -> e (h s)")
            for k in range(ROUNDS):
                link(nc.vector.max(best[:, 8 * k:8 * k + 8], both))
                if k < ROUNDS - 1:
                    link(nc.vector.match_replace(both, best[:, 8 * k:8 * k + 8], both, 0.0))
            link(nc.vector.scalar_tensor_tensor(empty[:], best[:], 0.0, slots[:], ALU.is_equal, ALU.mult))
            link(nc.vector.tensor_scalar(best[:], best[:], -1.0, float(T), ALU.mult, ALU.add))
            for k in range(2):
                nc.vector.tensor_tensor(tok[:, k, :], best[:], empty[:], ALU.add).then_inc(links, 1)
            dve.wait_ge(links, count[0] + 2)
            dve.sem_inc(twice, 1)
            dve.wait_ge(tok_psum, 1)
            for k in range(2):
                half = slice(k * 64, k * 64 + 64)
                mine = tok_bank[half, 0:64].rearrange("p (n k) -> p n k", k=2)[:, :, k]
                nc.vector.tensor_copy(c.idx[half, :], mine)
                nc.vector.tensor_scalar(c.sum_idx[half, :], mine, region[half, 0:1], None, ALU.add)


def experts(nc, c, w):
    PAIRS, XB, AHEAD, I = 32, 8, 6, 64
    (xt_psum, xt_ready, up_psum, silu_ready, h_ready, ht_psum, ht_ready, y_psum, ys_ready,
     cleared) = semaphores(nc, c, "x3", "xtp xt up silu h htp ht y ys clear")
    scattered, = gpsimd_dma_semaphores(nc, c, "x3", "scat")
    gathered = gpsimd_dma_semaphores(nc, c, "x3", " ".join(f"in{n}" for n in range(XB)))
    xt_bank, up_bank, ht_bank, y_bank = ([c.bank[n], c.bank[n + 1]] for n in (0, 2, 4, 6))
    halves = [slice(0, 64), slice(64, P)]
    FIRST, U, LOOPS, LAST = XB, XB, PAIRS // XB - 1, PAIRS + 3

    with ExitStack() as own, nc.Block() as block:
        rows, xT, silu, h, hT, ys = scratch(nc, own, "x3", dict(
            rows=([P, XB, P + 64], F32), xT=([P, 2, P], F32),
            silu=([P, 2, 2, I], F32), h=([P, 2, P], F32), hT=([P, 2, P], F32), ys=([P, 2, P], F32)))

        def Pair(i, r, lag=0):
            return Item(i - lag, r, U, PAIRS)

        @block.gpsimd
        def _(pool):
            nc.gpsimd.memset(h[:], 0.0).then_inc(cleared, 1)
            for n in range(PAIRS + AHEAD):
                if n < PAIRS:
                    if n >= XB:
                        pool.wait_ge(ys_ready, free(n))
                    nc.gpsimd.indirect_dma_start(rows[:, n % XB, :], None, c.table[:, :],
                                                 bass.IndirectOffsetOnAxis(ap=c.idx[:, n:n + 1], axis=0)
                                                 ).then_inc(gathered[n % XB], 16)
                y = n - AHEAD
                if y >= 0:
                    pool.wait_ge(ys_ready, done(y, XB))
                    if y >= 1:
                        pool.wait_ge(scattered, 16 * y)
                    nc.gpsimd.indirect_dma_start(c.sum_rows[:, :],
                                                 bass.IndirectOffsetOnAxis(ap=c.sum_idx[:, y:y + 1], axis=0),
                                                 ys[:, y % 2, :], None, compute_op=ALU.add).then_inc(scattered, 16)
            pool.wait_ge(scattered, 16 * PAIRS)

        @block.tensor
        def _(pe):
            for s in (xt_psum, up_psum, ht_psum, y_psum):
                pe.sem_inc(s, 2)

            def step(i, r):
                x, up, ht, y = (Pair(i, r, lag) for lag in range(4))
                if x.live:
                    pe.wait_ge(gathered[x.n % XB], r * 16 + (16 * (x.n // XB) + 16))
                    pe.wait_ge(xt_ready, free(x.t))
                    nc.tensor.transpose(xt_bank[x.b][:, 0:P], rows[:, x.n % XB, 0:P], c.ident[:]).then_inc(xt_psum, 1)
                if up.live:
                    pe.wait_ge(xt_ready, done(up.t))
                    pe.wait_ge(h_ready, free(up.t))
                    nc.tensor.matmul(up_bank[up.b][:, 0:2 * P], xT[:, up.b, :],
                                     w["up"][:, bass.ds(up.items(2), 2), :].rearrange("d a f -> d (a f)"),
                                     start=True, stop=True).then_inc(up_psum, 1)
                if ht.live:
                    pe.wait_ge(h_ready, done(ht.t))
                    pe.wait_ge(ht_ready, free(ht.t))
                    nc.tensor.transpose(ht_bank[ht.b][:, 0:P], h[:, ht.b, :], c.ident[:]).then_inc(ht_psum, 1)
                if y.live:
                    pe.wait_ge(ht_ready, done(y.t))
                    pe.wait_ge(ys_ready, y.items(1, XB - 1))
                    nc.tensor.matmul(y_bank[y.b][:, 0:P], hT[:, y.b, :],
                                     w["down"][:, bass.ds(y.t, 1), :].rearrange("d a f -> d (a f)"),
                                     start=True, stop=True).then_inc(y_psum, 1)

            run_steps(pe, step, FIRST, U, LOOPS, LAST)

        @block.scalar
        def _(act):
            for s in (xt_ready, silu_ready, ht_ready):
                act.sem_inc(s, 2)

            def step(i, r):
                x, up, ht = (Pair(i, r, lag) for lag in range(3))
                if x.live:
                    act.wait_ge(xt_psum, done(x.t))
                    act.wait_ge(up_psum, free(x.t))
                    nc.scalar.activation(xT[:, x.b, :], xt_bank[x.b][:, 0:P], ACT.Copy).then_inc(xt_ready, 1)
                if up.live:
                    act.wait_ge(up_psum, done(up.t))
                    act.wait_ge(h_ready, free(up.t))
                    nc.scalar.activation(silu[:, up.b], up_bank[up.b][:, 0:2 * P].rearrange("p (k f) -> p k f", k=2)[:, :, 0:I],
                                         ACT.Silu).then_inc(silu_ready, 1)
                if ht.live:
                    act.wait_ge(ht_psum, done(ht.t))
                    act.wait_ge(y_psum, free(ht.t))
                    nc.scalar.activation(hT[:, ht.b, :], ht_bank[ht.b][:, 0:P], ACT.Copy).then_inc(ht_ready, 1)

            run_steps(act, step, FIRST, U, LOOPS, LAST)

        @block.vector
        def _(dve):
            dve.sem_inc(h_ready, 2)
            dve.sem_inc(ys_ready, XB)

            def step(i, r):
                up, y = Pair(i, r, 1), Pair(i, r, 3)
                if up.live:
                    if up.n == 0 and isinstance(r, int):
                        dve.wait_ge(cleared, 1)
                    dve.wait_ge(silu_ready, done(up.t))
                    dve.wait_ge(ht_psum, free(up.t))
                    for k in range(2):
                        last = nc.vector.tensor_tensor(h[halves[k], up.b, k * I:(k + 1) * I], silu[halves[k], up.b, k, :],
                                                       up_bank[up.b][halves[k], k * P + I:(k + 1) * P], ALU.mult)
                    last.then_inc(h_ready, 1)
                if y.live:
                    dve.wait_ge(y_psum, done(y.t))
                    if y.n >= 2:
                        dve.wait_ge(scattered, y.items(16) - 16)
                    for k in range(2):
                        gate = rows[halves[k], y.n % XB, bass.ds(y.items(2, P + k), 1)]
                        last = nc.vector.tensor_scalar(ys[halves[k], y.b, :], y_bank[y.b][halves[k], 0:P], gate, None,
                                                       ALU.mult)
                    last.then_inc(ys_ready, 1)

            run_steps(dve, step, FIRST, U, LOOPS, LAST)


def ffn3(nc, c, d):
    with ExitStack() as own:
        gate, sgu, wd, chosen = scratch(nc, own, "w3", dict(
            gate=([P, 65], F32), sgu=([P, 512], F32), wd=([P, 2, P], F32), chosen=([P, NT // 2, 2, 64], F32)))
        c.chosen = chosen
        c.idx, c.sum_idx = scratch(nc, own, "w3", dict(idx=([P, 32], I32), sumidx=([P, 32], I32)))
        shared = dict(up=sgu, down=wd)
        route(nc, c, 3, 64, 8, [(gate[:], d["f3_gate"]), (sgu[:], d["f3_sgu"]), (wd[:], d["f3_sdown"])], shared)
        with ExitStack() as inner:
            up, down = scratch(nc, inner, "w3", dict(up=([P, 64, P], F32), down=([P, 32, P], F32)))
            dispatch(nc, c, d, [(up[:], d["f3_up"]), (down[:], d["f3_down"])], shared)
            experts(nc, c, dict(up=up, down=down))


def finish(nc, c, out):
    PARTS = 4
    loaded, added, stored = (semaphores(nc, c, "end", " ".join(f"{k}{n}" for n in range(PARTS)))
                             for k in ("load", "add", "store"))
    with ExitStack() as own, nc.Block() as block:
        sums, = scratch(nc, own, "end", dict(sums=([P, 2, NT, P], F32)))

        def part(n):
            return slice(n * NT // PARTS, (n + 1) * NT // PARTS)

        @block.sync
        def _(sp):
            for n in range(PARTS):
                for k in range(2):
                    sp.dma_start(sums[:, k, part(n), :],
                                 c.sums[k][0:T, :].rearrange("(j t) f -> t j f", t=P)[:, part(n), :]).then_inc(loaded[n], 16)
            for n in range(PARTS):
                sp.wait_ge(added[n], 2)
                sp.dma_start(out.rearrange("b t f -> t b f")[:, part(n), :], c.x[:, part(n), :]).then_inc(stored[n], 16)
            for n in range(PARTS):
                sp.wait_ge(stored[n], 16)

        @block.vector
        def _(dve):
            for n in range(PARTS):
                dve.wait_ge(loaded[n], 32)
                for k in range(2):
                    if k:
                        dve.wait_ge(added[n], 1)
                    nc.vector.tensor_tensor(c.x[:, part(n), :], c.x[:, part(n), :], sums[:, k, part(n), :],
                                            ALU.add).then_inc(added[n], 1)


def setup(nc, c, d):
    loaded, made, cleared, ones_over, stacks, stats, masks, zeroed, rows_out, c.context_in = semaphores(
        nc, c, "su", "load made clear ones stacks stats mask zero rows context")
    loads = [(c.ident[:], d["ident"]), (c.wa[:], d["wa"]), (c.wrot[:], d["wrot"]), (c.bcol[:], d["bcol"]),
             (c.rope[:], d["rope"]),
             (c.brow[:], d["brow"].partition_broadcast(P)), (c.causal[:], d["causal"]), (c.umask[:], d["umask"])]
    xs = [semaphores(nc, c, "su", f"x{g}")[0] for g in range(4)]
    with nc.Block() as block:
        @block.sync
        def _(sp):
            for g in range(4):
                part = slice(g * NT // 4, (g + 1) * NT // 4)
                sp.dma_start(c.x[:, part, :], d["x"].rearrange("b t f -> t b f")[:, part, :]).then_inc(xs[g], 16)
            for dst, src in loads:
                sp.dma_start(dst, src).then_inc(loaded, 16)
            sp.wait_ge(zeroed, 2)
            sp.dma_start(c.q_stack_dram[SR:SR + 2].rearrange("r h (j t) -> r (h j) t", t=P),
                         c.zeros[:].to_broadcast([2, H * NT, P])).then_inc(rows_out, 16)
            sp.dma_start(c.ctxT[:], d["ctxT"]).then_inc(c.context_in, 16)
            sp.wait_ge(rows_out, 16)

        @block.vector
        def _(dve):
            nc.vector.memset(c.zero_row[:], 0.0).then_inc(zeroed, 1)
            nc.vector.memset(c.ks[:, 0], 0.0).then_inc(ones_over, 1)
            dve.wait_ge(ones_over, 1)
            nc.vector.memset(c.ks[32:64, 0], 1.0)
            for t in range(NT):
                if t % (NT // 4) == 0:
                    dve.wait_ge(xs[t // (NT // 4)], 16)
                nc.vector.bn_stats(c.stats0[:, t, :], c.x[:, t, :]).then_inc(stats, 1)
            for t in range(NT):
                dve.wait_ge(stats, t + 1)
                nc.vector.bn_aggr(c.mv[:, t, :], c.stats0[:, t, :])
            dve.wait_ge(loaded, 16 * len(loads))
            nc.vector.tensor_copy(c.identb[:], c.ident[:]).then_inc(made, 1)
            for kind, src in enumerate((c.causal, c.umask)):
                for side in range(2):
                    nc.vector.tensor_scalar(c.mask[:, kind, side], src[:, side:side + 1, :].to_broadcast([P, 4, P]),
                                            NEG, None, ALU.mult).then_inc(masks, 1)

        @block.gpsimd
        def _(pool):
            nc.gpsimd.memset(c.zeros[:], 0.0).then_inc(zeroed, 1)
            nc.gpsimd.memset(c.qs[:], 0.0)
            nc.gpsimd.memset(c.vx[:], 0.0).then_inc(cleared, 1)
            pool.wait_ge(cleared, 1)
            for odd in range(2):
                nc.gpsimd.memset(c.vx.rearrange("p b (g o) e -> p b g o e", o=2)[
                    :, :, :, odd, 16 * odd + HD:16 * odd + 2 * HD], 1.0)

        @block.scalar
        def _(act):
            act.wait_ge(zeroed, 2)
            load_table(nc, c, ACT.Sqrt)
            for n, (value, rows) in enumerate(((0.0, slice(0, P)), (1.0, slice(32, 64)))):
                if n:
                    act.wait_ge(stacks, 1)
                k_rows = c.ks[rows, 1:STACKS].rearrange("p s h k -> p (s h k)")
                nc.scalar.activation(k_rows, c.zero_row[rows, 0, 0:1].to_broadcast(list(k_rows.shape)), ACT.Identity,
                                     bias=value).then_inc(stacks, 1)


def build(nc, d, out, stages=range(8)):
    with ExitStack() as ctx:
        c = Core()
        c.program = ctx
        c.next_gpsimd_semaphore = FIRST_GPSIMD_SEMAPHORE

        def sb(name, shape, dt=F32):
            return ctx.enter_context(nc.sbuf_tensor(name, shape, dt))

        c.psum = ctx.enter_context(nc.psum_tensor("psum", [P, 8, 512], F32))
        c.bank = [c.psum[:, n, :] for n in range(8)]
        c.x = sb("x_sb", [P, NT, P])
        c.ctxT = sb("ctx_T", [P, T])
        c.v = sb("v_sb", [P, NT, P])
        c.wa = sb("w_attn", [P, 4, 4, P])
        c.wrot = sb("w_rot", [P, 2, P])
        c.bcol = sb("b_cols", [P, 10])
        c.brow = sb("b_rows", [P, 8, P])
        c.rope = sb("rope_sb", [P, 2, P])
        c.ident = sb("ident_sb", [P, P])
        c.identb = sb("ident_bf", [P, P], BF16)
        c.causal = sb("causal_sb", [P, 2, P])
        c.umask = sb("umask_sb", [P, 2, P], U8)
        c.mask = sb("mask_sb", [P, 2, 2, 4, P], BF16)
        c.mv = sb("mean_var", [P, NT, 2])
        c.stats0 = sb("stats0", [P, NT, 6])
        c.stats = sb("stats", [P, 2, 6])
        c.mvs = sb("mean_var_new", [P, 2, 2])
        c.xs = sb("x_new", [P, 2, P])
        c.veps, c.root, c.rstd0, c.newt, c.rstd = (sb("ln_" + n, [P, NT]) for n in
                                                   ("veps", "root", "rstd0", "newt", "rstd"))
        c.gates = sb("gates", [P, NT, 64])
        c.shared_gate = sb("shared_gate", [P, NT])
        c.xT = c.v.rearrange("p t f -> p (t f)")
        c.q_stack_dram = nc.dram_tensor("q_parts", [SR + 2, H, T], BF16, kind="Internal").ap()
        c.k_stack_dram = nc.dram_tensor("k_parts", [3 * HD, H, T], BF16, kind="Internal").ap()
        c.q_dram = c.q_stack_dram[0:SR].rearrange("(c d) h t -> (d h) c t", d=HD)
        c.k_dram = c.k_stack_dram.rearrange("(c d) h t -> (d h) c t", d=HD)
        c.STACK_INCS = 16 * (1 + len(K_RUNS))

        c.qs = sb("q_stack", [P, STACKS, H, 2 * P], BF16)
        c.ks = sb("k_stack", [P, STACKS, H, 2 * P], BF16)
        c.zeros = sb("zeros", [2, 1, P], BF16)
        c.zero_row = sb("zero_row", [P, 1, P + 64])
        c.table_out, c.tables_loaded = sb("table_out", [P, 32]), 0
        c.vx = sb("v_x", [P, 2, H, 32])
        c.table = nc.dram_tensor("table", [T + CAPACITY, P + 64], F32, kind="Internal").ap()
        c.slots_x, c.slots_y = ([nc.dram_tensor(f"{name}{half}", [BLOCKS * P, P], F32, kind="Internal").ap()
                                 for half in range(HALVES)] for name in ("slots_x", "slots_y"))
        c.sum_rows = nc.dram_tensor("sum_rows", [2 * (T + CAPACITY), P], F32, kind="Internal").ap()
        c.sums = [c.sum_rows[k * (T + CAPACITY):(k + 1) * (T + CAPACITY), :] for k in range(2)]
        for layer in range(4):
            with ExitStack() as sems:
                c.ctx = sems
                c.next_semaphore = FIRST_SEMAPHORE
                if layer == 0:
                    setup(nc, c, d)
                if 2 * layer in stages:
                    with ExitStack() as own:
                        project(nc, c, layer, own)
                        attend(nc, c, layer, own)
                if 2 * layer + 1 in stages:
                    (ffn0, ffn1, ffn2, ffn3)[layer](nc, c, d)
                if layer == 3:
                    finish(nc, c, out)
                else:
                    zero_semaphores(nc, c)


def host_arrays(i):
    f = {}
    at = lambda n, k: np.asarray(i[f"L{n}_xattn_{k if n != 2 else k.lower()}"])
    f["x"] = np.asarray(i["x"])
    f["ctxT"] = np.ascontiguousarray(np.asarray(i["ctx_1024"]).reshape(T, P).T)
    order = np.arange(P).reshape(H, HD).T.reshape(P)
    f["wa"] = np.ascontiguousarray(np.stack([np.stack([at(n, k).T[:, order] for k in ("Wq", "Wk")]
                                                      + [at(n, k).T for k in ("Wv", "Wo")])
                                             for n in range(4)]).transpose(2, 0, 1, 3))
    swap = np.arange(P).reshape(H, 2, HD // 2)[:, ::-1].reshape(P)[order]
    f["wrot"] = np.ascontiguousarray(np.stack([at(3, k).T[:, swap] for k in ("Wq", "Wk")], 1))
    f["bcol"] = np.ascontiguousarray(np.stack([at(n, k)[order] for n in range(4) for k in ("bq", "bk")]
                                              + [at(3, k)[swap] for k in ("bq", "bk")], 1))
    f["brow"] = np.ascontiguousarray(np.stack([at(n, k) for n in range(4) for k in ("bv", "bo")]))
    angle = np.arange(P)[:, None] * (1.0 / 10000.0 ** (np.arange(0, HD, 2) / HD))[None, :]
    cos, sin = (np.tile(fn(angle), (1, 2 * H)).T for fn in (np.cos, np.sin))
    sign = np.where(np.arange(P) % HD < HD // 2, -1.0, 1.0)[:, None]
    f["rope"] = np.ascontiguousarray(np.stack([cos, sin * sign], 1)[order].astype(np.float32))
    f["ident"] = np.eye(P, dtype=np.float32)
    later = (np.arange(P)[None, :] > np.arange(P)[:, None]).astype(np.float32)
    f["causal"] = np.ascontiguousarray(np.stack([later, later.T], 1))
    up = {k: np.asarray(i[f"L0_ffn_{k}"]) for k in ("gate_w", "wg", "wu", "wd", "sg", "su", "sd")}
    f["f0_gate"] = np.ascontiguousarray(up["gate_w"].T)
    f["f0_wg"], f["f0_wu"] = (np.ascontiguousarray(up[k].reshape(512, P).T) for k in ("wg", "wu"))
    f["f0_ws"] = np.ascontiguousarray(np.concatenate([up["sg"], up["su"]]).T)
    f["f0_wd"] = np.ascontiguousarray(up["wd"].transpose(0, 2, 1).reshape(4, P, P).transpose(1, 0, 2))
    f["f0_sd"] = np.ascontiguousarray(up["sd"].T)
    up = {k: np.asarray(i[f"L1_ffn_{k}"]) for k in ("gate_w", "w1", "b1", "w2", "b2")}
    f["f1_gate"] = up["gate_w"]
    f["f1_w1"] = np.ascontiguousarray(up["w1"].transpose(1, 0, 2))
    f["f1_b1"] = up["b1"]
    f["f1_w2"] = np.ascontiguousarray(up["w2"].reshape(8, 4, P, P).transpose(2, 0, 1, 3).reshape(P, 8, 512))
    f["f1_b2"] = up["b2"]
    up = {k: np.asarray(i[f"L2_ffn_{k}"]) for k in ("router_indices", "routing_weights", "gate_up_proj",
                                                    "gate_up_proj_bias", "down_proj", "down_proj_bias")}
    f["f2_idx"], f["f2_weights"] = (np.ascontiguousarray(up[k].reshape(2, P, -1).transpose(1, 0, 2))
                                    for k in ("router_indices", "routing_weights"))
    f["numbers"] = np.arange(BLOCKS, dtype=np.float32).reshape(1, BLOCKS)
    f["f2_wgu"] = np.ascontiguousarray(up["gate_up_proj"].reshape(8, P, P, 2).transpose(1, 0, 3, 2))
    f["f2_bgu"] = np.ascontiguousarray(up["gate_up_proj_bias"].reshape(8, P, 2).transpose(1, 0, 2))
    f["f2_down"] = np.ascontiguousarray(up["down_proj"].transpose(1, 0, 2))
    f["f2_bdown"] = up["down_proj_bias"]
    up = {k: np.asarray(i[f"L3_ffn_{k}"]) for k in ("gate_w", "shared_gate_w", "shared_gate_up_w", "shared_down_w",
                                                    "expert_gate_up_w", "expert_down_w")}
    f["f3_gate"] = np.ascontiguousarray(np.concatenate([up["gate_w"], up["shared_gate_w"]], 1))
    f["f3_up"] = np.ascontiguousarray(up["expert_gate_up_w"].transpose(1, 0, 2))
    f["f3_down"] = np.ascontiguousarray(up["expert_down_w"].reshape(32, P, P).transpose(1, 0, 2))
    f["f3_sgu"] = up["shared_gate_up_w"]
    f["f3_sdown"] = np.ascontiguousarray(up["shared_down_w"].reshape(2, P, P).transpose(1, 0, 2))
    f["order"] = (T // 2 - np.arange(T // 2, dtype=np.float32)).reshape(1, -1)
    f["slots"] = np.arange(CAPACITY, dtype=np.float32).reshape(1, -1)
    f["region"] = np.repeat(np.array([0, T + CAPACITY], np.float32), 64).reshape(P, 1)
    mask = np.asarray(i["mask_SxS2_bk1"]).view(np.uint8)
    f["umask"] = np.ascontiguousarray(np.stack([mask, mask.T], 1))
    return f


def kernel(**inputs):
    import numpy as _np
    import concourse.bacc as _bacc
    from concourse import mybir as _mybir
    from concourse.bass_utils import run_bass_kernel_spmd as _run

    nc = _bacc.Bacc("TRN2", target_bir_lowering=False, num_devices=1)
    arrays = {f"in_{k}": _np.ascontiguousarray(a) for k, a in host_arrays(inputs).items()}
    dram = {k[3:]: nc.dram_tensor(k, a.shape, _mybir.dt.from_np(a.dtype), kind="ExternalInput").ap()
            for k, a in arrays.items()}
    out = nc.dram_tensor("out_0_dram", (NT, P, P), F32, kind="ExternalOutput").ap()
    build(nc, dram, out)
    r = _run(nc, [arrays], core_ids=[0])
    return r.results[0]["out_0_dram"]
```
